# Optimizing a Trainium2 kernel written in Bass

```python
import numpy as np
import jax
import jax.numpy as jnp

def _softmax(x, axis=-1):
    return jax.nn.softmax(x, axis=axis)

def _gelu(x):
    return jax.nn.gelu(x, approximate=True)

def _silu(x):
    return jax.nn.silu(x)

def _sigmoid(x):
    return jax.nn.sigmoid(x)

def _layernorm(x, axis=-1, eps=1e-05):
    m = jnp.mean(x, axis=axis, keepdims=True)
    v = jnp.var(x, axis=axis, keepdims=True)
    return (x - m) / jnp.sqrt(v + eps)

def _scatter_add(tgt, idx, src, axis=0):
    return tgt.at[idx].add(src)

def _segment_sum(src, seg, n):
    return jax.ops.segment_sum(src, seg, n)
kernel_name = 'mk_vit_tower_d1_tok_img256_r4_299e37'

def setup_inputs(seed: int=0):
    np.random.seed(seed)
    _w = jnp.asarray

    def _rec_inputs():
        import jax
        import jax.numpy as jnp
        _rk = jax.random.key(seed)
        x = -0.000928989 + 1.00043 * jax.random.normal(jax.random.fold_in(_rk, 1), (64, 64, 64, 1), jnp.float32)
        return x
    x = _rec_inputs()

    def _L0_tok_setup():
        import jax, jax.numpy as jnp
        import numpy as np
        L = 4
        M1 = 12
        M2 = 12
        BN_EPS = 1e-05

        def _fourier_layer(v, W1, W2):
            B, C, Sx, Sy = v.shape
            x_ft = jnp.fft.rfft2(v)
            out1 = jnp.einsum('bixy,ioxy->boxy', x_ft[:, :, :M1, :M2], W1)
            out2 = jnp.einsum('bixy,ioxy->boxy', x_ft[:, :, -M1:, :M2], W2)
            out_ft = jnp.zeros((B, C, Sx, Sy // 2 + 1), jnp.complex64)
            out_ft = out_ft.at[:, :, :M1, :M2].set(out1)
            out_ft = out_ft.at[:, :, Sx - M1:, :M2].set(out2)
            return jnp.fft.irfft2(out_ft, s=(Sx, Sy))
        key = jax.random.key(seed)
        ks = jax.random.split(key, 10)
        B, S, d_a, d_v, d_u = (16, 64, 3, 32, 1)
        return {'x': jax.random.normal(ks[0], (B, S, S, 1), jnp.float32), 'p_w': jax.random.normal(ks[1], (d_a, d_v), jnp.float32) * 0.3, 'p_b': jax.random.normal(ks[2], (d_v,), jnp.float32) * 0.1, 'fw1': jax.random.normal(ks[3], (L, d_v, d_v, M1, M2, 2), jnp.float32) * (1.0 / d_v), 'fw2': jax.random.normal(ks[4], (L, d_v, d_v, M1, M2, 2), jnp.float32) * (1.0 / d_v), 'w_w': jax.random.normal(ks[5], (L, d_v, d_v), jnp.float32) * (1.0 / np.sqrt(d_v)), 'w_b': jax.random.normal(ks[6], (L, d_v), jnp.float32) * 0.1, 'bn_g': jnp.ones((L, d_v), jnp.float32), 'bn_b': jnp.zeros((L, d_v), jnp.float32), 'q_w': jax.random.normal(ks[7], (d_v, d_u), jnp.float32) * 0.3, 'q_b': jax.random.normal(ks[8], (d_u,), jnp.float32) * 0.1}
    _L0_tok_all = _L0_tok_setup()
    _L0_tok_in = {k: v for k, v in _L0_tok_all.items() if k in ('p_w', 'p_b', 'fw1', 'fw2', 'w_w', 'w_b', 'bn_g', 'bn_b', 'q_w', 'q_b')}
    del _L0_tok_all

    def _L0_attn_setup():
        import math
        import jax, jax.numpy as jnp
        import numpy as np
        EPS_DIV = 1e-07
        EPS_NORM = 1e-12

        def _l2_normalize(x, axis):
            n = jnp.sqrt(jnp.sum(x * x, axis=axis, keepdims=True))
            return x / jnp.maximum(n, EPS_NORM)
        key = jax.random.key(seed)
        ks = jax.random.split(key, 5)
        b, N, C = (8, 1024, 64)
        x = jax.random.normal(ks[0], (b, N, C), dtype=jnp.float32)
        W_qkv = jax.random.normal(ks[1], (C, 3 * C), dtype=jnp.float32) * (1.0 / math.sqrt(C))
        b_qkv = jax.random.normal(ks[2], (3 * C,), dtype=jnp.float32) * 0.02
        W_out = jax.random.normal(ks[3], (C, C), dtype=jnp.float32) * (1.0 / math.sqrt(C))
        b_out = jax.random.normal(ks[4], (C,), dtype=jnp.float32) * 0.02
        return {'x': x, 'W_qkv': W_qkv, 'b_qkv': b_qkv, 'W_out': W_out, 'b_out': b_out}
    _L0_attn_all = _L0_attn_setup()
    _L0_attn_in = {k: v for k, v in _L0_attn_all.items() if k in ('W_qkv', 'b_qkv', 'W_out', 'b_out')}
    del _L0_attn_all

    def _L0_ffn_setup():
        import jax, jax.numpy as jnp
        import numpy as np
        B, S, D, H, E, K = (8, 2048, 64, 256, 8, 2)
        key = jax.random.key(seed)
        ks = jax.random.split(key, 7)
        s_in = 1.0 / np.sqrt(D)
        s_hid = 1.0 / np.sqrt(H)
        return {'x': jax.random.normal(ks[0], (B, S, D), dtype=jnp.float32), 'Wg': jax.random.uniform(ks[1], (E, D), jnp.float32, -s_in, s_in), 'bg': jax.random.uniform(ks[2], (E,), jnp.float32, -s_in, s_in), 'W1': jax.random.uniform(ks[3], (E, H, D), jnp.float32, -s_in, s_in), 'b1': jax.random.uniform(ks[4], (E, H), jnp.float32, -s_in, s_in), 'W2': jax.random.uniform(ks[5], (E, D, H), jnp.float32, -s_hid, s_hid), 'b2': jax.random.uniform(ks[6], (E, D), jnp.float32, -s_hid, s_hid)}
    _L0_ffn_all = _L0_ffn_setup()
    _L0_ffn_in = {k: v for k, v in _L0_ffn_all.items() if k in ('Wg', 'bg', 'W1', 'b1', 'W2', 'b2')}
    del _L0_ffn_all
    return {'x': x, 'L0_tok_p_w': _L0_tok_in['p_w'], 'L0_tok_p_b': _L0_tok_in['p_b'], 'L0_tok_fw1': _L0_tok_in['fw1'], 'L0_tok_fw2': _L0_tok_in['fw2'], 'L0_tok_w_w': _L0_tok_in['w_w'], 'L0_tok_w_b': _L0_tok_in['w_b'], 'L0_tok_bn_g': _L0_tok_in['bn_g'], 'L0_tok_bn_b': _L0_tok_in['bn_b'], 'L0_tok_q_w': _L0_tok_in['q_w'], 'L0_tok_q_b': _L0_tok_in['q_b'], 'L0_attn_W_qkv': _L0_attn_in['W_qkv'], 'L0_attn_b_qkv': _L0_attn_in['b_qkv'], 'L0_attn_W_out': _L0_attn_in['W_out'], 'L0_attn_b_out': _L0_attn_in['b_out'], 'L0_ffn_Wg': _L0_ffn_in['Wg'], 'L0_ffn_bg': _L0_ffn_in['bg'], 'L0_ffn_W1': _L0_ffn_in['W1'], 'L0_ffn_b1': _L0_ffn_in['b1'], 'L0_ffn_W2': _L0_ffn_in['W2'], 'L0_ffn_b2': _L0_ffn_in['b2']}

def reference(x, L0_tok_p_w, L0_tok_p_b, L0_tok_fw1, L0_tok_fw2, L0_tok_w_w, L0_tok_w_b, L0_tok_bn_g, L0_tok_bn_b, L0_tok_q_w, L0_tok_q_b, L0_attn_W_qkv, L0_attn_b_qkv, L0_attn_W_out, L0_attn_b_out, L0_ffn_Wg, L0_ffn_bg, L0_ffn_W1, L0_ffn_b1, L0_ffn_W2, L0_ffn_b2):
    import jax
    import jax.numpy as jnp

    def _L0_tok_ref(x, p_w, p_b, fw1, fw2, w_w, w_b, bn_g, bn_b, q_w, q_b):
        import jax, jax.numpy as jnp
        import numpy as np
        L = 4
        M1 = 12
        M2 = 12
        BN_EPS = 1e-05

        def _fourier_layer(v, W1, W2):
            B, C, Sx, Sy = v.shape
            x_ft = jnp.fft.rfft2(v)
            out1 = jnp.einsum('bixy,ioxy->boxy', x_ft[:, :, :M1, :M2], W1)
            out2 = jnp.einsum('bixy,ioxy->boxy', x_ft[:, :, -M1:, :M2], W2)
            out_ft = jnp.zeros((B, C, Sx, Sy // 2 + 1), jnp.complex64)
            out_ft = out_ft.at[:, :, :M1, :M2].set(out1)
            out_ft = out_ft.at[:, :, Sx - M1:, :M2].set(out2)
            return jnp.fft.irfft2(out_ft, s=(Sx, Sy))
        B, Sx, Sy, _ = x.shape
        gx = jnp.broadcast_to(jnp.linspace(0.0, 1.0, Sx, dtype=jnp.float32)[None, :, None, None], (B, Sx, Sy, 1))
        gy = jnp.broadcast_to(jnp.linspace(0.0, 1.0, Sy, dtype=jnp.float32)[None, None, :, None], (B, Sx, Sy, 1))
        h = jnp.concatenate([x, gx, gy], axis=-1)
        v = h @ p_w + p_b
        v = jnp.transpose(v, (0, 3, 1, 2))
        for i in range(L):
            W1 = fw1[i, ..., 0] + 1j * fw1[i, ..., 1]
            W2 = fw2[i, ..., 0] + 1j * fw2[i, ..., 1]
            x1 = _fourier_layer(v, W1, W2)
            x2 = jnp.einsum('bcxy,cd->bdxy', v, w_w[i]) + w_b[i][None, :, None, None]
            v = x1 + x2
            mean = jnp.mean(v, axis=(0, 2, 3), keepdims=True)
            var = jnp.var(v, axis=(0, 2, 3), keepdims=True)
            v = (v - mean) * jax.lax.rsqrt(var + BN_EPS)
            v = v * bn_g[i][None, :, None, None] + bn_b[i][None, :, None, None]
            if i < L - 1:
                v = jax.nn.relu(v)
        out = jnp.einsum('bcxy,cu->bxyu', v, q_w) + q_b
        return jnp.squeeze(out)

    def _L0_attn_ref(x, W_qkv, b_qkv, W_out, b_out):
        import math
        import jax, jax.numpy as jnp
        import numpy as np
        EPS_DIV = 1e-07
        EPS_NORM = 1e-12

        def _l2_normalize(x, axis):
            n = jnp.sqrt(jnp.sum(x * x, axis=axis, keepdims=True))
            return x / jnp.maximum(n, EPS_NORM)
        b, N, C = x.shape
        qkv = x @ W_qkv + b_qkv
        q, k, v = jnp.split(qkv, 3, axis=2)
        q = q - jnp.mean(q, axis=2, keepdims=True)
        k = k - jnp.mean(k, axis=2, keepdims=True)
        q2 = q * q
        k2 = k * k
        q2s = jnp.sum(q2, axis=2, keepdims=True)
        k2s = jnp.sum(k2, axis=2, keepdims=True)
        k2 = _l2_normalize(k2 / (k2s + EPS_DIV), axis=-2)
        q2 = _l2_normalize(q2 / (q2s + EPS_DIV), axis=-1)
        kv = jnp.einsum('bnc,bnd->bcd', k2, v)
        t2 = jnp.einsum('bnc,bcd->bnd', q2, kv) / math.sqrt(N)
        attn = v + t2
        return attn @ W_out + b_out

    def _L0_ffn_ref(x, Wg, bg, W1, b1, W2, b2):
        import jax, jax.numpy as jnp
        import numpy as np
        B, S, D, H, E, K = (8, 2048, 64, 256, 8, 2)
        gate_scores = jnp.einsum('bsd,ed->bse', x, Wg) + bg
        topk_scores, topk_idx = jax.lax.top_k(gate_scores, K)
        topk_probs = jax.nn.softmax(topk_scores, axis=-1)
        combine = jnp.sum(topk_probs[..., None] * jax.nn.one_hot(topk_idx, E, dtype=x.dtype), axis=-2)
        out = jnp.zeros_like(x)
        for e in range(E):
            h = jax.nn.relu(jnp.einsum('bsd,hd->bsh', x, W1[e]) + b1[e])
            y = jnp.einsum('bsh,dh->bsd', h, W2[e]) + b2[e]
            out = out + combine[..., e:e + 1] * y
        return out
    h = _L0_tok_ref(x, L0_tok_p_w, L0_tok_p_b, L0_tok_fw1, L0_tok_fw2, L0_tok_w_w, L0_tok_w_b, L0_tok_bn_g, L0_tok_bn_b, L0_tok_q_w, L0_tok_q_b)
    h = h + _L0_attn_ref(_layernorm(h, axis=-1), L0_attn_W_qkv, L0_attn_b_qkv, L0_attn_W_out, L0_attn_b_out)
    h = h + _L0_ffn_ref(_layernorm(h, axis=-1), L0_ffn_Wg, L0_ffn_bg, L0_ffn_W1, L0_ffn_b1, L0_ffn_W2, L0_ffn_b2)
    return h

_drawn_inputs = setup_inputs


def setup_inputs(seed=0):
    import zlib

    import numpy as np

    out = dict(_drawn_inputs(seed))
    spreads = {'L0_tok_bn_g': (1.0, 0.2), 'L0_tok_bn_b': (0.0, 0.1)}
    factors = {'L0_tok_p_b': 8.0,
     'L0_tok_w_b': 8.0,
     'L0_attn_b_out': 6.103,
     'L0_ffn_b1': 6.605,
     'L0_ffn_b2': 4.887}
    for name, (base, spread) in spreads.items():
        noise = np.random.default_rng([zlib.crc32(name.encode()), seed]).standard_normal(out[name].shape)
        drawn = base * np.exp(spread * noise) if base else spread * noise
        out[name] = jnp.asarray(drawn.astype(out[name].dtype))
    for name, factor in factors.items():
        out[name] = (out[name] * factor).astype(out[name].dtype)
    return out
```

```python
from contextlib import ExitStack

import numpy as np
import concourse.bass as bass
from concourse import mybir

F32 = mybir.dt.float32
ALU = mybir.AluOpType
ACT = mybir.ActivationFunctionType
AX = mybir.AxisListType

P = 128
BANKS = 8
B, S, C = 64, 64, 32
LAYERS, M = 4, 12
KX = 2 * M
XQ, XR = 4, 16
BQ, B2 = 4, 2
CH = BQ * B2
CHUNKS = B // CH
COLS = CH * XR * S
QUART = COLS // 4
KYG = M // 4
E, H, D = 8, 256, 64
TILES = B * S // P
BN_STEPS = 14
BN_EPS = 1e-5
LN_EPS = 1e-5

JOBS = []
for hf in range(2):
    JOBS += [("turn", hf, j) for j in range(8)]
    JOBS += [("dfty", hf, j) for j in range(4)]
    JOBS += [("dftx", hf, j) for j in range(2)]
JOBS += [("mix", j) for j in range(KYG)]
JOBS += [("back", bq, ri) for bq in range(BQ) for ri in range(2)]
JOBS += [("idftx", j) for j in range(8)]
JOBS += [("out", j) for j in range(16)]
NJ = len(JOBS)
POS = BANKS * ((NJ + BANKS - 1) // BANKS)
assert NJ == POS - 1


def on_act(j):
    return JOBS[j][0] == "out" or j % 2 == 0


ACT_N = sum(on_act(j) for j in range(NJ))
DVE_N = NJ - ACT_N


def emptied(j):
    a = sum(on_act(i) for i in range(j + 1))
    return a, j + 1 - a


def first(kind, *rest):
    return min(i for i, job in enumerate(JOBS) if job[:1 + len(rest)] == (kind,) + rest)


def last(kind, *rest):
    return max(i for i, job in enumerate(JOBS) if job[:1 + len(rest)] == (kind,) + rest)


TAIL = []
for kind, n in (("hT", CHUNKS), ("h", 4), ("xnT", 8), ("qkv", 16), ("knorm", 2), ("kv", 8), ("qT", 8), ("attnT", 8),
                ("proj", 4), ("x2T", 8), ("gate", 1), ("combT", 8), ("b2", 4)):
    TAIL += [(kind, j) for j in range(n)]
TAIL_ACT = ("xnT", "qkv", "qT", "attnT", "x2T", "combT")


def tail_no(kind, j):
    return TAIL.index((kind, j))


def tail_count(n):
    a = sum(k in TAIL_ACT for k, _ in TAIL[:n + 1])
    return a, n + 1 - a


def build(nc, x_f, p_w, w_bd, w_b, spec_w, bn_g, bn_b, q_bd, q_b, wqkv, wout, wgate, w1t, w2t, b2,
          c_fy, c_g, c_gi, c_fyi, c_id, c_avg, c_ones, out):
    ctx = ExitStack()
    with ctx:
        def sb(name, cols, parts=P):
            return ctx.enter_context(nc.sbuf_tensor(name, [parts, cols], F32))

        def sem(name):
            return ctx.enter_context(nc.semaphore(name))

        bank = [ctx.enter_context(nc.psum_tensor(f"bank{i}", [P, 512], F32)) for i in range(BANKS)]
        u_dram = nc.dram_tensor("u_scratch", [CHUNKS, P, COLS], F32, kind="Internal").ap()

        v = [sb("v0", COLS), sb("v1", COLS)]
        w_spec = sb("w_spec", KYG * KX * 2 * P)
        pix = sb("pix", 4096)
        fy_out = sb("fy_out", 2 * 2 * M * C)
        xs = sb("xs", KYG * 3 * CH * KX)
        os_ = sb("os", KYG * CH * KX * 3)
        turned = sb("turned", BQ * 32 * C)
        fy = sb("fy", 2 * 2 * M)
        gx = sb("gx", 2 * 96)
        gi = sb("gi", P)
        fyi = sb("fyi", BQ * S)
        wconv = sb("wconv", P)
        ident = sb("ident", P)
        avg = sb("avg", P)
        ones = sb("ones", P)
        pw = sb("pw", P)
        chan = sb("chan", 4 * LAYERS)
        qbd = sb("qbd", 8)
        stats = sb("stats", CHUNKS * 16 * 6)
        bnw = sb("bnw", 16)
        wb_now = sb("wb_now", 1)
        sc = sb("sc", 4)

        hT = turned[:, 0:2048]
        h = turned[:, 2048:4096]
        qkv = w_spec[:, 0:6144]
        w1s = w_spec[0:65, 6144:6144 + 2048]
        w2s = w_spec[:, 8192:8192 + 1024]
        wk = w_spec[:, 9216:9216 + 8192]
        xnT = v[0][0:65, 0:4096]
        qT = v[0][0:64, 4096:8192]
        atT = v[1][0:65, 0:4096]
        kvs = v[1][0:64, 4096:8192]
        hb = [pix[:, 0:1024], pix[:, 1024:2048]]
        xn = pix[:, 2048:4096]
        y_w = xs[:, 0:512]
        small = os_
        wq_s = fy_out[0:65, 0:192]
        wo_s = fy_out[0:65, 192:256]
        wg_s = fy_out[0:65, 256:264]
        b2_s = fy_out[0:8, 264:328]

        const_in = sem("const_in")
        field_in = [sem("field_in0"), sem("field_in1")]
        field_out = [sem("field_out0"), sem("field_out1")]
        field_mm = sem("field_mm")
        field_cp = sem("field_cp")
        v_in = [[sem(f"v_in{p}{q}") for q in range(4)] for p in range(2)]
        v_out = [[sem(f"v_out{p}{q}") for q in range(4)] for p in range(2)]
        w_in = sem("w_in")
        w_zero = sem("w_zero")
        v_act = sem("v_act")
        v_half = sem("v_half")
        pe_job = sem("pe_job")
        act_job = sem("act_job")
        dve_job = sem("dve_job")
        stat_done = sem("stat_done")
        bn_agg = sem("bn_agg")
        bn_mm = sem("bn_mm")
        bn_dev = sem("bn_dev")
        bn_var = sem("bn_var")
        bn_sqrt = sem("bn_sqrt")
        sc_ready = sem("sc_ready")
        dve_chain = sem("dve_chain")
        a_ready = sem("a_ready")
        tail_in = sem("tail_in")
        fin_in = [sem("fin_in0"), sem("fin_in1")]
        pe_tail = sem("pe_tail")
        act_tail = sem("act_tail")
        dve_tail = sem("dve_tail")
        s_step = sem("s_step")
        a_step = sem("a_step")
        hid_mm = sem("hid_mm")
        hid_relu = sem("hid_relu")
        y_mm = sem("y_mm")
        y_done = sem("y_done")
        out_done = sem("out_done")
        s_root = sem("s_root")
        y_mm_free = sem("y_mm_free")

        passed = {e: sem(f"passed_{e}") for e in ("pe", "dve", "pool", "sp")}

        def stop_for(eng, name, signal, value):
            eng.wait_ge(signal, value)
            eng.sem_inc(passed[name], 1)

        CONSTS = [(fy, c_fy), (gx, c_g), (fyi, c_fyi), (ident, c_id), (avg, c_avg), (ones, c_ones)]

        block = ctx.enter_context(nc.Block())

        @block.sync
        def _(sp):
            for dst, src in CONSTS:
                sp.dma_start(dst[:, :], src).then_inc(const_in, 16)
            sp.dma_start(gi[0:96, :], c_gi).then_inc(const_in, 16)
            sp.dma_start(pw[0:16, :], p_w).then_inc(const_in, 16)
            sp.dma_start(chan[:, 0:LAYERS], w_b).then_inc(const_in, 16)
            sp.dma_start(chan[:, LAYERS:2 * LAYERS], bn_g).then_inc(const_in, 16)
            sp.dma_start(chan[:, 2 * LAYERS:3 * LAYERS], bn_b).then_inc(const_in, 16)
            sp.dma_start(qbd[:, 0:4], q_bd).then_inc(const_in, 16)
            sp.dma_start(qbd[:, 4:5], q_b).then_inc(const_in, 16)

            fbuf = [pix, turned]
            with sp.Fori(0, CHUNKS) as c:
                for half in range(2):
                    stop_for(sp, "sp", field_mm, c * 16 + (half * 8 + 8))
                    sp.dma_start(fbuf[half][0:16, :],
                                 x_f[bass.ds(c, 1), :, half * 4096:(half + 1) * 4096].rearrange("a p n -> (a p) n"))\
                      .then_inc(field_in[half], 16)
            for half in range(2):
                sp.wait_ge(field_out[half], 16 + 16 * CHUNKS)

            with sp.Fori(0, LAYERS) as l:
                sp.wait_ge(w_zero, 1)
                stop_for(sp, "sp", sc_ready, l + 1)
                sp.dma_start(wconv[:, :], w_bd[bass.ds(l, 1)].rearrange("a p n -> (a p) n")).then_inc(w_in, 16)
                for g in range(4):
                    sp.dma_start(w_spec[32 * g:32 * g + 32, :].rearrange("p (m k) -> p m k", k=P)[:, :, 32 * g:32 * g + 32],
                                 spec_w[bass.ds(l, 1), 32 * g:32 * g + 32, :].rearrange("a p (m o) -> (a p) m o", o=C))\
                      .then_inc(w_in, 16)
                with sp.Fori(0, CHUNKS // 2) as i:
                    for p in range(2):
                        for q in range(4):
                            stop_for(sp, "sp", v_out[p][q], (l * 4 + i) * 16 + 16)
                            stop_for(sp, "sp", stat_done, (l * 4 + i) * 32 + 16 * p)
                            sp.dma_start(v[p][:, q * QUART:(q + 1) * QUART],
                                         u_dram[bass.ds(i * 2 + p, 1), :, q * QUART:(q + 1) * QUART]
                                         .rearrange("a p n -> (a p) n")).then_inc(v_in[p][q], 16)

            sp.wait_ge(stat_done, 16 + 16 * CHUNKS * LAYERS)
            for p in range(2):
                for q in range(4):
                    sp.wait_ge(v_out[p][q], 16 + 16 * LAYERS * CHUNKS // 2)
            sp.wait_ge(pe_job, NJ * CHUNKS * LAYERS)
            for dst, src in ((w1s, w1t), (w2s, w2t), (wq_s, wqkv), (wo_s, wout), (wg_s, wgate), (b2_s, b2)):
                sp.dma_start(dst, src).then_inc(tail_in, 16)
            for c in range(CHUNKS):
                if c >= 2:
                    sp.wait_ge(pe_tail, c - 1)
                sp.dma_start(v[c % 2][:, :], u_dram[c]).then_inc(fin_in[c % 2], 16)
            sp.wait_ge(y_done, 8)
            sp.dma_start(out.rearrange("(t b) x y -> (b x) t y", b=B2), h.rearrange("p (t y) -> p t y", y=D))\
              .then_inc(out_done, 16)
            sp.wait_ge(out_done, 16)

        @block.tensor
        def _(pe):
            pe.wait_ge(const_in, 16 * (len(CONSTS) + 7))
            pe.sem_inc(field_mm, 16)
            with pe.Fori(0, CHUNKS) as c:
                for j in range(16):
                    if j % 8 == 0:
                        pe.wait_ge(field_in[j // 8], c * 16 + 16)
                    pe.wait_ge(field_cp, c * 16 + (j + 1))
                    src = (pix, turned)[j // 8]
                    pe.matmul(bank[j % 8][:, :], pw[0:16, :], src[0:16, (j % 8) * 512:(j % 8 + 1) * 512],
                              start=True, stop=True).then_inc(field_mm, 1)

            def wait_emptied(g, j):
                a, d = emptied(j)
                pe.wait_ge(act_job, g * ACT_N + (ACT_N + a))
                pe.wait_ge(dve_job, g * DVE_N + (DVE_N + d))

            def wait_bank(g, j):
                before = j - BANKS if j >= BANKS else min(j - BANKS + POS, NJ - 1 if j % 8 < 7 else NJ - 8)
                a, d = emptied(before)
                if j < BANKS:
                    a, d = a - ACT_N, d - DVE_N
                if on_act(before):
                    pe.wait_ge(act_job, g * ACT_N + (ACT_N + a))
                else:
                    pe.wait_ge(dve_job, g * DVE_N + (DVE_N + d))

            def run(g, j, par):
                job = JOBS[j]
                kind = job[0]
                ps = bank[j % 8]
                wait_bank(g, j)
                if kind == "turn":
                    _, hf, n = job
                    bq, quad = 2 * hf + n // 4, n % 4
                    if n == 0 and hf == 0:
                        pe.wait_ge(v_act, g * 4 + 4)
                    for k in range(4):
                        at = ((4 * quad + k) * BQ + bq) * P
                        mm = pe.transpose(ps[:, k * P:(k + 1) * P], v[par][:, at:at + P], ident[:, :])
                elif kind == "dfty":
                    _, hf, n = job
                    if n == 0:
                        wait_emptied(g, last("turn", hf))
                    for k in range(8):
                        c = 8 * n + k
                        mm = pe.matmul(ps[:, k * 48:(k + 1) * 48],
                                       pix[:, :].rearrange("p (m c) -> p m c", c=C)[:, :, c], fy[:, :],
                                       start=True, stop=True)
                elif kind == "dftx":
                    _, hf, b2_ = job
                    if b2_ == 0:
                        wait_emptied(g, last("dfty", hf))
                    for kyg in range(KYG):
                        for ri in range(2):
                            at = b2_ * 768 + ri * 384 + kyg * P
                            mm = pe.matmul(ps[:, kyg * 96:(kyg + 1) * 96], fy_out[:, at:at + P],
                                           gx[:, ri * 96:(ri + 1) * 96], start=(ri == 0), stop=(ri == 1))
                elif kind == "mix":
                    kyg = job[1]
                    if kyg == 0:
                        wait_emptied(g, last("dftx"))
                    xv = xs[:, kyg * 576:(kyg + 1) * 576].rearrange("p (r b k) -> p r b k", r=3, b=CH)
                    for kx in range(KX):
                        for ri in range(2):
                            at = ((kyg * KX + kx) * 2 + ri) * P
                            mm = pe.matmul(ps[:, kx * 16:(kx + 1) * 16], w_spec[:, at:at + P],
                                           xv[:, 1 - ri:3 - ri, :, kx], start=(ri == 0), stop=(ri == 1))
                elif kind == "back":
                    _, bq, ri = job
                    if bq == 0 and ri == 0:
                        wait_emptied(g, last("mix"))
                    for kyg in range(KYG):
                        at = kyg * 576 + bq * 144 + ri * 48
                        mm = pe.transpose(ps[0:96, kyg * P:(kyg + 1) * P], os_[:, at:at + 96], ident[:, :])
                elif kind == "idftx":
                    n = job[1]
                    if n == 0:
                        wait_emptied(g, last("back"))
                    for k in range(4):
                        mm = pe.matmul(ps[:, k * P:(k + 1) * P],
                                       turned[0:96, :].rearrange("p (m o) -> p m o", o=C)[:, :, 4 * n + k],
                                       gi[0:96, :], start=True, stop=True)
                else:
                    n = job[1]
                    if n == 0:
                        wait_emptied(g, last("idftx"))
                    for k in range(2):
                        pe.matmul(ps[:, :].rearrange("p (q b y) -> p q b y", q=BQ, b=B2)[:, :, k],
                                  pix[:, (XR * k + n) * P:(XR * k + n + 1) * P], fyi[:, :],
                                  start=(k == 0), stop=False)
                    mm = pe.matmul(ps[:, :], wconv[:, :], v[par][:, n * 512:(n + 1) * 512], start=False, stop=True)
                mm.then_inc(pe_job, 1)

            pe.wait_ge(field_cp, 8 + 16 * CHUNKS)
            with pe.Fori(0, LAYERS) as l:
                stop_for(pe, "pe", w_in, l * 80 + 80)
                with pe.Fori(0, CHUNKS // 2) as i:
                    for par in range(2):
                        g = (l * 4 + i) * 2 + par
                        for j in range(NJ):
                            run(g, j, par)
                pe.wait_ge(bn_agg, l + 1)
                pe.matmul(bank[7][:, 0:1], avg[:, :], bnw[:, 0:1], start=True, stop=True).then_inc(bn_mm, 1)
                pe.wait_ge(bn_dev, l + 1)
                pe.matmul(bank[7][:, 8:9], avg[:, :], bnw[:, 2:3], start=True, stop=True).then_inc(bn_mm, 1)
                stop_for(pe, "pe", sc_ready, l + 2)

            def start_tail(kind, j):
                n = tail_no(kind, j)
                if n >= BANKS:
                    tail_wait(n - BANKS)
                return bank[n % BANKS]

            def tail_wait(n):
                a, d = tail_count(n)
                if a:
                    pe.wait_ge(act_tail, a)
                if d:
                    pe.wait_ge(dve_tail, d)

            pe.wait_ge(tail_in, 16 * 6)
            pe.wait_ge(a_ready, 1)
            pe.matmul(bank[7][:, 0:1], wk[:, 0:P], qbd[:, 0:1], start=True, stop=True).then_inc(bn_mm, 1)
            pe.wait_ge(a_ready, 2)
            for c in range(CHUNKS):
                ps = start_tail("hT", c)
                pe.wait_ge(fin_in[c % 2], 16 * (c // 2 + 1))
                for n in range(64):
                    mm = pe.matmul(ps[:, n * 4:n * 4 + 4], v[c % 2][:, n * P:(n + 1) * P], bnw[:, 8:12],
                                   start=True, stop=True)
                mm.then_inc(pe_tail, 1)
            for j in range(4):
                ps = start_tail("h", j)
                if j == 0:
                    tail_wait(tail_no("hT", CHUNKS - 1))
                for k in range(4):
                    n = 4 * j + k
                    mm = pe.transpose(ps[:, k * P:(k + 1) * P], hT[:, n * P:(n + 1) * P], ident[:, :])
                mm.then_inc(pe_tail, 1)

            def flip(kind, src, width, step):
                for j in range(8):
                    ps = start_tail(kind, j)
                    if j == 0:
                        pe.wait_ge(s_step, step)
                    for k in range(4):
                        mm = pe.transpose(ps[0:width, k * P:(k + 1) * P], src(4 * j + k), ident[:, :])
                    mm.then_inc(pe_tail, 1)

            flip("xnT", lambda t: xn[:, t * D:(t + 1) * D], D, 1)
            for j in range(16):
                ps = start_tail("qkv", j)
                if j == 0:
                    tail_wait(tail_no("xnT", 7))
                for k in range(2):
                    t = 2 * j + k
                    mm = pe.matmul(ps[:, k * 192:(k + 1) * 192], xnT[:, t * P:(t + 1) * P], wq_s, start=True, stop=True)
                mm.then_inc(pe_tail, 1)
            for b in range(2):
                ps = start_tail("knorm", b)
                pe.wait_ge(s_step, 2)
                for t in range(TILES):
                    mm = pe.matmul(ps[0:D, t:t + 1], wk[64 * b:64 * b + 64, 4096 + t * D:4096 + (t + 1) * D],
                                   ones[64 * b:64 * b + 64, 0:1], start=True, stop=True)
                mm.then_inc(pe_tail, 1)
            k_v = wk[:, 0:4096].rearrange("p (t a c) -> p t a c", a=2, c=D)
            for j in range(8):
                ps = start_tail("kv", j)
                for k in range(8):
                    t, b = 8 * (j % 4) + k, j // 4
                    mm = pe.matmul(ps[0:D, k * D:(k + 1) * D], k_v[64 * b:64 * b + 64, t, 1, :],
                                   qkv[64 * b:64 * b + 64, t * 192 + 128:t * 192 + 192], start=True, stop=True)
                mm.then_inc(pe_tail, 1)
            flip("qT", lambda t: xn[:, t * D:(t + 1) * D], D, 3)
            for j in range(8):
                ps = start_tail("attnT", j)
                if j == 0:
                    tail_wait(tail_no("qT", 7))
                for k in range(8):
                    b = 8 * j + k
                    pe.matmul(ps[0:D, k * D:(k + 1) * D], kvs[:, (32 * (b % 2) + b // 2) * D:(32 * (b % 2) + b // 2 + 1) * D], qT[:, b * D:(b + 1) * D],
                              start=(k == 0), stop=False)
                mm = pe.matmul(ps[0:D, :], wq_s[:, 128:192], xnT[:, j * 512:(j + 1) * 512], start=False, stop=True)
                mm.then_inc(pe_tail, 1)
            for j in range(4):
                ps = start_tail("proj", j)
                if j == 0:
                    tail_wait(tail_no("attnT", 7))
                for k in range(8):
                    t = 8 * j + k
                    mm = pe.matmul(ps[:, k * D:(k + 1) * D], atT[:, t * P:(t + 1) * P], wo_s, start=True, stop=True)
                mm.then_inc(pe_tail, 1)
            flip("x2T", lambda t: xn[:, t * D:(t + 1) * D], D, 4)
            ps = start_tail("gate", 0)
            tail_wait(tail_no("x2T", 7))
            for t in range(TILES):
                mm = pe.matmul(ps[:, t * E:(t + 1) * E], xnT[:, t * P:(t + 1) * P], wg_s, start=True, stop=True)
            mm.then_inc(pe_tail, 1)
            flip("combT", lambda t: small[:, t * E:(t + 1) * E], E, 5)
            for j in range(4):
                ps = start_tail("b2", j)
                if j == 0:
                    tail_wait(tail_no("combT", 7))
                for k in range(8):
                    t = 8 * j + k
                    mm = pe.matmul(ps[:, k * D:(k + 1) * D], qT[0:E, t * P:(t + 1) * P], b2_s, start=True, stop=True)
                mm.then_inc(pe_tail, 1)
            tail_wait(len(TAIL) - 1)
            pe.sem_inc(y_mm, 2)
            with pe.Fori(0, 8) as tg:
                def hidden(e):
                    for half in range(2):
                        n = 2 * e + half
                        pe.wait_ge(hid_relu, tg * 16 + (n + 1))
                        pe.matmul(bank[n % 4][:, :], w1s[:, e * H + half * P:e * H + (half + 1) * P],
                                  xnT[:, bass.ds(tg * 512, 512)], start=True, stop=True).then_inc(hid_mm, 1)

                def outputs(e):
                    pe.wait_ge(hid_relu, tg * 16 + (2 * e + 6))
                    pe.wait_ge(y_mm_free, tg * 8 + (e + 1))
                    for k in range(4):
                        for half in range(2):
                            mm = pe.matmul(bank[6 + e % 2][:, k * D:(k + 1) * D],
                                           hb[e % 2][:, half * 512 + k * P:half * 512 + (k + 1) * P],
                                           w2s[:, (2 * e + half) * D:(2 * e + half + 1) * D],
                                           start=(half == 0), stop=(half == 1))
                    mm.then_inc(y_mm, 1)

                hidden(0)
                for e in range(E):
                    if e + 1 < E:
                        hidden(e + 1)
                    outputs(e)

        def unload(eng, copy, neg, j, par):
            job = JOBS[j]
            kind = job[0]
            ps = bank[j % 8]
            if kind == "turn":
                _, hf, n = job
                bqi, quad = n // 4, n % 4
                dst = pix[:, bqi * 2048:(bqi + 1) * 2048].rearrange("p (q x c) -> p x q c", q=XQ, x=XR)
                return copy(dst[:, 4 * quad:4 * quad + 4], ps[:, :].rearrange("p (x q c) -> p x q c", x=4, q=XQ))
            if kind == "dfty":
                n = job[2]
                dst = fy_out[:, :].rearrange("p (m c) -> p c m", c=C)
                return copy(dst[:, 8 * n:8 * n + 8, :], ps[:, 0:384].rearrange("p (c m) -> p c m", c=8))
            if kind == "dftx":
                _, hf, b2_ = job
                dst = xs[:, :].rearrange("p (g r b m) -> p g r b m", g=KYG, r=3, b=B2)
                src = ps[:, 0:288].rearrange("p (g r m) -> p g r m", g=KYG, r=2)
                copy(dst[:, :, 1:3, b2_, hf * 48:hf * 48 + 48], src)
                return neg(dst[:, :, 0, b2_, hf * 48:hf * 48 + 48], src[:, :, 1])
            if kind == "mix":
                kyg = job[1]
                dst = os_[:, kyg * 576:(kyg + 1) * 576].rearrange("p (q m k) -> p q m k", q=BQ, m=3 * B2)
                src = ps[:, 0:384].rearrange("p (k m q) -> p q m k", m=2 * B2, q=BQ)
                copy(dst[:, :, 0:4], src)
                return neg(dst[:, :, 4:6], src[:, :, 0:2])
            if kind == "back":
                _, bq, ri = job
                at = bq * 1024 + ri * 384
                return copy(turned[0:96, at:at + 384], ps[0:96, 0:384])
            if kind == "idftx":
                n = job[1]
                dst = pix[:, :].rearrange("p (m o) -> p o m", o=C)
                return copy(dst[:, 4 * n:4 * n + 4, :], ps[:, :].rearrange("p (o m) -> p o m", o=4))

        @block.scalar
        def _(act):
            def copy(dst, src):
                return act.activation(dst, src, ACT.Copy)

            def neg(dst, src):
                return act.activation(dst, src, ACT.Copy, scale=-1.0)

            act.wait_ge(const_in, 16 * (len(CONSTS) + 7))
            act.sem_inc(act_job, ACT_N)
            act.sem_inc(field_cp, 8)
            for half in range(2):
                act.sem_inc(field_out[half], 16)
            for p in range(2):
                for q in range(4):
                    act.sem_inc(v_out[p][q], 16)
            with act.Fori(0, CHUNKS) as c:
                for half in range(2):
                    act.wait_ge(field_out[half], c * 16 + 16)
                    for j in range(8):
                        n = 8 * half + j
                        act.wait_ge(field_mm, c * 16 + (n + 17))
                        act.activation(v[half][:, j * 512:(j + 1) * 512], bank[j][:, :], ACT.Copy).then_inc(field_cp, 1)
                    act.wait_ge(field_cp, c * 16 + (8 + 8 * half + 8))
                    act.dma_start(u_dram[bass.ds(c, 1), :, half * 4096:(half + 1) * 4096].rearrange("a p n -> (a p) n"),
                                  v[half][:, 0:4096]).then_inc(field_out[half], 16)

            with act.Fori(0, LAYERS) as l:
                with act.Fori(0, CHUNKS // 2) as i:
                    for par in range(2):
                        g = (l * 4 + i) * 2 + par
                        for j in range(NJ):
                            if not on_act(j):
                                continue
                            act.wait_ge(pe_job, g * NJ + (j + 1))
                            if JOBS[j][0] != "out":
                                unload(act, copy, neg, j, par).then_inc(act_job, 1)
                                continue
                            n = JOBS[j][1]
                            act.activation(v[par][:, n * 512:(n + 1) * 512], bank[j % 8][:, :], ACT.Identity,
                                           bias=wb_now[:, 0:1]).then_inc(act_job, 1)
                            if n % 4 == 3:
                                q = n // 4
                                act.wait_ge(act_job, g * ACT_N + (ACT_N + emptied(j)[0]))
                                act.dma_start(u_dram[bass.ds(i * 2 + par, 1), :, q * QUART:(q + 1) * QUART]
                                              .rearrange("a p n -> (a p) n"),
                                              v[par][:, q * QUART:(q + 1) * QUART]).then_inc(v_out[par][q], 16)
                act.wait_ge(bn_var, l + 1)
                act.activation(bnw[:, 4:5], bnw[:, 3:4], ACT.Sqrt).then_inc(bn_sqrt, 1)

            def empty(kind, dst, rows, cols):
                for j in range(sum(k == kind for k, _ in TAIL)):
                    n = tail_no(kind, j)
                    act.wait_ge(pe_tail, n + 1)
                    act.activation(dst(j), bank[n % BANKS][0:rows, 0:cols], ACT.Copy).then_inc(act_tail, 1)

            def root(step, dst, src):
                act.wait_ge(s_root, step)
                act.activation(dst, src, ACT.Sqrt).then_inc(a_step, 1)

            root(1, small[:, 320:352], small[:, 288:320])
            empty("xnT", lambda j: xnT[0:D, j * 512:(j + 1) * 512], D, 512)
            empty("qkv", lambda j: qkv[:, j * 384:(j + 1) * 384], P, 384)
            root(2, small[:, 320:352], small[:, 288:320])
            root(3, small[0:D, 448:512], small[0:D, 384:448])
            empty("qT", lambda j: qT[0:D, j * 512:(j + 1) * 512], D, 512)
            empty("attnT", lambda j: atT[0:D, j * 512:(j + 1) * 512], D, 512)
            root(4, small[:, 320:352], small[:, 288:320])
            empty("x2T", lambda j: xnT[0:D, j * 512:(j + 1) * 512], D, 512)
            act.wait_ge(s_root, 5)
            act.activation(small[:, 320:352], small[:, 288:320], ACT.Exp).then_inc(a_step, 1)
            empty("combT", lambda j: qT[0:E, j * 512:(j + 1) * 512], E, 512)
            act.sem_inc(hid_relu, 4)
            with act.Fori(0, 8) as tg:
                for e in range(E):
                    act.wait_ge(y_mm, tg * 8 + (e + 1))
                    for half in range(2):
                        n = 2 * e + half
                        act.wait_ge(hid_mm, tg * 16 + (n + 1))
                        act.activation(hb[e % 2][:, half * 512:(half + 1) * 512], bank[n % 4][:, :], ACT.Relu)\
                           .then_inc(hid_relu, 1)

        @block.vector
        def _(dve):
            chained = [0]

            def link(ins):
                chained[0] += 1
                ins.then_inc(dve_chain, 1)
                dve.wait_ge(dve_chain, chained[0])

            def copy(dst, src):
                return dve.tensor_copy(dst, src)

            def neg(dst, src):
                return dve.tensor_scalar(dst, src, -1.0, None, ALU.mult)

            dve.wait_ge(const_in, 16 * (len(CONSTS) + 7))
            dve.sem_inc(dve_job, DVE_N)
            dve.sem_inc(stat_done, 16)
            dve.memset(w_spec[:, :], 0.0).then_inc(w_zero, 1)
            dve.memset(sc[:, 0:1], 1.0)
            dve.memset(sc[:, 1:2], 0.0)
            link(dve.memset(sc[:, 2:3], -3.0e38))
            dve.wait_ge(field_mm, 16 + 16 * CHUNKS)
            link(dve.memset(turned[:, :], 0.0))
            link(dve.tensor_copy(wb_now[:, 0:1], chan[:, 0:1]))
            dve.sem_inc(sc_ready, 1)
            before_layers = chained[0]

            with dve.Fori(0, LAYERS) as l:
                with dve.Fori(0, CHUNKS // 2) as i:
                    for par in range(2):
                        g = (l * 4 + i) * 2 + par

                        def stat(n):
                            stop_for(dve, "dve", act_job, g * ACT_N + (ACT_N + emptied(first("out") + n)[0]))
                            at = (i * 2 + par) * 96 + n * 6
                            dve.bn_stats(stats[:, bass.ds(at, 6)], v[par][:, n * 512:(n + 1) * 512])\
                               .then_inc(stat_done, 1)

                        for j in range(NJ):
                            if JOBS[j][0] == "out":
                                stat(JOBS[j][1])
                            elif not on_act(j):
                                dve.wait_ge(pe_job, g * NJ + (j + 1))
                                unload(dve, copy, neg, j, par).then_inc(dve_job, 1)
                steps = [0]

                def step(ins):
                    steps[0] += 1
                    ins.then_inc(dve_chain, 1)
                    dve.wait_ge(dve_chain, l * BN_STEPS + (before_layers + steps[0]))

                stop_for(dve, "dve", stat_done, l * (16 * CHUNKS) + (16 + 16 * CHUNKS))
                step(dve.bn_aggr(bnw[:, 0:2], stats[:, :]))
                dve.sem_inc(bn_agg, 1)
                dve.wait_ge(bn_mm, l * 2 + 1)
                step(dve.tensor_copy(bnw[:, 5:6], bank[7][:, 0:1]))
                step(dve.tensor_tensor(bnw[:, 6:7], bnw[:, 0:1], bnw[:, 5:6], ALU.subtract))
                step(dve.scalar_tensor_tensor(out=bnw[:, 2:3], in0=bnw[:, 6:7], scalar=bnw[:, 6:7],
                                              in1=bnw[:, 1:2], op0=ALU.mult, op1=ALU.add))
                dve.sem_inc(bn_dev, 1)
                dve.wait_ge(bn_mm, l * 2 + 2)
                step(dve.tensor_scalar(bnw[:, 3:4], bank[7][:, 8:9], BN_EPS, None, ALU.add))
                dve.sem_inc(bn_var, 1)
                dve.wait_ge(bn_sqrt, l + 1)
                step(dve.reciprocal(bnw[:, 6:7], bnw[:, 4:5]))
                step(dve.scalar_tensor_tensor(out=bnw[:, 7:8], in0=bnw[:, 6:7], scalar=bnw[:, 3:4],
                                              in1=bnw[:, 4:5], op0=ALU.mult, op1=ALU.add))
                step(dve.tensor_scalar(bnw[:, 6:7], bnw[:, 7:8], 0.5, None, ALU.mult))
                step(dve.reciprocal(bnw[:, 7:8], bnw[:, 6:7]))
                step(dve.tensor_tensor(sc[:, 0:1], bnw[:, 7:8], chan[:, bass.ds(l + LAYERS, 1)], ALU.mult))
                step(dve.tensor_tensor(bnw[:, 6:7], sc[:, 0:1], bnw[:, 5:6], ALU.mult))
                step(dve.tensor_tensor(sc[:, 1:2], chan[:, bass.ds(l + 2 * LAYERS, 1)], bnw[:, 6:7], ALU.subtract))
                step(dve.memset(sc[:, 2:3], 0.0))
                step(dve.tensor_copy(wb_now[:, 0:1], chan[:, bass.ds(l + 1, 1)]))
                dve.sem_inc(sc_ready, 1)
                assert steps[0] == BN_STEPS
            chained[0] = before_layers + LAYERS * BN_STEPS

            link(dve.tensor_scalar(bnw[:, 8:12], qbd[:, 0:4], sc[:, 0:1], None, ALU.mult))
            dve.wait_ge(pe_job, NJ * CHUNKS * LAYERS)
            link(dve.tensor_scalar(wk[:, 0:P], ones[:, :], sc[:, 1:2], None, ALU.mult))
            dve.sem_inc(a_ready, 1)
            dve.wait_ge(bn_mm, 2 * LAYERS + 1)
            link(dve.tensor_tensor(bnw[:, 12:13], bank[7][:, 0:1], qbd[:, 4:5], ALU.add))
            dve.sem_inc(a_ready, 1)
            for c in range(CHUNKS):
                n = tail_no("hT", c)
                dve.wait_ge(pe_tail, n + 1)
                for bqh in range(2):
                    dst = hT[:, (2 * c + bqh) * P:(2 * c + bqh + 1) * P].rearrange("p (b q x) -> p b x q", b=2, q=XQ)
                    src = bank[n % BANKS][:, 0:256].rearrange("p (x h b q) -> p h b x q", x=XR, h=2, b=2)[:, bqh]
                    ins = dve.tensor_scalar(dst, src, bnw[:, 12:13], None, ALU.add)
                ins.then_inc(dve_tail, 1)
            for j in range(4):
                n = tail_no("h", j)
                dve.wait_ge(pe_tail, n + 1)
                dve.tensor_copy(h[:, j * 512:(j + 1) * 512], bank[n % BANKS][:, :]).then_inc(dve_tail, 1)
            dve.wait_ge(dve_tail, tail_count(tail_no("h", 3))[1])

            def root_of(dst, a, r, tmp, s_val, a_val, floor=None):
                dve.sem_inc(s_root, 1)
                dve.wait_ge(a_step, a_val)
                if floor is not None:
                    link(dve.tensor_scalar(r, r, floor, None, ALU.max))
                link(dve.reciprocal(tmp, r))
                link(dve.tensor_tensor(tmp, tmp, a, ALU.mult))
                link(dve.tensor_tensor(tmp, tmp, r, ALU.add))
                link(dve.tensor_scalar(tmp, tmp, 0.5, floor, ALU.mult, ALU.max) if floor is not None
                     else dve.tensor_scalar(tmp, tmp, 0.5, None, ALU.mult))
                link(dve.reciprocal(dst, tmp))

            def wide(ap, n=TILES):
                return ap.rearrange("p (t y) -> p t y", y=D)

            def spread(ap, n=TILES):
                return ap.unsqueeze(2).to_broadcast([P, n, D])

            sq = wk[:, 4096:6144]

            def norm_rows(step_no):
                m, var, r, tmp, inv = (small[:, 256 + 32 * k:288 + 32 * k] for k in range(5))
                link(dve.tensor_reduce(m, wide(h), AX.X, ALU.add))
                link(dve.tensor_scalar(m, m, 1.0 / D, None, ALU.mult))
                link(dve.tensor_tensor(wide(xn), wide(h), spread(m), ALU.subtract))
                link(dve.tensor_tensor(sq, xn, xn, ALU.mult))
                link(dve.tensor_reduce(var, wide(sq), AX.X, ALU.add))
                link(dve.tensor_scalar(var, var, 1.0 / D, LN_EPS, ALU.mult, ALU.add))
                root_of(inv, var, r, tmp, 0, step_no)
                link(dve.tensor_tensor(wide(xn), wide(xn), spread(inv), ALU.mult))
                dve.sem_inc(s_step, 1)

            dve.memset(xnT[D:D + 1, :], 1.0)
            link(dve.memset(atT[D:D + 1, :], 1.0))
            norm_rows(1)
            dve.wait_ge(act_tail, tail_count(tail_no("qkv", 15))[0])
            qk = qkv.rearrange("p (t a c) -> p t a c", a=3, c=D)[:, :, 0:2]
            qk2 = wk[:, 0:4096].rearrange("p (t a c) -> p t a c", a=2, c=D)
            sums = small[:, 512:576]
            sums2 = sums.rearrange("p (t a) -> p t a", a=2)
            bsum = sums2.unsqueeze(3).to_broadcast([P, TILES, 2, D])
            link(dve.tensor_reduce(sums2, qk, AX.X, ALU.add))
            link(dve.tensor_scalar(sums, sums, 1.0 / D, None, ALU.mult))
            link(dve.tensor_tensor(qk2, qk, bsum, ALU.subtract))
            link(dve.tensor_tensor(wk[:, 0:4096], wk[:, 0:4096], wk[:, 0:4096], ALU.mult))
            link(dve.tensor_reduce(sums2, qk2, AX.X, ALU.add))
            link(dve.tensor_scalar(sums, sums, 1e-7, None, ALU.add))
            link(dve.reciprocal(sums, sums))
            link(dve.tensor_tensor(qk2, qk2, bsum, ALU.mult))
            link(dve.tensor_tensor(wide(sq), qk2[:, :, 1], qk2[:, :, 1], ALU.mult))
            dve.sem_inc(s_step, 1)
            link(dve.tensor_tensor(wide(xn), qk2[:, :, 0], qk2[:, :, 0], ALU.mult))
            link(dve.tensor_reduce(small[:, 288:320], wide(xn), AX.X, ALU.add))
            root_of(small[:, 384:416], small[:, 288:320], small[:, 320:352], small[:, 352:384], 0, 2, floor=1e-12)
            link(dve.tensor_tensor(wide(xn), qk2[:, :, 0], spread(small[:, 384:416]), ALU.mult))
            dve.sem_inc(s_step, 1)
            for b in range(2):
                n = tail_no("knorm", b)
                dve.wait_ge(pe_tail, n + 1)
                dve.tensor_copy(small[0:D, 384 + 32 * b:416 + 32 * b], bank[n % BANKS][0:D, 0:32]).then_inc(dve_tail, 1)
            dve.wait_ge(dve_tail, tail_count(n)[1])
            root_of(small[0:D, 640:704], small[0:D, 384:448], small[0:D, 448:512], small[0:D, 576:640], 0, 3, floor=1e-12)
            link(dve.tensor_scalar(small[0:D, 640:704], small[0:D, 640:704], float(S) ** -0.5, None, ALU.mult))
            for j in range(8):
                n = tail_no("kv", j)
                dve.wait_ge(pe_tail, n + 1)
                dve.tensor_tensor(wide(kvs[:, j * 512:(j + 1) * 512]), wide(bank[n % BANKS][0:D, :]),
                                  small[0:D, 640 + 8 * j:648 + 8 * j].unsqueeze(2).to_broadcast([D, 8, D]),
                                  ALU.mult).then_inc(dve_tail, 1)
            for j in range(4):
                n = tail_no("proj", j)
                dve.wait_ge(pe_tail, n + 1)
                hs = h[:, j * 512:(j + 1) * 512]
                dve.tensor_tensor(hs, bank[n % BANKS][:, :], hs, ALU.add).then_inc(dve_tail, 1)
            dve.wait_ge(dve_tail, tail_count(tail_no("proj", 3))[1])
            norm_rows(4)
            n = tail_no("gate", 0)
            score, rank, hot1, hot2, comb = (w_spec[:, 17408 + 256 * k:17408 + 256 * (k + 1)] for k in (0, 1, 2, 3, 3))
            comb = small[:, 0:256]
            m1, dm, ex, den, pr = (small[:, 256 + 32 * k:288 + 32 * k] for k in range(5))
            pr2 = small[:, 416:448]

            def each(ap):
                return ap.rearrange("p (t e) -> p t e", e=E)

            def per(ap):
                return ap.unsqueeze(2).to_broadcast([P, TILES, E])

            dve.wait_ge(pe_tail, n + 1)
            dve.tensor_copy(score, bank[n % BANKS][:, 0:256]).then_inc(dve_tail, 1)
            dve.wait_ge(dve_tail, tail_count(n)[1])
            for e in range(E):
                ins = dve.memset(each(rank)[:, :, e], float(E - e))
            link(ins)

            def pick(hot, top, tmp):
                link(dve.tensor_reduce(top, each(score), AX.X, ALU.max))
                link(dve.tensor_tensor(each(hot), each(score), per(top), ALU.is_equal))
                link(dve.tensor_tensor(hot, hot, rank, ALU.mult))
                link(dve.tensor_reduce(tmp, each(hot), AX.X, ALU.max))
                link(dve.tensor_tensor(each(hot), each(rank), per(tmp), ALU.is_equal))

            pick(hot1, m1, den)
            link(dve.scalar_tensor_tensor(out=score, in0=hot1, scalar=-3.0e38, in1=score, op0=ALU.mult, op1=ALU.add))
            pick(hot2, pr, den)
            link(dve.tensor_tensor(dm, pr, m1, ALU.subtract))
            dve.sem_inc(s_root, 1)
            dve.wait_ge(a_step, 5)
            link(dve.tensor_scalar(den, ex, 1.0, None, ALU.add))
            link(dve.reciprocal(pr, den))
            link(dve.tensor_tensor(pr2, pr, ex, ALU.mult))
            link(dve.tensor_tensor(each(hot1), each(hot1), per(pr), ALU.mult))
            link(dve.tensor_tensor(each(hot2), each(hot2), per(pr2), ALU.mult))
            link(dve.tensor_tensor(comb, hot1, hot2, ALU.add))
            dve.sem_inc(s_step, 1)
            for j in range(4):
                n = tail_no("b2", j)
                dve.wait_ge(pe_tail, n + 1)
                hs = h[:, j * 512:(j + 1) * 512]
                dve.tensor_tensor(hs, bank[n % BANKS][:, :], hs, ALU.add).then_inc(dve_tail, 1)
            dve.wait_ge(dve_tail, tail_count(len(TAIL) - 1)[1])
            dve.sem_inc(y_mm_free, 2)
            base = chained[0]
            with dve.Fori(0, 8) as tg:
                for e in range(E):
                    dve.wait_ge(y_mm, tg * 8 + (e + 3))
                    yw = y_w[:, (e % 2) * 256:(e % 2) * 256 + 256]
                    cw = comb.rearrange("p (t e) -> p t e", e=E)[:, bass.ds(tg * 4, 4), e]
                    dve.tensor_tensor(yw.rearrange("p (t y) -> p t y", y=D),
                                      bank[6 + e % 2][:, 0:256].rearrange("p (t y) -> p t y", y=D),
                                      cw.unsqueeze(2).to_broadcast([P, 4, D]), ALU.mult).then_inc(y_mm_free, 1)
                    dve.wait_ge(y_mm_free, tg * 8 + (e + 3))
                    hs = h[:, bass.ds(tg * 256, 256)]
                    dve.tensor_tensor(hs, yw, hs, ALU.add).then_inc(dve_chain, 1)
                    dve.wait_ge(dve_chain, tg * 8 + (base + e + 1))
                dve.sem_inc(y_done, 1)

        @block.gpsimd
        def _(pool):
            with pool.Fori(0, LAYERS) as l:
                stop_for(pool, "pool", sc_ready, l + 1)
                with pool.Fori(0, CHUNKS // 2) as i:
                    for par in range(2):
                        for q in range(4):
                            at = v[par][:, q * QUART:(q + 1) * QUART]
                            stop_for(pool, "pool", v_in[par][q], (l * 4 + i) * 16 + 16)
                            pool.tensor_scalar(at, at, sc[:, 0:1], sc[:, 1:2], ALU.mult, ALU.add).then_inc(v_half, 1)
                            stop_for(pool, "pool", v_half, (l * 4 + i) * 8 + (par * 4 + q + 1))
                            pool.tensor_scalar(at, at, 3.0e38, sc[:, 2:3], ALU.min, ALU.max).then_inc(v_act, 1)



def _constants():
    f32 = np.float32
    y = np.arange(S)
    ky = np.arange(M)
    kx = np.concatenate([np.arange(M), np.arange(S - M, S)])
    x_of = np.arange(S)
    fy = np.zeros((B2, S, B2, 2, M))
    th = 2 * np.pi * np.outer(y, ky) / S
    for b in range(B2):
        fy[b, :, b, 0], fy[b, :, b, 1] = np.cos(th), -np.sin(th)
    th = 2 * np.pi * np.outer(x_of, kx) / S
    g = np.zeros((2, 2, S, 2, 2, KX))
    for b in range(2):
        g[0, b, :, 0, b], g[0, b, :, 1, b] = np.cos(th), -np.sin(th)
        g[1, b, :, 0, b], g[1, b, :, 1, b] = np.sin(th), np.cos(th)
    xs = (np.arange(XQ)[None, :] * XR + np.arange(XR)[:, None]).reshape(-1)
    th = 2 * np.pi * np.outer(kx, xs) / S
    gi = np.zeros((2, B2, KX, B2, S))
    for b in range(B2):
        gi[0, b, :, b], gi[1, b, :, b] = np.cos(th), -np.sin(th)
    wt = np.where(ky == 0, 1.0, 2.0)[:, None] / (S * S)
    th = 2 * np.pi * np.outer(ky, y) / S
    fyi = np.zeros((BQ, 32, BQ, S))
    for b in range(BQ):
        fyi[b, 0:M, b], fyi[b, M:2 * M, b] = wt * np.cos(th), -wt * np.sin(th)
    avg = np.kron(np.ones((XQ, XQ)), np.eye(C)) / XQ
    return {
        "c_fy": fy.reshape(P, -1).astype(f32),
        "c_g": g.transpose(1, 2, 0, 3, 4, 5).reshape(P, -1).astype(f32),
        "c_gi": gi.reshape(96, P).astype(f32),
        "c_fyi": fyi.reshape(P, -1).astype(f32),
        "c_id": np.eye(P, dtype=f32),
        "c_avg": avg.astype(f32),
        "c_ones": np.ones((P, P), f32),
    }


def _layout(i):
    f32 = np.float32
    a = {k: np.asarray(v) for k, v in i.items()}
    x = a["x"].reshape(CHUNKS, 2, B2, 2, XQ, XR, S)
    fields = np.zeros((CHUNKS, XQ, 4, XR, 2, 2, B2, S), f32)
    fields[:, :, 0] = x.transpose(0, 4, 5, 1, 3, 2, 6)
    pos = np.linspace(0.0, 1.0, S, dtype=f32)
    fields[:, :, 1] = pos.reshape(1, XQ, XR, 1, 1, 1, 1)
    fields[:, :, 2] = pos
    fields[:, :, 3] = 1.0
    p4 = np.concatenate([a["L0_tok_p_w"], a["L0_tok_p_b"][None]], 0)
    pw = np.zeros((XQ, 4, XQ, C), f32)
    wbd = np.zeros((LAYERS, XQ, C, XQ, C), f32)
    qbd = np.zeros((XQ, C, XQ), f32)
    for q in range(XQ):
        pw[q, :, q] = p4
        wbd[:, q, :, q] = a["L0_tok_w_w"]
        qbd[q, :, q] = a["L0_tok_q_w"][:, 0]
    w = np.concatenate([a["L0_tok_fw1"], a["L0_tok_fw2"]], 3).reshape(LAYERS, C, C, KX, KYG, 4, 2)
    spec = w.transpose(0, 5, 1, 4, 3, 6, 2).reshape(LAYERS, P, -1)

    def channels(t):
        return np.tile(t.T, (XQ, 1))

    def under(wm, bias):
        return np.concatenate([wm, bias[None]], 0)

    w1 = a["L0_ffn_W1"].reshape(E * H, D).T
    w2 = a["L0_ffn_W2"].reshape(E, D, 2, P).transpose(3, 0, 2, 1).reshape(P, -1)
    return {
        "x_f": fields.reshape(CHUNKS, 16, COLS),
        "p_w": pw.reshape(16, P),
        "w_bd": wbd.reshape(LAYERS, P, P),
        "w_b": channels(a["L0_tok_w_b"]),
        "spec_w": spec,
        "bn_g": channels(a["L0_tok_bn_g"]),
        "bn_b": channels(a["L0_tok_bn_b"]),
        "q_bd": qbd.reshape(P, XQ),
        "q_b": np.tile(a["L0_tok_q_b"].reshape(1, 1), (P, 1)),
        "wqkv": under(a["L0_attn_W_qkv"], a["L0_attn_b_qkv"]),
        "wout": under(a["L0_attn_W_out"], a["L0_attn_b_out"]),
        "wgate": under(a["L0_ffn_Wg"].T, a["L0_ffn_bg"]),
        "w1t": under(w1, a["L0_ffn_b1"].reshape(-1)),
        "w2t": w2,
        "b2": a["L0_ffn_b2"],
    }


def kernel(**inputs):
    import concourse.bacc as _bacc
    from concourse.bass_utils import run_bass_kernel_spmd as _run

    data = {**_layout(inputs), **_constants()}
    nc = _bacc.Bacc("TRN2", target_bir_lowering=False, num_devices=1)
    arrays, args = {}, {}
    for name, t in data.items():
        arrays[f"in_{name}"] = np.ascontiguousarray(t)
        args[name] = nc.dram_tensor(f"in_{name}", t.shape, mybir.dt.from_np(t.dtype), kind="ExternalInput").ap()
    args["out"] = nc.dram_tensor("out_0", (B, S, S), F32, kind="ExternalOutput").ap()
    build(nc, **args)
    r = _run(nc, [arrays], core_ids=[0])
    return r.results[0]["out_0"]
```

```python
from contextlib import ExitStack

import numpy as np
import concourse.bass as bass
from concourse import mybir

F32 = mybir.dt.float32
ALU = mybir.AluOpType
ACT = mybir.ActivationFunctionType
AX = mybir.AxisListType

P = 128
BANKS = 8
B, S, C = 64, 64, 32
LAYERS, M = 4, 12
KX = 2 * M
XQ, XR = 4, 16
BQ, B2 = 4, 2
CH = BQ * B2
CHUNKS = B // CH
COLS = CH * XR * S
QUART = COLS // 4
PAIRS = CHUNKS // 2
XB = 3 * B
STAGE = 3 * BQ * 144
PIECE = 12
KYG = M // 4
E, H, D = 8, 256, 64
TILES = B * S // P
BN_STEPS = 13
BN_EPS = 1e-5
LN_EPS = 1e-5



def forward_jobs(c, first=False, last=False):
    if first:
        return [("turn", 0, 0, j) for j in range(8)]
    jobs = []
    for hf in range(2):
        for j in range(4):
            jobs.append(("dfty", c, hf, j))
            if not (last and hf == 1):
                jobs += [("turn", c + hf, 1 - hf, 2 * j), ("turn", c + hf, 1 - hf, 2 * j + 1)]
        jobs += [("dftx", c, hf, j) for j in range(2)]
    return jobs


def inverse_jobs(c, first=False, last=False):
    back = [("back", c + 1, bq, ri) for bq in range(BQ) for ri in range(2)]
    idft = [("idftx", c + 1, j) for j in range(8)]
    if first:
        return [("back", 0, *j[2:]) for j in back] + [("idftx", 0, *j[2:]) for j in idft]
    out = [("out", c, j) for j in range(16)]
    if last:
        return out
    jobs = []
    for j in range(8):
        jobs += [out[j], back[j]]
    jobs += [out[8], idft[0], out[9], idft[1], out[10], idft[2], idft[3], out[11], idft[4], idft[5], out[12],
             idft[6], idft[7], out[13], out[14], out[15]]
    return jobs


def field_jobs():
    jobs = []
    for c in range(CHUNKS + 2):
        if c < CHUNKS:
            jobs.append(("fdfty", c))
        if 1 <= c <= CHUNKS:
            jobs.append(("fdftx", c - 1))
        if c >= 2:
            jobs += [("lift", c - 2, hf, j) for hf in range(2) for j in range(2)]
    return jobs


FIELD = field_jobs()
FWD_FIRST = forward_jobs(0, first=True)
FWD_PAIR = forward_jobs(0) + forward_jobs(1)
FWD_LAST = forward_jobs(0) + forward_jobs(1, last=True)
MIX = [("mix", j) for j in range(KYG * KX // 3)]
INV_FIRST = inverse_jobs(0, first=True)
INV_PAIR = inverse_jobs(0) + inverse_jobs(1)
INV_LAST = inverse_jobs(0) + inverse_jobs(1, last=True)
for seg in (FIELD, FWD_FIRST, FWD_PAIR, FWD_LAST, MIX, INV_FIRST, INV_PAIR, INV_LAST):
    assert len(seg) % BANKS == 0
N_FWD = len(FWD_FIRST) + (PAIRS - 1) * len(FWD_PAIR) + len(FWD_LAST)
N_INV = len(INV_FIRST) + (PAIRS - 1) * len(INV_PAIR) + len(INV_LAST)
N_LAYER = N_FWD + len(MIX) + N_INV
N_ZERO = len(FIELD) + len(MIX) + N_INV
N_ALL = N_ZERO + (LAYERS - 1) * N_LAYER


def place(seg, *job):
    return seg.index(job)


def done_after(half_base, j):
    return half_base + (j // 2 + 5), half_base + ((j + 1) // 2 + 4)


TAIL = []
for kind, n in (("xnT", 8), ("qkv", 16), ("knorm", 2), ("kv", 8), ("qT", 8), ("attnT", 8),
                ("proj", 4), ("x2T", 8), ("gate", 1), ("combT", 8)):
    TAIL += [(kind, j) for j in range(n)]
TAIL_ACT = ("xnT", "qkv", "qT", "attnT", "x2T", "combT")


def tail_no(kind, j):
    return TAIL.index((kind, j))


def tail_count(n):
    a = sum(k in TAIL_ACT for k, _ in TAIL[:n + 1])
    return a, n + 1 - a


def build(nc, x_f, x_t, c_pos, p_t, p_e, w_bd, w_b, spec_w, bn_g, bn_b, q_bd, q_b, wqkv, wout, wgate, w1t, w2t, b2,
          c_fy, c_g, c_gi, c_fyi, c_id, c_avg, c_ones, out):
    ctx = ExitStack()
    with ctx:
        def sb(name, cols, parts=P):
            return ctx.enter_context(nc.sbuf_tensor(name, [parts, cols], F32))

        def sem(name):
            return ctx.enter_context(nc.semaphore(name))

        bank = [ctx.enter_context(nc.psum_tensor(f"bank{i}", [P, 512], F32)) for i in range(BANKS)]
        u_dram = nc.dram_tensor("u_scratch", [CHUNKS, P, COLS], F32, kind="Internal").ap()
        h_dram = nc.dram_tensor("h_scratch", [B, S, S], F32, kind="Internal").ap()
        comb_dram = nc.dram_tensor("comb_scratch", [E, B * S], F32, kind="Internal").ap()

        area_x = sb("area_x", KYG * KX * XB)
        area_o = sb("area_o", KYG * KX * XB)
        area_v = sb("area_v", COLS)
        area_p = sb("area_p", 4096)
        area_t = sb("area_t", 4096)
        area_s = sb("area_s", 2 * STAGE)
        fy = sb("fy", 2 * 2 * M)
        gx = sb("gx", 2 * 96)
        gi = sb("gi", P)
        fyi = sb("fyi", BQ * S)
        wconv = sb("wconv", P)
        ident = sb("ident", P)
        avg = sb("avg", P)
        ones = sb("ones", P)
        pw = sb("pw", 4 * P + KYG * P)
        wfield = sb("wfield", 4 * P)
        chan = sb("chan", 3 * LAYERS + 1)
        qbd = sb("qbd", 33)
        a32 = sb("a32", 32)
        stats = sb("stats", CHUNKS * 16 * 6)
        bnw = sb("bnw", 16)
        wb_now = sb("wb_now", 1)
        sc = sb("sc", 2)

        xs = area_x
        os_ = area_o
        stage = [area_s[:, 0:STAGE], area_s[:, STAGE:2 * STAGE]]
        fy_out = area_s[:, 0:2 * 2 * M * C]
        turned = area_t
        v_fwd = [area_v[:, :], area_o[:, 0:COLS]]
        pix_fwd = [area_p[:, :], area_o[:, COLS:COLS + 4096]]
        v_inv = [area_v[:, :], area_x[:, 0:COLS]]
        pix_inv = [area_p[:, :], area_x[:, COLS:COLS + 4096]]
        W = PIECE * 2 * P
        w_slot = [area_v[:, 0:W], area_v[:, W:2 * W], area_p[:, 0:W], area_s[:, 0:W]]
        W_PLAN = [0, 1, 2, 0, 3, 2]
        fpix = area_o[:, 0:2048]
        fpos = area_o[:, 2048:2432]
        f_y = [area_o[:, COLS + 384 * k:COLS + 384 * (k + 1)] for k in range(2)]
        f_x = [area_o[:, COLS + 768 + 384 * k:COLS + 768 + 384 * (k + 1)] for k in range(2)]

        v_last = [area_v[:, :], area_o[:, 0:COLS]]
        hq = [area_t[:, 0:2048], area_p[:, 0:2048]]
        h = area_t[:, 2048:4096]
        qkv = area_x[:, 0:6144]
        wk = area_x[:, 6144:12288]
        xnT = area_v[0:65, 0:4096]
        qT = area_v[0:64, 4096:8192]
        atT = area_o[0:65, 0:4096]
        cT = area_v[:, 4096:8192]
        kvs = area_o[0:64, 4096:8192]
        w1s = area_o[0:65, 8192:10240]
        w2s = area_o[:, 10240:11264]
        hb = [area_p[:, 0:1024], area_p[:, 1024:2048]]
        xn = area_p[:, 2048:4096]
        wq_s = area_s[0:65, 0:192]
        wo_s = area_s[0:65, 192:256]
        wg_s = area_s[0:65, 256:264]
        b2_s = area_s[:, 264:328]
        yT = [area_s[0:64, 512:1024], area_s[0:64, 1024:1536]]
        small = area_s[:, 1536:2304]
        xe = [area_s[0:65, 2304:2816], area_s[0:65, 2816:3328]]
        cb = [area_x[0:65, 0:4096], area_x[0:65, 4096:8192]]

        const_in = sem("const_in")
        fpix_in = sem("fpix_in")
        v_in = [[sem(f"v_in{p}{q}") for q in range(4)] for p in range(2)]
        v_out = [[sem(f"v_out{p}{q}") for q in range(4)] for p in range(2)]
        wc_in = sem("wc_in")
        w_in = [sem(f"w_in{k}") for k in range(4)]
        t_zero = sem("t_zero")
        wf_mm = sem("wf_mm")
        wf_cp = sem("wf_cp")
        v_act = sem("v_act")
        pe_job = sem("pe_job")
        act_job = sem("act_job")
        dve_job = sem("dve_job")
        stage_cp = sem("stage_cp")
        stat_done = sem("stat_done")
        bn_agg = sem("bn_agg")
        bn_mm = sem("bn_mm")
        bn_dev = sem("bn_dev")
        bn_var = sem("bn_var")
        bn_sqrt = sem("bn_sqrt")
        sc_ready = sem("sc_ready")
        dve_chain = sem("dve_chain")
        a_ready = sem("a_ready")
        tail_in = sem("tail_in")
        fin_in = [sem("fin_in0"), sem("fin_in1")]
        read_mm = sem("read_mm")
        read_act = sem("read_act")
        read_dve = sem("read_dve")
        hq_out = [sem("hq_out0"), sem("hq_out1")]
        h_in = sem("h_in")
        pe_tail = sem("pe_tail")
        act_tail = sem("act_tail")
        dve_tail = sem("dve_tail")
        s_step = sem("s_step")
        s_root = sem("s_root")
        a_step = sem("a_step")
        comb_out = sem("comb_out")
        cb_in = [sem("cb_in0"), sem("cb_in1")]
        x_e = sem("x_e")
        hid_mm = sem("hid_mm")
        hid_relu = sem("hid_relu")
        y_mm = sem("y_mm")
        y_cp = sem("y_cp")
        y_turn = sem("y_turn")
        y_done = sem("y_done")
        out_done = sem("out_done")
        passed = {e: sem(f"passed_{e}") for e in ("pe", "dve", "pool", "sp")}

        def stop_for(eng, name, signal, value):
            eng.wait_ge(signal, value)
            eng.sem_inc(passed[name], 1)

        CONSTS = [(fy[:, :], c_fy), (gx[:, :], c_g), (fyi[:, :], c_fyi), (ident[:, :], c_id), (avg[:, :], c_avg),
                  (ones[:, :], c_ones), (gi[0:96, :], c_gi), (pw[:, 0:4 * P], p_t), (pw[0:48, 4 * P:], p_e),
                  (chan[:, 0:LAYERS], w_b), (chan[:, LAYERS:2 * LAYERS], bn_g), (chan[:, 2 * LAYERS:3 * LAYERS], bn_b),
                  (qbd[:, 0:32], q_bd), (qbd[:, 32:33], q_b)]
        CONST_READY = 16 * len(CONSTS)

        def at_fwd(m):
            return m * (N_LAYER // 2) + N_ZERO // 2

        def at_mix(m):
            return len(FIELD) // 2 if m is None else at_fwd(m) + N_FWD // 2

        def at_inv(m):
            return at_mix(m) + len(MIX) // 2

        FWD_IN = len(FWD_FIRST) // 2
        INV_IN = len(INV_FIRST) // 2
        INV_END = N_INV // 2

        def layer(m):
            return 0 if m is None else m + 1

        block = ctx.enter_context(nc.Block())

        def read_out_store(sp, c):
            sp.wait_ge(read_act, 2 * c + 2)
            sp.wait_ge(read_dve, 2 * c + 2)
            for j in range(4):
                dst = h_dram[8 * c:8 * c + 8].rearrange("b (q g j) y -> j q g b y", q=XQ, j=4)[j]
                src = hq[c % 2][32 * j:32 * j + 4, :].rearrange("q (g b y) -> q g b y", g=4, y=S)
                sp.dma_start(dst, src).then_inc(hq_out[c % 2], 16)

        def final_store(sp, tg):
            sp.wait_ge(y_done, tg + 3)
            sp.dma_start(out[8 * tg:8 * tg + 8].rearrange("(t b) x y -> (b x) t y", b=2),
                         h[:, tg * 256:(tg + 1) * 256].rearrange("p (t y) -> p t y", y=D)).then_inc(out_done, 16)

        @block.sync
        def _(sp):
            for dst, src in CONSTS:
                sp.dma_start(dst, src).then_inc(const_in, 16)
            sp.dma_start(wconv[:, :], w_bd[0]).then_inc(wc_in, 16)
            sp.dma_start(fpix, x_t).then_inc(fpix_in, 16)
            sp.dma_start(fpos, c_pos).then_inc(fpix_in, 16)

            def emptied(half_base, j):
                a, d = done_after(half_base, j)
                stop_for(sp, "sp", act_job, a)
                stop_for(sp, "sp", dve_job, d)

            def pe_done(half_base, j):
                stop_for(sp, "sp", pe_job, half_base * 2 + (j + 1))

            def weights(m, piece):
                k = W_PLAN[piece]
                src = spec_w[:, piece * W:(piece + 1) * W] if m is None else \
                    spec_w[:, bass.ds(m * (KYG * KX * 2 * P) + (KYG * KX * 2 * P + piece * W), W)]
                sp.dma_start(w_slot[k], src).then_inc(w_in[k], 16)

            def load(dst, c, p, q):
                src = u_dram[c] if isinstance(c, int) else u_dram[bass.ds(c, 1)].rearrange("a p n -> (a p) n")
                sp.dma_start(dst[:, q * QUART:(q + 1) * QUART], src[:, q * QUART:(q + 1) * QUART])\
                  .then_inc(v_in[p][q], 16)

            def load_field(dst, c, p, q):
                src = x_f[c] if isinstance(c, int) else x_f[bass.ds(c, 1)].rearrange("a p n -> (a p) n")
                sp.dma_start(dst[:, 3 * QUART + q * 512:3 * QUART + (q + 1) * 512], src[:, q * 512:(q + 1) * 512])\
                  .then_inc(v_in[p][q], 16)

            def mixing(m):
                base = at_mix(m)
                pe_done(base, -1)
                weights(m, 4)
                pe_done(base, 3)
                weights(m, 3)
                pe_done(base, 11)
                weights(m, 5)

            def inverse(m):
                fetch = load_field if m is None else load
                base = at_mix(m)
                pe_done(base, 15)
                for q in range(4):
                    fetch(v_inv[0], 0, 0, q)
                pe_done(base, len(MIX) - 1)
                for q in range(4):
                    fetch(v_inv[1], 1, 1, q)

                def store(seg, half_base, i, c):
                    chunk = i * 2 + c
                    for q in range(4):
                        emptied(half_base, place(seg, "out", c, 4 * q + 3))
                        dst = u_dram[chunk] if isinstance(chunk, int) else \
                            u_dram[bass.ds(chunk, 1)].rearrange("a p n -> (a p) n")
                        sp.dma_start(dst[:, q * QUART:(q + 1) * QUART], v_inv[c][:, q * QUART:(q + 1) * QUART])\
                          .then_inc(v_out[c][q], 16)

                with sp.Fori(0, PAIRS - 1) as i:
                    for c in range(2):
                        store(INV_PAIR, at_inv(m) + INV_IN + i * (len(INV_PAIR) // 2), i, c)
                        stop_for(sp, "sp", stat_done, (i * 2 + layer(m) * CHUNKS) * 16 + (c * 16 + 16))
                        for q in range(4):
                            for stored in (range(4) if m is None and q == 0 else () if m is None else (q,)):
                                stop_for(sp, "sp", v_out[c][stored], (i + layer(m) * PAIRS) * 16 + 16)
                            fetch(v_inv[c], i * 2 + (2 + c), c, q)
                for c in range(2):
                    store(INV_LAST, at_inv(m) + INV_IN + (PAIRS - 1) * (len(INV_PAIR) // 2), PAIRS - 1, c)

            for piece in (0, 1, 2):
                weights(None, piece)
            mixing(None)
            inverse(None)

            with sp.Fori(0, LAYERS - 1) as m:
                for q in range(4):
                    stop_for(sp, "sp", v_out[0][q], m * (16 * PAIRS) + 16 * PAIRS)
                stop_for(sp, "sp", stat_done, m * (16 * CHUNKS) + 16 * (CHUNKS - 1))
                for q in range(4):
                    load(v_fwd[0], 0, 0, q)
                for q in range(4):
                    stop_for(sp, "sp", v_out[1][q], m * (16 * PAIRS) + 16 * PAIRS)
                stop_for(sp, "sp", stage_cp, m * CHUNKS + CHUNKS)
                for q in range(4):
                    load(v_fwd[1], 1, 1, q)
                stop_for(sp, "sp", sc_ready, m + 1)
                sp.dma_start(wconv[:, :], w_bd[bass.ds(m + 1, 1)].rearrange("a p n -> (a p) n")).then_inc(wc_in, 16)
                with sp.Fori(0, PAIRS - 1) as i:
                    for c in range(2):
                        pe_done(at_fwd(m) + FWD_IN + i * (len(FWD_PAIR) // 2), place(FWD_PAIR, "turn", c, 1, 7))
                        for q in range(4):
                            load(v_fwd[c], i * 2 + (2 + c), c, q)
                last = at_fwd(m) + FWD_IN + (PAIRS - 1) * (len(FWD_PAIR) // 2)
                pe_done(last, place(FWD_LAST, "turn", 0, 1, 7))
                weights(m, 0)
                weights(m, 1)
                pe_done(last, place(FWD_LAST, "dfty", 1, 0, 3))
                weights(m, 2)
                mixing(m)
                inverse(m)

            for dst, src in ((w1s, w1t), (w2s, w2t), (wq_s, wqkv), (wo_s, wout), (wg_s, wgate), (b2_s, b2)):
                if dst is w1s:
                    sp.wait_ge(stage_cp, CHUNKS * LAYERS)
                if dst is wq_s:
                    sp.wait_ge(pe_job, N_ALL)
                sp.dma_start(dst, src).then_inc(tail_in, 16)
            for c in range(CHUNKS):
                for p in range(2):
                    for q in range(4):
                        if c == p:
                            sp.wait_ge(v_out[p][q], 16 * PAIRS * LAYERS)
                if c >= 2:
                    sp.wait_ge(read_mm, 4 * c - 4)
                else:
                    sp.wait_ge(stat_done, 16 * CHUNKS * LAYERS)
                sp.dma_start(v_last[c % 2], u_dram[c]).then_inc(fin_in[c % 2], 16)
                if c >= 1:
                    read_out_store(sp, c - 1)
            read_out_store(sp, CHUNKS - 1)
            for c in range(CHUNKS):
                sp.wait_ge(hq_out[c % 2], 64 * (c // 2 + 1))
                if c == 0:
                    sp.wait_ge(read_mm, 4 * CHUNKS)
                sp.dma_start(h[:, c * 256:(c + 1) * 256].rearrange("p (t y) -> p t y", y=D),
                             h_dram[8 * c:8 * c + 8].rearrange("(t b) x y -> (b x) t y", b=2)).then_inc(h_in, 16)
            sp.wait_ge(act_tail, tail_count(len(TAIL) - 1)[0])
            sp.dma_start(comb_dram, cT[0:E, :]).then_inc(comb_out, 16)
            sp.wait_ge(comb_out, 16)
            for tg in range(8):
                if tg >= 2:
                    sp.wait_ge(x_e, 8 * (tg - 1))
                for e in range(E):
                    sp.dma_start(cb[tg % 2][:, e * 512:(e + 1) * 512],
                                 comb_dram[e:e + 1, tg * 512:(tg + 1) * 512].to_broadcast([65, 512]))\
                      .then_inc(cb_in[tg % 2], 16)
                if tg >= 1:
                    final_store(sp, tg - 1)
            final_store(sp, 7)
            sp.wait_ge(out_done, 16 * 8)

        @block.tensor
        def _(pe):
            pe.wait_ge(const_in, CONST_READY)
            pe.wait_ge(wc_in, 16)
            for q in range(4):
                mm = pe.matmul(bank[0][:, q * P:(q + 1) * P], pw[:, q * P:(q + 1) * P], wconv[:, :],
                               start=True, stop=True)
            mm.then_inc(wf_mm, 1)
            pe.wait_ge(wf_cp, 1)

            def emptied(half_base, j):
                a, d = done_after(half_base, j)
                pe.wait_ge(act_job, a)
                pe.wait_ge(dve_job, d)

            def run(seg, half_base, m, i=0):
                for j, job in enumerate(seg):
                    pe.wait_ge((act_job, dve_job)[j % 2], half_base + (j // 2 + 1))
                    product(seg, half_base, m, i, j, job)

            def product(seg, half_base, m, i, j, job):
                kind = job[0]
                ps = bank[j % BANKS]
                if kind == "fdfty":
                    c = job[1]
                    if c == 0:
                        pe.wait_ge(fpix_in, 32)
                        for f in range(3):
                            pe.matmul(ps[:, 96 + f * 48:96 + (f + 1) * 48], fpos[:, f * P:(f + 1) * P], fy[:, :],
                                      start=True, stop=True)
                    for hf in range(2):
                        mm = pe.matmul(ps[:, hf * 48:(hf + 1) * 48], fpix[:, (2 * c + hf) * P:(2 * c + hf + 1) * P],
                                       fy[:, :], start=True, stop=True)
                elif kind == "fdftx":
                    c = job[1]
                    emptied(half_base, place(seg, "fdfty", c))
                    for hb2 in range(4):
                        for ri in range(2):
                            at = hb2 * 96 + ri * 48
                            mm = pe.matmul(ps[0:48, hb2 * 96:(hb2 + 1) * 96], f_y[c % 2][:, at:at + 48],
                                           gx[:, ri * 96:(ri + 1) * 96], start=(ri == 0), stop=(ri == 1))
                elif kind == "lift":
                    _, c, hf, b2_ = job
                    if hf == 0 and b2_ == 0:
                        emptied(half_base, place(seg, "fdftx", c))
                    at = (2 * hf + b2_) * 96
                    for kyg in range(KYG):
                        mm = pe.matmul(ps[:, kyg * 96:(kyg + 1) * 96], pw[0:48, (4 + kyg) * P:(5 + kyg) * P],
                                       f_x[c % 2][0:48, at:at + 96], start=True, stop=True)
                elif kind == "turn":
                    _, c, hf, n = job
                    bq, quad = 2 * hf + n // 4, n % 4
                    if n == 0 and hf == 0:
                        pe.wait_ge(v_act, (i * 2 + m * (4 * CHUNKS // 2)) * 4 + (c * 4 + 4))
                    for k in range(4):
                        at = ((4 * quad + k) * BQ + bq) * P
                        mm = pe.transpose(ps[:, k * P:(k + 1) * P], v_fwd[c % 2][:, at:at + P], ident[:, :])
                elif kind == "dfty":
                    _, c, hf, n = job
                    if n == 0:
                        emptied(half_base, -1 if (c, hf) == (0, 0) else place(seg, "turn", c, hf, 7))
                    src = pix_fwd[hf].rearrange("p (x c) -> p x c", c=C)
                    for k in range(8):
                        mm = pe.matmul(ps[:, k * 48:(k + 1) * 48], src[:, :, 8 * n + k], fy[:, :], start=True, stop=True)
                elif kind == "dftx":
                    _, c, hf, b2_ = job
                    if b2_ == 0:
                        emptied(half_base, place(seg, "dfty", c, hf, 3))
                    for kyg in range(KYG):
                        for ri in range(2):
                            at = b2_ * 768 + ri * 384 + kyg * P
                            mm = pe.matmul(ps[:, kyg * 96:(kyg + 1) * 96], fy_out[:, at:at + P],
                                           gx[:, ri * 96:(ri + 1) * 96], start=(ri == 0), stop=(ri == 1))
                elif kind == "mix":
                    n = job[1]
                    if n == 0:
                        emptied(half_base, -1)
                    if n % 4 == 0:
                        k = W_PLAN[n // 4]
                        uses = W_PLAN.count(k)
                        nth = W_PLAN[:n // 4].count(k) + 1
                        pe.wait_ge(w_in[k], 16 * nth if m is None else m * (16 * uses) + 16 * (uses + nth))
                    for k in range(3):
                        g = 3 * n + k
                        for ri in range(2):
                            at = (g % PIECE * 2 + ri) * P
                            x_at = g * XB + (1 - ri) * B
                            mm = pe.matmul(ps[:, k * P:(k + 1) * P], w_slot[W_PLAN[n // 4]][:, at:at + P],
                                           xs[:, x_at:x_at + P], start=(ri == 0), stop=(ri == 1))
                elif kind == "back":
                    _, c, bq, ri = job
                    if bq == 0 and ri == 0:
                        pe.wait_ge(stage_cp, i * 2 + c + 1 if m is None else m * CHUNKS + i * 2 + (CHUNKS + c + 1))
                    for kyg in range(KYG):
                        at = kyg * 576 + bq * 144 + ri * 48
                        mm = pe.transpose(ps[0:96, kyg * P:(kyg + 1) * P], stage[c % 2][:, at:at + 96], ident[:, :])
                elif kind == "idftx":
                    _, c, n = job
                    if n == 0:
                        emptied(half_base, place(seg, "back", c, BQ - 1, 1))
                    src = turned[0:96, :].rearrange("p (k o) -> p k o", o=C)
                    for k in range(4):
                        mm = pe.matmul(ps[:, k * P:(k + 1) * P], src[:, :, 4 * n + k], gi[0:96, :],
                                       start=True, stop=True)
                else:
                    _, c, n = job
                    if n == 0:
                        emptied(half_base, -1 if c == 0 else place(seg, "idftx", c, 7))
                    if m is None and n < 4:
                        pe.wait_ge(v_in[c][n], i * 16 + 16)
                    if m is not None and n % 4 == 0:
                        pe.wait_ge(v_act, (i * 2 + m * (4 * CHUNKS // 2)) * 4 + (4 * CHUNKS + c * 4 + n // 4 + 1))
                    for k in range(2):
                        at = (XR * k + n) * P
                        pe.matmul(ps[:, :].rearrange("p (q b y) -> p q b y", q=BQ, b=B2)[:, :, k],
                                  pix_inv[c][:, at:at + P], fyi[:, :], start=(k == 0), stop=False)
                    at, w = n * 512, wconv[:, :]
                    if m is None:
                        at, w = 3 * QUART + n % 4 * 512, wfield[:, n // 4 * P:(n // 4 + 1) * P]
                    mm = pe.matmul(ps[:, :], w, v_inv[c][:, at:at + 512], start=False, stop=True)
                mm.then_inc(pe_job, 1)

            def inverse(m):
                run(MIX, at_mix(m), m)
                run(INV_FIRST, at_inv(m), m)
                with pe.Fori(0, PAIRS - 1) as i:
                    run(INV_PAIR, at_inv(m) + INV_IN + i * (len(INV_PAIR) // 2), m, i)
                run(INV_LAST, at_inv(m) + INV_IN + (PAIRS - 1) * (len(INV_PAIR) // 2), m, PAIRS - 1)
                emptied(at_inv(m) + INV_END, -1)
                pe.wait_ge(bn_agg, layer(m) + 1)
                pe.matmul(bank[7][:, 0:1], avg[:, :], bnw[:, 0:1], start=True, stop=True).then_inc(bn_mm, 1)
                pe.wait_ge(bn_dev, layer(m) + 1)
                pe.matmul(bank[7][:, 8:9], avg[:, :], bnw[:, 2:3], start=True, stop=True).then_inc(bn_mm, 1)
                stop_for(pe, "pe", sc_ready, layer(m) + 1)

            run(FIELD, 0, None)
            pe.wait_ge(t_zero, 1)
            inverse(None)
            with pe.Fori(0, LAYERS - 1) as m:
                run(FWD_FIRST, at_fwd(m), m)
                with pe.Fori(0, PAIRS - 1) as i:
                    run(FWD_PAIR, at_fwd(m) + FWD_IN + i * (len(FWD_PAIR) // 2), m, i)
                run(FWD_LAST, at_fwd(m) + FWD_IN + (PAIRS - 1) * (len(FWD_PAIR) // 2), m, PAIRS - 1)
                pe.wait_ge(wc_in, m * 16 + 32)
                inverse(m)

            pe.wait_ge(a_ready, 1)
            pe.matmul(bank[7][:, 0:1], wfield[:, 0:P], qbd[:, 0:1], start=True, stop=True).then_inc(bn_mm, 1)
            pe.wait_ge(a_ready, 2)
            for c in range(CHUNKS):
                pe.wait_ge(fin_in[c % 2], 16 * (c // 2 + 1))
                for g in range(4):
                    n = 4 * c + g
                    if n >= BANKS:
                        pe.wait_ge((read_act, read_dve)[n % 2], (n - BANKS) // 2 + 1)
                    for j in range(4):
                        mm = pe.matmul(bank[n % BANKS][32 * j:32 * j + 32, :], a32[:, :],
                                       v_last[c % 2][:, (4 * g + j) * 512:(4 * g + j + 1) * 512], start=True, stop=True)
                    mm.then_inc(read_mm, 1)
            pe.wait_ge(read_act, 2 * CHUNKS)
            pe.wait_ge(read_dve, 2 * CHUNKS)

            def start_tail(kind, j):
                n = tail_no(kind, j)
                if n >= BANKS:
                    tail_wait(n - BANKS)
                return bank[n % BANKS]

            def tail_wait(n):
                a, d = tail_count(n)
                if a:
                    pe.wait_ge(act_tail, a)
                if d:
                    pe.wait_ge(dve_tail, d)

            pe.wait_ge(tail_in, 16 * 6)

            def flip(kind, src, width, step):
                for j in range(8):
                    ps = start_tail(kind, j)
                    if j == 0:
                        pe.wait_ge(s_step, step)
                    for k in range(4):
                        mm = pe.transpose(ps[0:width, k * P:(k + 1) * P], src(4 * j + k), ident[:, :])
                    mm.then_inc(pe_tail, 1)

            flip("xnT", lambda t: xn[:, t * D:(t + 1) * D], D, 1)
            for j in range(16):
                ps = start_tail("qkv", j)
                if j == 0:
                    tail_wait(tail_no("xnT", 7))
                for k in range(2):
                    t = 2 * j + k
                    mm = pe.matmul(ps[:, k * 192:(k + 1) * 192], xnT[:, t * P:(t + 1) * P], wq_s, start=True, stop=True)
                mm.then_inc(pe_tail, 1)
            for b in range(2):
                ps = start_tail("knorm", b)
                pe.wait_ge(s_step, 2)
                for t in range(TILES):
                    mm = pe.matmul(ps[0:D, t:t + 1], wk[64 * b:64 * b + 64, 4096 + t * D:4096 + (t + 1) * D],
                                   ones[64 * b:64 * b + 64, 0:1], start=True, stop=True)
                mm.then_inc(pe_tail, 1)
            k_v = wk[:, 0:4096].rearrange("p (t a c) -> p t a c", a=2, c=D)
            for j in range(8):
                ps = start_tail("kv", j)
                for k in range(8):
                    t, b = 8 * (j % 4) + k, j // 4
                    mm = pe.matmul(ps[0:D, k * D:(k + 1) * D], k_v[64 * b:64 * b + 64, t, 1, :],
                                   qkv[64 * b:64 * b + 64, t * 192 + 128:t * 192 + 192], start=True, stop=True)
                mm.then_inc(pe_tail, 1)
            flip("qT", lambda t: xn[:, t * D:(t + 1) * D], D, 3)
            for j in range(8):
                ps = start_tail("attnT", j)
                if j == 0:
                    tail_wait(tail_no("qT", 7))
                for k in range(8):
                    b = 8 * j + k
                    at = (32 * (b % 2) + b // 2) * D
                    pe.matmul(ps[0:D, k * D:(k + 1) * D], kvs[:, at:at + D], qT[:, b * D:(b + 1) * D],
                              start=(k == 0), stop=False)
                mm = pe.matmul(ps[0:D, :], wq_s[:, 128:192], xnT[:, j * 512:(j + 1) * 512], start=False, stop=True)
                mm.then_inc(pe_tail, 1)
            for j in range(4):
                ps = start_tail("proj", j)
                if j == 0:
                    tail_wait(tail_no("attnT", 7))
                for k in range(8):
                    t = 8 * j + k
                    mm = pe.matmul(ps[:, k * D:(k + 1) * D], atT[:, t * P:(t + 1) * P], wo_s, start=True, stop=True)
                mm.then_inc(pe_tail, 1)
            flip("x2T", lambda t: xn[:, t * D:(t + 1) * D], D, 4)
            ps = start_tail("gate", 0)
            tail_wait(tail_no("x2T", 7))
            for t in range(TILES):
                mm = pe.matmul(ps[:, t * E:(t + 1) * E], xnT[:, t * P:(t + 1) * P], wg_s, start=True, stop=True)
            mm.then_inc(pe_tail, 1)
            flip("combT", lambda t: small[:, t * E:(t + 1) * E], E, 5)
            tail_wait(len(TAIL) - 1)
            pe.sem_inc(hid_mm, 4)
            pe.sem_inc(y_mm, 2)
            pe.sem_inc(y_turn, 2)
            with pe.Fori(0, 4) as i:
                def turn_back(k):
                    stop_for(pe, "pe", y_cp, i * 2 + (k + 3))
                    stop_for(pe, "pe", y_done, i * 2 + (k + 1))
                    for t in range(4):
                        mm = pe.transpose(bank[6 + k][:, t * D:(t + 1) * D], yT[k][:, t * P:(t + 1) * P],
                                          ident[0:64, 0:64])
                    mm.then_inc(y_turn, 1)

                for k in range(2):
                    def hidden(e):
                        pe.wait_ge(x_e, i * 16 + (8 * k + e + 1))
                        for half in range(2):
                            n = 2 * e + half
                            pe.wait_ge(hid_relu, i * 32 + (16 * k + n + 1))
                            pe.matmul(bank[n % 4][:, :], w1s[:, e * H + half * P:e * H + (half + 1) * P],
                                      xe[e % 2], start=True, stop=True).then_inc(hid_mm, 1)

                    hidden(0)
                    hidden(1)
                    pe.wait_ge(y_cp, i * 2 + (k + 1))
                    pe.matmul(bank[4 + k][0:D, :], b2_s, cT[:, bass.ds(i * 1024 + k * 512, 512)],
                              start=True, stop=False)
                    for e in range(E):
                        pe.wait_ge(hid_relu, i * 32 + (16 * k + 2 * e + 6))
                        for half in range(2):
                            mm = pe.matmul(bank[4 + k][0:D, :], w2s[:, (2 * e + half) * D:(2 * e + half + 1) * D],
                                           hb[e % 2][:, half * 512:(half + 1) * 512],
                                           start=False, stop=(e == E - 1 and half == 1))
                        mm.then_inc(y_mm, 1)
                        if e + 2 < E:
                            hidden(e + 2)
                        if e == 3 and k == 1:
                            turn_back(0)
                turn_back(1)

        def unload(copy, neg, add_bias, j, job):
            kind = job[0]
            ps = bank[j % BANKS]
            if kind == "fdfty":
                if job[1] == 0:
                    for k in range(2):
                        for hf in range(2):
                            copy(f_y[k].rearrange("p (h m f) -> p h m f", h=2, f=4)[:, hf, :, 1:4],
                                 ps[:, 96:240].rearrange("p (f m) -> p m f", f=3))
                return copy(f_y[job[1] % 2].rearrange("p (m f) -> p m f", f=4)[:, :, 0], ps[:, 0:96])
            if kind == "fdftx":
                return copy(f_x[job[1] % 2][0:48, :], ps[0:48, 0:384])
            if kind == "turn":
                _, c, hf, n = job
                bqi, quad = n // 4, n % 4
                dst = pix_fwd[hf][:, bqi * 2048:(bqi + 1) * 2048].rearrange("p (q x c) -> p x q c", q=XQ, x=XR)
                return copy(dst[:, 4 * quad:4 * quad + 4], ps[:, :].rearrange("p (x q c) -> p x q c", x=4, q=XQ))
            if kind == "dfty":
                n = job[3]
                dst = fy_out.rearrange("p (m c) -> p c m", c=C)
                return copy(dst[:, 8 * n:8 * n + 8, :], ps[:, 0:384].rearrange("p (c m) -> p c m", c=8))
            if kind == "back":
                _, c, bq, ri = job
                at = bq * 1024 + ri * 384
                return copy(turned[0:96, at:at + 384], ps[0:96, 0:384])
            if kind == "idftx":
                _, c, n = job
                dst = pix_inv[c % 2].rearrange("p (m o) -> p o m", o=C)
                return copy(dst[:, 4 * n:4 * n + 4, :], ps[:, :].rearrange("p (o m) -> p o m", o=4))
            if kind == "mix":
                n = job[1]
                kyg, kx = 3 * n // KX, 3 * n % KX
                dst = os_[:, :].rearrange("p (g q m k) -> p g k m q", g=KYG, m=3 * B2, k=KX)[:, kyg, kx:kx + 3]
                src = ps[:, 0:384].rearrange("p (k m q) -> p k m q", k=3, m=2 * B2)
                copy(dst[:, :, 0:4], src)
                return neg(dst[:, :, 4:6], src[:, :, 0:2])
            assert kind == "out"
            _, c, n = job
            return add_bias(v_inv[c][:, n * 512:(n + 1) * 512], ps[:, :])

        def unload_dftx(copy, neg, j, job, chunk):
            hf, b2_ = job[2:]
            src = bank[j % BANKS][:, 0:288].rearrange("p (k r q) -> p k r q", r=2, q=2)
            dst = xs[:, :].rearrange("p (k r b) -> p k r b", r=3, b=B)
            at = chunk * BQ + (b2_ * 32 + 2 * hf)
            cols = slice(at, at + 2) if isinstance(at, int) else bass.ds(at, 2)
            copy(dst[:, :, 1:3, cols], src)
            return neg(dst[:, :, 0, cols], src[:, :, 1])

        @block.scalar
        def _(act):
            def copy(dst, src):
                return act.activation(dst, src, ACT.Copy)

            def neg(dst, src):
                return act.activation(dst, src, ACT.Copy, scale=-1.0)

            def add_bias(dst, src):
                return act.activation(dst, src, ACT.Identity, bias=wb_now[:, 0:1])

            def run(seg, half_base, i, extra):
                for j in range(0, len(seg), 2):
                    act.wait_ge(pe_job, half_base * 2 + (j + 1))
                    job = seg[j]
                    if job[0] in ("dftx", "lift"):
                        chunk = job[1] if job[0] == "lift" else i * 2 + job[1]
                        unload_dftx(copy, neg, j, job, chunk).then_inc(act_job, 1)
                    else:
                        unload(copy, neg, add_bias, j, job).then_inc(act_job, 1)
                    if extra and j in extra:
                        extra[j]()

            def relu(m, i, c, q, buf, inv):
                p = c % 2
                i_in = i + c // 2
                act.wait_ge(v_in[p][q], (i_in + m * (2 * PAIRS)) * 16 + 16 * (PAIRS + PAIRS * inv + 1))
                at = buf[p][:, q * QUART:(q + 1) * QUART]
                act.activation(at, at, ACT.Relu, bias=sc[:, 1:2], scale=sc[:, 0:1]).then_inc(v_act, 1)

            def spread(positions, m, i, c, buf, inv):
                return {j: (lambda q=q: relu(m, i, c, q, buf, inv)) for q, j in enumerate(positions)}

            def inverse(m):
                run(MIX, at_mix(m), 0, None)
                if m is not None:
                    for q in range(4):
                        relu(m, 0, 0, q, v_inv, 1)
                run(INV_FIRST, at_inv(m), 0, None)

                def extra(i, c):
                    if m is None:
                        return {}
                    base = 32 * c
                    return spread([base + k for k in (6, 12, 18, 24)], m, i, c + 1, v_inv, 1)

                with act.Fori(0, PAIRS - 1) as i:
                    run(INV_PAIR, at_inv(m) + INV_IN + i * (len(INV_PAIR) // 2), i, {**extra(i, 0), **extra(i, 1)})
                run(INV_LAST, at_inv(m) + INV_IN + (PAIRS - 1) * (len(INV_PAIR) // 2), PAIRS - 1, extra(PAIRS - 1, 0))
                act.wait_ge(bn_var, layer(m) + 1)
                act.activation(bnw[:, 4:5], bnw[:, 3:4], ACT.Sqrt).then_inc(bn_sqrt, 1)

            act.wait_ge(const_in, CONST_READY)
            act.sem_inc(act_job, 4)
            act.wait_ge(wf_mm, 1)
            act.activation(wfield[:, :], bank[0][:, :], ACT.Copy).then_inc(wf_cp, 1)
            run(FIELD, 0, 0, None)
            inverse(None)
            with act.Fori(0, LAYERS - 1) as m:
                act.wait_ge(sc_ready, m + 1)
                for q in range(4):
                    relu(m, 0, 0, q, v_fwd, 0)
                run(FWD_FIRST, at_fwd(m), 0, None)
                for q in range(4):
                    act.wait_ge(v_out[1][q], m * (16 * PAIRS) + 16 * PAIRS)
                with act.Fori(0, PAIRS - 1) as i:
                    run(FWD_PAIR, at_fwd(m) + FWD_IN + i * (len(FWD_PAIR) // 2), i,
                        {**spread((0, 4, 8, 12), m, i, 1, v_fwd, 0), **spread((28, 32, 36, 40), m, i, 2, v_fwd, 0)})
                run(FWD_LAST, at_fwd(m) + FWD_IN + (PAIRS - 1) * (len(FWD_PAIR) // 2), PAIRS - 1,
                    spread((0, 4, 8, 12), m, PAIRS - 1, 1, v_fwd, 0))
                inverse(m)

            for c in range(CHUNKS):
                for g in (0, 2):
                    n = 4 * c + g
                    if g == 0 and c >= 2:
                        act.wait_ge(hq_out[c % 2], 64 * (c // 2))
                    act.wait_ge(read_mm, n + 1)
                    act.activation(hq[c % 2][:, g * 512:(g + 1) * 512], bank[n % BANKS][:, :], ACT.Identity,
                                   bias=bnw[:, 12:13]).then_inc(read_act, 1)

            def empty(kind, dst, rows, cols):
                for j in range(sum(k == kind for k, _ in TAIL)):
                    n = tail_no(kind, j)
                    act.wait_ge(pe_tail, n + 1)
                    act.activation(dst(j), bank[n % BANKS][0:rows, 0:cols], ACT.Copy).then_inc(act_tail, 1)

            def root(step, dst, src):
                act.wait_ge(s_root, step)
                act.activation(dst, src, ACT.Sqrt).then_inc(a_step, 1)

            root(1, small[:, 320:352], small[:, 288:320])
            empty("xnT", lambda j: xnT[0:D, j * 512:(j + 1) * 512], D, 512)
            empty("qkv", lambda j: qkv[:, j * 384:(j + 1) * 384], P, 384)
            root(2, small[:, 320:352], small[:, 288:320])
            root(3, small[0:D, 448:512], small[0:D, 384:448])
            empty("qT", lambda j: qT[0:D, j * 512:(j + 1) * 512], D, 512)
            empty("attnT", lambda j: atT[0:D, j * 512:(j + 1) * 512], D, 512)
            root(4, small[:, 320:352], small[:, 288:320])
            empty("x2T", lambda j: xnT[0:D, j * 512:(j + 1) * 512], D, 512)
            act.wait_ge(s_root, 5)
            act.activation(small[:, 320:352], small[:, 288:320], ACT.Exp).then_inc(a_step, 1)
            empty("combT", lambda j: cT[0:E, j * 512:(j + 1) * 512], E, 512)
            act.sem_inc(hid_relu, 4)
            act.sem_inc(y_cp, 2)
            with act.Fori(0, 4) as i:
                for k in range(2):
                    for e in range(E):
                        act.wait_ge(y_mm, i * 16 + (8 * k + e + 1))
                        for half in range(2):
                            n = 2 * e + half
                            act.wait_ge(hid_mm, i * 32 + (16 * k + n + 5))
                            act.activation(hb[e % 2][:, half * 512:(half + 1) * 512], bank[n % 4][:, :], ACT.Relu)\
                               .then_inc(hid_relu, 1)
                    act.wait_ge(y_mm, i * 16 + (8 * k + 10))
                    act.wait_ge(y_turn, i * 2 + (k + 1))
                    act.activation(yT[k], bank[4 + k][0:D, :], ACT.Copy).then_inc(y_cp, 1)

        @block.vector
        def _(dve):
            chained = [0]

            def link(ins):
                chained[0] += 1
                ins.then_inc(dve_chain, 1)
                dve.wait_ge(dve_chain, chained[0])

            def copy(dst, src):
                return dve.tensor_copy(dst, src)

            def neg(dst, src):
                return dve.tensor_scalar(dst, src, -1.0, None, ALU.mult)

            def add_bias(dst, src):
                return dve.tensor_scalar(dst, src, wb_now[:, 0:1], None, ALU.add)

            def stat(seg, half_base, m, i, c, n):
                a, d = done_after(half_base, place(seg, "out", c, n))
                if place(seg, "out", c, n) % 2 == 0:
                    stop_for(dve, "dve", act_job, a)
                else:
                    stop_for(dve, "dve", dve_job, d)
                at = i * 192 + (c * 96 + n * 6)
                cols = slice(at, at + 6) if isinstance(at, int) else bass.ds(at, 6)
                dve.bn_stats(stats[:, cols], v_inv[c][:, n * 512:(n + 1) * 512]).then_inc(stat_done, 1)

            def run(seg, half_base, m=None, i=0):
                for j, job in enumerate(seg):
                    if j % 2:
                        dve.wait_ge(pe_job, half_base * 2 + (j + 1))
                        if job[0] in ("dftx", "lift"):
                            chunk = job[1] if job[0] == "lift" else i * 2 + job[1]
                            unload_dftx(copy, neg, j, job, chunk).then_inc(dve_job, 1)
                        else:
                            unload(copy, neg, add_bias, j, job).then_inc(dve_job, 1)
                    if job[0] == "out":
                        _, c, n = job
                        for back in range(n - 2, (n if n == 15 else n - 2) + 1):
                            if back >= 0:
                                stat(seg, half_base, m, i, c, back)

            def batch_norm(m, wait_at):
                steps = [0]

                def step(ins):
                    steps[0] += 1
                    ins.then_inc(dve_chain, 1)
                    dve.wait_ge(dve_chain, wait_at(steps[0]))

                n = layer(m)

                def column(k):
                    return chan[:, k:k + 1] if m is None else chan[:, bass.ds(m + (k + 1), 1)]

                stop_for(dve, "dve", stat_done, n * (16 * CHUNKS) + 16 * CHUNKS)
                step(dve.bn_aggr(bnw[:, 0:2], stats[:, :]))
                dve.sem_inc(bn_agg, 1)
                dve.wait_ge(bn_mm, n * 2 + 1)
                step(dve.tensor_copy(bnw[:, 5:6], bank[7][:, 0:1]))
                step(dve.tensor_tensor(bnw[:, 6:7], bnw[:, 0:1], bnw[:, 5:6], ALU.subtract))
                step(dve.scalar_tensor_tensor(out=bnw[:, 2:3], in0=bnw[:, 6:7], scalar=bnw[:, 6:7],
                                              in1=bnw[:, 1:2], op0=ALU.mult, op1=ALU.add))
                dve.sem_inc(bn_dev, 1)
                dve.wait_ge(bn_mm, n * 2 + 2)
                step(dve.tensor_scalar(bnw[:, 3:4], bank[7][:, 8:9], BN_EPS, None, ALU.add))
                dve.sem_inc(bn_var, 1)
                dve.wait_ge(bn_sqrt, n + 1)
                step(dve.reciprocal(bnw[:, 6:7], bnw[:, 4:5]))
                step(dve.scalar_tensor_tensor(out=bnw[:, 7:8], in0=bnw[:, 6:7], scalar=bnw[:, 3:4],
                                              in1=bnw[:, 4:5], op0=ALU.mult, op1=ALU.add))
                step(dve.tensor_scalar(bnw[:, 6:7], bnw[:, 7:8], 0.5, None, ALU.mult))
                step(dve.reciprocal(bnw[:, 7:8], bnw[:, 6:7]))
                step(dve.tensor_tensor(sc[:, 0:1], bnw[:, 7:8], column(LAYERS), ALU.mult))
                step(dve.tensor_tensor(bnw[:, 6:7], sc[:, 0:1], bnw[:, 5:6], ALU.mult))
                step(dve.tensor_tensor(sc[:, 1:2], column(2 * LAYERS), bnw[:, 6:7], ALU.subtract))
                step(dve.tensor_copy(wb_now[:, 0:1], column(1)))
                dve.sem_inc(sc_ready, 1)
                assert steps[0] == BN_STEPS

            def inverse(m):
                run(MIX, at_mix(m))
                run(INV_FIRST, at_inv(m))
                with dve.Fori(0, PAIRS - 1) as i:
                    run(INV_PAIR, at_inv(m) + INV_IN + i * (len(INV_PAIR) // 2), m, i)
                run(INV_LAST, at_inv(m) + INV_IN + (PAIRS - 1) * (len(INV_PAIR) // 2), m, PAIRS - 1)

            dve.sem_inc(dve_job, 4)
            dve.memset(turned[:, :], 0.0).then_inc(t_zero, 1)
            dve.wait_ge(const_in, CONST_READY)
            link(dve.tensor_copy(wb_now[:, 0:1], chan[:, 0:1]))
            run(FIELD, 0)
            inverse(None)
            before = chained[0]
            batch_norm(None, lambda k: before + k)
            with dve.Fori(0, LAYERS - 1) as m:
                run(FWD_FIRST, at_fwd(m))
                for q in range(4):
                    stop_for(dve, "dve", v_out[1][q], m * (16 * PAIRS) + 16 * PAIRS)
                with dve.Fori(0, PAIRS - 1) as i:
                    run(FWD_PAIR, at_fwd(m) + FWD_IN + i * (len(FWD_PAIR) // 2), m, i)
                run(FWD_LAST, at_fwd(m) + FWD_IN + (PAIRS - 1) * (len(FWD_PAIR) // 2), m, PAIRS - 1)
                inverse(m)
                batch_norm(m, lambda k: m * BN_STEPS + (before + BN_STEPS + k))
            chained[0] = before + LAYERS * BN_STEPS

            link(dve.tensor_scalar(a32[:, :], qbd[:, 0:32], sc[:, 0:1], None, ALU.mult))
            link(dve.tensor_scalar(wfield[:, 0:P], ones[:, :], sc[:, 1:2], None, ALU.mult))
            dve.sem_inc(a_ready, 1)
            dve.wait_ge(bn_mm, 2 * LAYERS + 1)
            link(dve.tensor_tensor(bnw[:, 12:13], bank[7][:, 0:1], qbd[:, 32:33], ALU.add))
            dve.sem_inc(a_ready, 1)
            for c in range(CHUNKS):
                for g in (1, 3):
                    n = 4 * c + g
                    if g == 1 and c >= 2:
                        dve.wait_ge(hq_out[c % 2], 64 * (c // 2))
                    dve.wait_ge(read_mm, n + 1)
                    dve.tensor_scalar(hq[c % 2][:, g * 512:(g + 1) * 512], bank[n % BANKS][:, :], bnw[:, 12:13],
                                      None, ALU.add).then_inc(read_dve, 1)
            dve.wait_ge(h_in, 16 * CHUNKS)

            def root_of(dst, a, r, tmp, a_val, floor=None):
                dve.sem_inc(s_root, 1)
                dve.wait_ge(a_step, a_val)
                if floor is not None:
                    link(dve.tensor_scalar(r, r, floor, None, ALU.max))
                link(dve.reciprocal(tmp, r))
                link(dve.tensor_tensor(tmp, tmp, a, ALU.mult))
                link(dve.tensor_tensor(tmp, tmp, r, ALU.add))
                link(dve.tensor_scalar(tmp, tmp, 0.5, floor, ALU.mult, ALU.max) if floor is not None
                     else dve.tensor_scalar(tmp, tmp, 0.5, None, ALU.mult))
                link(dve.reciprocal(dst, tmp))

            def wide(ap):
                return ap.rearrange("p (t y) -> p t y", y=D)

            def spread(ap):
                return ap.unsqueeze(2).to_broadcast([P, TILES, D])

            sq = wk[:, 4096:6144]

            def norm_rows(step_no):
                mean, var, r, tmp, inv = (small[:, 256 + 32 * k:288 + 32 * k] for k in range(5))
                link(dve.tensor_reduce(mean, wide(h), AX.X, ALU.add))
                link(dve.tensor_scalar(mean, mean, 1.0 / D, None, ALU.mult))
                link(dve.tensor_tensor(wide(xn), wide(h), spread(mean), ALU.subtract))
                link(dve.tensor_tensor(sq, xn, xn, ALU.mult))
                link(dve.tensor_reduce(var, wide(sq), AX.X, ALU.add))
                link(dve.tensor_scalar(var, var, 1.0 / D, LN_EPS, ALU.mult, ALU.add))
                root_of(inv, var, r, tmp, step_no)
                link(dve.tensor_tensor(wide(xn), wide(xn), spread(inv), ALU.mult))
                dve.sem_inc(s_step, 1)

            dve.memset(xnT[D:D + 1, :], 1.0)
            link(dve.memset(atT[D:D + 1, :], 1.0))
            norm_rows(1)
            dve.wait_ge(act_tail, tail_count(tail_no("qkv", 15))[0])
            qk = qkv.rearrange("p (t a c) -> p t a c", a=3, c=D)[:, :, 0:2]
            qk2 = wk[:, 0:4096].rearrange("p (t a c) -> p t a c", a=2, c=D)
            sums = small[:, 512:576]
            sums2 = sums.rearrange("p (t a) -> p t a", a=2)
            bsum = sums2.unsqueeze(3).to_broadcast([P, TILES, 2, D])
            link(dve.tensor_reduce(sums2, qk, AX.X, ALU.add))
            link(dve.tensor_scalar(sums, sums, 1.0 / D, None, ALU.mult))
            link(dve.tensor_tensor(qk2, qk, bsum, ALU.subtract))
            link(dve.tensor_tensor(wk[:, 0:4096], wk[:, 0:4096], wk[:, 0:4096], ALU.mult))
            link(dve.tensor_reduce(sums2, qk2, AX.X, ALU.add))
            link(dve.tensor_scalar(sums, sums, 1e-7, None, ALU.add))
            link(dve.reciprocal(sums, sums))
            link(dve.tensor_tensor(qk2, qk2, bsum, ALU.mult))
            link(dve.tensor_tensor(wide(sq), qk2[:, :, 1], qk2[:, :, 1], ALU.mult))
            dve.sem_inc(s_step, 1)
            link(dve.tensor_tensor(wide(xn), qk2[:, :, 0], qk2[:, :, 0], ALU.mult))
            link(dve.tensor_reduce(small[:, 288:320], wide(xn), AX.X, ALU.add))
            root_of(small[:, 384:416], small[:, 288:320], small[:, 320:352], small[:, 352:384], 2, floor=1e-12)
            link(dve.tensor_tensor(wide(xn), qk2[:, :, 0], spread(small[:, 384:416]), ALU.mult))
            dve.sem_inc(s_step, 1)
            for b in range(2):
                n = tail_no("knorm", b)
                dve.wait_ge(pe_tail, n + 1)
                dve.tensor_copy(small[0:D, 384 + 32 * b:416 + 32 * b], bank[n % BANKS][0:D, 0:32]).then_inc(dve_tail, 1)
            dve.wait_ge(dve_tail, tail_count(n)[1])
            root_of(small[0:D, 640:704], small[0:D, 384:448], small[0:D, 448:512], small[0:D, 576:640], 3, floor=1e-12)
            link(dve.tensor_scalar(small[0:D, 640:704], small[0:D, 640:704], float(S) ** -0.5, None, ALU.mult))
            for j in range(8):
                n = tail_no("kv", j)
                dve.wait_ge(pe_tail, n + 1)
                dve.tensor_tensor(wide(kvs[:, j * 512:(j + 1) * 512]), wide(bank[n % BANKS][0:D, :]),
                                  small[0:D, 640 + 8 * j:648 + 8 * j].unsqueeze(2).to_broadcast([D, 8, D]),
                                  ALU.mult).then_inc(dve_tail, 1)
            for j in range(4):
                n = tail_no("proj", j)
                dve.wait_ge(pe_tail, n + 1)
                hs = h[:, j * 512:(j + 1) * 512]
                dve.tensor_tensor(hs, bank[n % BANKS][:, :], hs, ALU.add).then_inc(dve_tail, 1)
            dve.wait_ge(dve_tail, tail_count(tail_no("proj", 3))[1])
            link(dve.memset(cT, 0.0))
            norm_rows(4)
            n = tail_no("gate", 0)
            score, rank, hot1, hot2 = (wk[:, 256 * k:256 * (k + 1)] for k in range(4))
            comb = small[:, 0:256]
            m1, dm, ex, den, pr = (small[:, 256 + 32 * k:288 + 32 * k] for k in range(5))
            pr2 = small[:, 416:448]

            def each(ap):
                return ap.rearrange("p (t e) -> p t e", e=E)

            def per(ap):
                return ap.unsqueeze(2).to_broadcast([P, TILES, E])

            dve.wait_ge(pe_tail, n + 1)
            dve.tensor_copy(score, bank[n % BANKS][:, 0:256]).then_inc(dve_tail, 1)
            dve.wait_ge(dve_tail, tail_count(n)[1])
            for e in range(E):
                ins = dve.memset(each(rank)[:, :, e], float(E - e))
            link(ins)

            def pick(hot, top, tmp):
                link(dve.tensor_reduce(top, each(score), AX.X, ALU.max))
                link(dve.tensor_tensor(each(hot), each(score), per(top), ALU.is_equal))
                link(dve.tensor_tensor(hot, hot, rank, ALU.mult))
                link(dve.tensor_reduce(tmp, each(hot), AX.X, ALU.max))
                link(dve.tensor_tensor(each(hot), each(rank), per(tmp), ALU.is_equal))

            pick(hot1, m1, den)
            link(dve.scalar_tensor_tensor(out=score, in0=hot1, scalar=-3.0e38, in1=score, op0=ALU.mult, op1=ALU.add))
            pick(hot2, pr, den)
            link(dve.tensor_tensor(dm, pr, m1, ALU.subtract))
            dve.sem_inc(s_root, 1)
            dve.wait_ge(a_step, 5)
            link(dve.tensor_scalar(den, ex, 1.0, None, ALU.add))
            link(dve.reciprocal(pr, den))
            link(dve.tensor_tensor(pr2, pr, ex, ALU.mult))
            link(dve.tensor_tensor(each(hot1), each(hot1), per(pr), ALU.mult))
            link(dve.tensor_tensor(each(hot2), each(hot2), per(pr2), ALU.mult))
            link(dve.tensor_tensor(comb, hot1, hot2, ALU.add))
            dve.sem_inc(s_step, 1)
            dve.sem_inc(y_done, 2)

            def finish(i, k):
                dve.wait_ge(y_turn, i * 2 + (k + 3))
                hs = h[:, bass.ds(i * 512 + 256 * k, 256)]
                dve.tensor_tensor(hs, bank[6 + k][:, 0:256], hs, ALU.add).then_inc(y_done, 1)

            with dve.Fori(0, 4) as i:
                for k in range(2):
                    for e in range(E):
                        if e == 0:
                            dve.wait_ge(cb_in[k], i * 128 + 128)
                        dve.wait_ge(hid_mm, i * 32 + (16 * k + 2 * e + 2))
                        dve.tensor_tensor(xe[e % 2], xnT[:, bass.ds(i * 1024 + k * 512, 512)],
                                          cb[k][:, e * 512:(e + 1) * 512], ALU.mult).then_inc(x_e, 1)
                        if e == 5 and k == 1:
                            finish(i, 0)
                finish(i, 1)

        @block.gpsimd
        def _(pool):
            src = os_[:, :].rearrange("p (g n) -> p g n", g=KYG)

            def copy(chunk, c):
                at = chunk * 576
                cols = slice(at, at + 576) if isinstance(at, int) else bass.ds(at, 576)
                pool.tensor_copy(stage[c].rearrange("p (g n) -> p g n", g=KYG), src[:, :, cols]).then_inc(stage_cp, 1)

            def inverse(m):
                a, d = done_after(at_inv(m), -1)
                stop_for(pool, "pool", act_job, a)
                stop_for(pool, "pool", dve_job, d)
                copy(0, 0)
                copy(1, 1)
                with pool.Fori(0, PAIRS - 1) as i:
                    base = at_inv(m) + INV_IN + i * (len(INV_PAIR) // 2)
                    stop_for(pool, "pool", pe_job, base * 2 + 1)
                    copy(i * 2 + 2, 0)
                    stop_for(pool, "pool", pe_job, base * 2 + (place(INV_PAIR, "back", 1, BQ - 1, 1) + 1))
                    copy(i * 2 + 3, 1)

            inverse(None)
            with pool.Fori(0, LAYERS - 1) as m:
                inverse(m)


def _constants():
    f32 = np.float32
    y = np.arange(S)
    ky = np.arange(M)
    kx = np.concatenate([np.arange(M), np.arange(S - M, S)])
    x_of = np.arange(S)
    fy = np.zeros((B2, S, B2, 2, M))
    th = 2 * np.pi * np.outer(y, ky) / S
    for b in range(B2):
        fy[b, :, b, 0], fy[b, :, b, 1] = np.cos(th), -np.sin(th)
    th = 2 * np.pi * np.outer(x_of, kx) / S
    g = np.zeros((2, 2, S, 2, 2, KX))
    for b in range(2):
        g[0, b, :, 0, b], g[0, b, :, 1, b] = np.cos(th), -np.sin(th)
        g[1, b, :, 0, b], g[1, b, :, 1, b] = np.sin(th), np.cos(th)
    xs = (np.arange(XQ)[None, :] * XR + np.arange(XR)[:, None]).reshape(-1)
    th = 2 * np.pi * np.outer(kx, xs) / S
    gi = np.zeros((2, B2, KX, B2, S))
    for b in range(B2):
        gi[0, b, :, b], gi[1, b, :, b] = np.cos(th), -np.sin(th)
    wt = np.where(ky == 0, 1.0, 2.0)[:, None] / (S * S)
    th = 2 * np.pi * np.outer(ky, y) / S
    fyi = np.zeros((BQ, 32, BQ, S))
    for b in range(BQ):
        fyi[b, 0:M, b], fyi[b, M:2 * M, b] = wt * np.cos(th), -wt * np.sin(th)
    avg = np.kron(np.ones((XQ, XQ)), np.eye(C)) / XQ
    pos = np.zeros((B2, S, 3, 2, S))
    at = np.linspace(0.0, 1.0, S, dtype=f32)
    pos[:, :, 0], pos[:, :, 1], pos[:, :, 2] = at, at[:, None, None], 1.0
    return {
        "c_pos": pos.reshape(P, -1).astype(f32),
        "c_fy": fy.reshape(P, -1).astype(f32),
        "c_g": g.transpose(1, 2, 0, 5, 3, 4).reshape(P, -1).astype(f32),
        "c_gi": gi.reshape(96, P).astype(f32),
        "c_fyi": fyi.reshape(P, -1).astype(f32),
        "c_id": np.eye(P, dtype=f32),
        "c_avg": avg.astype(f32),
        "c_ones": np.ones((P, P), f32),
    }


def _layout(i):
    f32 = np.float32
    a = {k: np.asarray(v) for k, v in i.items()}
    x = a["x"].reshape(CHUNKS, BQ, B2, XQ, XR, S)
    pos = np.linspace(0.0, 1.0, S, dtype=f32)
    fields = np.zeros((CHUNKS, BQ, B2, XQ, XR, S, 4), f32)
    fields[..., 0] = x
    fields[..., 1] = pos.reshape(XQ, XR, 1)
    fields[..., 2] = pos
    fields[..., 3] = 1.0
    x_f = np.zeros((CHUNKS, 4, 32, XR // 4 * CH * S), f32)
    x_f[:, :, 0:16] = fields.transpose(0, 4, 3, 6, 1, 2, 5).reshape(CHUNKS, 4, 4, XQ, 4, -1)\
        .transpose(0, 1, 3, 4, 2, 5).reshape(CHUNKS, 4, 16, -1)
    p4 = np.concatenate([a["L0_tok_p_w"], a["L0_tok_p_b"][None]], 0)
    p_t = np.zeros((XQ, C, 4, 4, 32), f32)
    wbd = np.zeros((LAYERS, XQ, C, XQ, C), f32)
    qbd = np.zeros((XQ, C, 32), f32)
    for q in range(XQ):
        for k in range(4):
            p_t[q, :, k, k, 4 * q:4 * q + 4] = p4.T
        wbd[:, q, :, q] = a["L0_tok_w_w"]
        qbd[q, :, q] = a["L0_tok_q_w"][:, 0]
    p_e = np.zeros((KYG, 4, 4, KYG, 4, C), f32)
    w = np.concatenate([a["L0_tok_fw1"], a["L0_tok_fw2"]], 3).reshape(LAYERS, C, C, KX, KYG, 4, 2)
    spec = np.zeros((4, C, LAYERS, KYG, KX, 2, 4, C), f32)
    for k in range(4):
        spec[k, ..., k, :] = w[:, :, :, :, :, k].transpose(1, 0, 4, 3, 5, 2)
        for g in range(KYG):
            p_e[g, k, :, g, k] = p4

    def channels(t):
        return np.tile(t.T, (XQ, 1))

    def under(wm, bias):
        return np.concatenate([wm, bias[None]], 0)

    w1 = a["L0_ffn_W1"].reshape(E * H, D).T
    w2 = a["L0_ffn_W2"].reshape(E, D, 2, P).transpose(3, 0, 2, 1).reshape(P, -1)
    return {
        "x_f": x_f.reshape(CHUNKS, P, -1),
        "x_t": x.transpose(2, 5, 0, 1, 3, 4).reshape(P, -1),
        "p_t": p_t.reshape(P, -1),
        "p_e": p_e.reshape(48, -1),
        "w_bd": wbd.reshape(LAYERS, P, P),
        "w_b": channels(a["L0_tok_w_b"]),
        "spec_w": spec.reshape(P, -1),
        "bn_g": channels(a["L0_tok_bn_g"]),
        "bn_b": channels(a["L0_tok_bn_b"]),
        "q_bd": qbd.reshape(P, 32),
        "q_b": np.tile(a["L0_tok_q_b"].reshape(1, 1), (P, 1)),
        "wqkv": under(a["L0_attn_W_qkv"], a["L0_attn_b_qkv"]),
        "wout": under(a["L0_attn_W_out"], a["L0_attn_b_out"]),
        "wgate": under(a["L0_ffn_Wg"].T, a["L0_ffn_bg"]),
        "w1t": under(w1, a["L0_ffn_b1"].reshape(-1)),
        "w2t": w2,
        "b2": np.concatenate([a["L0_ffn_b2"], np.zeros((P - E, D), f32)], 0),
    }


def kernel(**inputs):
    import concourse.bacc as _bacc
    from concourse.bass_utils import run_bass_kernel_spmd as _run

    data = {**_layout(inputs), **_constants()}
    nc = _bacc.Bacc("TRN2", target_bir_lowering=False, num_devices=1)
    arrays, args = {}, {}
    for name, t in data.items():
        arrays[f"in_{name}"] = np.ascontiguousarray(t)
        args[name] = nc.dram_tensor(f"in_{name}", t.shape, mybir.dt.from_np(t.dtype), kind="ExternalInput").ap()
    args["out"] = nc.dram_tensor("out_0", (B, S, S), F32, kind="ExternalOutput").ap()
    build(nc, **args)
    r = _run(nc, [arrays], core_ids=[0])
    return r.results[0]["out_0"]
```

```python
from contextlib import ExitStack

import numpy as np
import concourse.bass as bass
from concourse import mybir

F32 = mybir.dt.float32
F32R = mybir.dt.float32r
I32 = mybir.dt.int32
HIGH = -4096
ALU = mybir.AluOpType
ACT = mybir.ActivationFunctionType
AX = mybir.AxisListType

P = 128
BANKS = 8
B, S, C = 64, 64, 32
LAYERS, M = 4, 12
KX = 2 * M
XQ, XR = 4, 16
BQ, B2 = 4, 2
CH = BQ * B2
CHUNKS = B // CH
COLS = CH * XR * S
QUART = COLS // 4
PAIRS = CHUNKS // 2
XB = 3 * B
STAGE = 3 * BQ * 144
STAGED = CHUNKS - 1
PIECE = 12
KYG = M // 4
E, H, D = 8, 256, 64
TILES = B * S // P
LOADS = 4 * CHUNKS + PAIRS
V_ACT = 2 * 4 * CHUNKS
BN_STEPS = 13
BN_EPS = 1e-5
LN_EPS = 1e-5



def forward_jobs(c, first=False, last=False):
    over_y = [("dfty", c + 1, j) for j in range(8)]
    if first:
        return [("dfty", 0, j) for j in range(8)]
    over_x = [("dftx", c, j) for j in range(BQ)]
    if last:
        return over_x
    jobs = []
    for j in range(BQ):
        jobs += [over_y[j], over_x[j]]
    return jobs + over_y[BQ:]


def inverse_jobs(c, first=False, last=False):
    back = [("back", c + 1, bq, ri) for bq in range(BQ) for ri in range(2)]
    idft = [("idftx", c + 1, j) for j in range(8)]
    if first:
        return [("back", 0, *j[2:]) for j in back] + [("idftx", 0, *j[2:]) for j in idft]
    out = [("out", c, j) for j in range(16)]
    if last:
        return out
    jobs = []
    for j in range(8):
        jobs += [out[j], back[j]]
    jobs += [out[8], idft[0], out[9], idft[1], out[10], idft[2], idft[3], out[11], idft[4], idft[5], out[12],
             idft[6], idft[7], out[13], out[14], out[15]]
    return jobs


def field_jobs():
    jobs = []
    for c in range(CHUNKS + 2):
        if c < CHUNKS:
            jobs.append(("fdfty", c))
        if 1 <= c <= CHUNKS:
            jobs.append(("fdftx", c - 1))
        if c >= 2:
            jobs += [("lift", c - 2, hf, j) for hf in range(2) for j in range(2)]
    return jobs


FIELD = field_jobs()
FWD_FIRST = forward_jobs(0, first=True)
FWD_PAIR = forward_jobs(0) + forward_jobs(1)
FWD_LAST = forward_jobs(0) + forward_jobs(1, last=True)
MIX = [("mix", j) for j in range(KYG * KX // 3)]
INV_FIRST = inverse_jobs(0, first=True)
INV_PAIR = inverse_jobs(0) + inverse_jobs(1)
INV_LAST = inverse_jobs(0) + inverse_jobs(1, last=True)
for seg in (FIELD, FWD_FIRST, FWD_PAIR, FWD_LAST, MIX, INV_FIRST, INV_PAIR, INV_LAST):
    assert len(seg) % BANKS == 0
N_FWD = len(FWD_FIRST) + (PAIRS - 1) * len(FWD_PAIR) + len(FWD_LAST)
N_INV = len(INV_FIRST) + (PAIRS - 1) * len(INV_PAIR) + len(INV_LAST)
N_LAYER = N_FWD + len(MIX) + N_INV
N_ZERO = len(FIELD) + len(MIX) + N_INV
N_ALL = N_ZERO + (LAYERS - 1) * N_LAYER


def place(seg, *job):
    return seg.index(job)


def done_after(half_base, j):
    return half_base + (j // 2 + 5), half_base + ((j + 1) // 2 + 4)


TAIL = []
for j in range(8):
    TAIL += [("xnT", j)] + ([("qkv", 2 * j - 2), ("qkv", 2 * j - 1)] if j else [])
TAIL += [("qkv", 14), ("qkv", 15), ("knorm", 0)] + [("kv", j) for j in range(8)] + [("qT", 0), ("qT", 1)]
for j in range(8):
    TAIL += [("attnT", j)] + ([("qT", j + 2)] if j < 6 else []) + ([("proj", (j - 3) // 2)] if j in (3, 5) else [])
TAIL += [("proj", 2), ("proj", 3)] + [("x2T", j) for j in range(5)] + [("gate", 0)]
TAIL += [("x2T", j) for j in range(5, 8)] + [("gate", 1)] + [("combT", j) for j in range(4)]
TAIL_ACT = ("xnT", "qkv", "qT", "attnT", "x2T", "combT")


def tail_no(kind, j):
    return TAIL.index((kind, j))


def tail_count(n):
    a = sum(k in TAIL_ACT for k, _ in TAIL[:n + 1])
    return a, n + 1 - a


def build(nc, x_f, x_t, c_pos, p_t, p_e, w_bd, w_b, spec_w, bn_g, bn_b, q_bd, q_b, wqkv, wout, wgate, w1t, w2t, b1, bg, b2,
          c_fy, c_fyt, c_g, c_gf, c_gi, c_fyi, c_id, c_avg, c_ones, c_image, out):
    ctx = ExitStack()
    with ctx:
        def sb(name, cols, parts=P):
            return ctx.enter_context(nc.sbuf_tensor(name, [parts, cols], F32))

        def sem(name):
            return ctx.enter_context(nc.semaphore(name))

        bank = [ctx.enter_context(nc.psum_tensor(f"bank{i}", [P, 512], F32)) for i in range(BANKS)]
        u_dram = nc.dram_tensor("u_scratch", [CHUNKS, P, COLS], F32, kind="Internal").ap()
        h_dram = nc.dram_tensor("h_scratch", [B, S, S], F32, kind="Internal").ap()
        comb_dram = nc.dram_tensor("comb_scratch", [E, B * S], F32, kind="Internal").ap()

        base = (nc.sbuf_base + 31) // 32 * 32
        area_x = sb("area_x", KYG * KX * XB)
        area_o = sb("area_o", KYG * KX * XB)
        area_v = sb("area_v", COLS)
        area_pt = sb("area_pt", 2 * 4096)
        area_p, area_t = area_pt[:, 0:4096], area_pt[:, 4096:8192]
        area_s = sb("area_s", max(2 * STAGE, 512 + 2 * QUART))
        fy = sb("fy", 2 * 2 * M)
        gx = sb("gx", 2 * 96)
        fyt = sb("fyt", 2 * P)
        gxf = sb("gxf", 2 * 96)
        gi = sb("gi", P)
        fyi = sb("fyi", BQ * S)
        wconv = sb("wconv", P)
        ident = sb("ident", P)
        avg = sb("avg", P)
        ones = sb("ones", P)
        image = sb("image", 2)
        pw = sb("pw", 4 * P + KYG * P)
        wfield = sb("wfield", 4 * P)
        chan = sb("chan", 3 * LAYERS + 1)
        qbd = sb("qbd", 33)
        a32 = sb("a32", 32)
        stats = sb("stats", CHUNKS * 16 * 6)
        bnw = sb("bnw", 16)
        wb_now = sb("wb_now", 1)
        sc = sb("sc", 2)

        xs = area_x
        os_ = area_o
        stage = [area_s[:, 0:STAGE], area_s[:, STAGE:2 * STAGE]]
        fy_out = [area_s[:, 0:96 * C], area_o[:, COLS:COLS + 96 * C]]
        turned = area_t
        v_fwd = area_v
        v_t = [area_o[:, 0:COLS], area_pt[:, :]]
        v_inv = [area_v[:, :], area_x[:, 0:COLS]]
        pix_inv = [area_p, area_x[:, COLS:COLS + 4096]]
        W = PIECE * 2 * P
        w_slot = [area_v[:, 0:W], area_v[:, W:2 * W], area_p[:, 0:W], area_s[:, 0:W]]
        W_PLAN = [0, 1, 3, 2, 3, 2]
        fpix = area_o[:, 0:2048]
        fpos = area_o[:, 2048:2432]
        f_y = [area_o[:, COLS + 384 * k:COLS + 384 * (k + 1)] for k in range(2)]
        f_x = [area_o[:, COLS + 768 + 384 * k:COLS + 768 + 384 * (k + 1)] for k in range(2)]

        READ_ORDER = [CHUNKS - 2, CHUNKS - 1] + list(range(CHUNKS - 2))
        v_last = [[a[:, QUART * q:QUART * (q + 1)] for q in range(4)] for a in (area_v, area_x, area_o)]
        READ_BUF = [0, 1, 2, 3, 4, 5, 2, 6]
        v_last.append([area_o[:, COLS:COLS + QUART], area_o[:, COLS + QUART:COLS + 2 * QUART],
                       area_p[:, 0:QUART], area_p[:, QUART:2 * QUART]])
        v_last.append([area_s[:, 512:512 + QUART], area_s[:, 512 + QUART:512 + 2 * QUART],
                       area_x[:, COLS + QUART:COLS + 2 * QUART], v_last[0][3]])
        v_last.append(v_last[0][0:3] + v_last[1][0:1])
        v_last.append(v_last[1][1:4] + v_last[0][3:4])
        hq = [area_t[:, 0:2048], area_x[:, COLS:COLS + 2048]]
        h = area_t[:, 2048:4096]
        vv = area_x[:, 0:2048]
        wk = area_x[:, 6144:12288]
        xnT = area_v[:, 0:4096]
        qT = area_v[:, 4096:8192]
        atT = area_o[:, 0:4096]
        cT = area_v[:, 4096:6144]
        sq = wk[:, 4096:6144]
        xhl = wk[:, 0:4096]
        score, rank, hot1, hot2 = (wk[:, 256 * k:256 * (k + 1)] for k in range(4))
        kvs = area_o[:, 4096:8192]
        w1s = area_o[:, 8192:10240]
        w1_high = area_t[:, 0:2048]
        w2s = area_o[:, 10240:11264]
        hb = [area_p[:, 0:2048], area_p[:, 2048:4096]]
        xn = area_p[:, 2048:4096]
        wq_s = area_s[:, 0:192]
        wo_s = area_s[:, 192:256]
        wg_s = area_s[:, 256:264]
        b2_s = area_s[:, 264:392]
        yT = area_s[:, 512:1024]
        small = stats[:, 0:768]
        def in_area(name, area_cols, at, cols):
            return nc.alloc_sbuf_tensor_at(name, [P, cols], F32R, offset=base + 4 * (area_cols + at))

        w1_high_r = in_area("w1_high_r", 2 * KYG * KX * XB + COLS, 4096, 2048)
        w1_rest_r = in_area("w1_rest_r", KYG * KX * XB, 8192, 2048)
        xnT_r = in_area("xnT_r", 2 * KYG * KX * XB, 0, 4096)
        b1s = area_s[:, 1024:1040]
        bg_s = area_s[:, 1040:1048]
        cb = area_x[:, 0:8192]

        const_in = sem("const_in")
        fpix_in = sem("fpix_in")
        v_in = [[sem(f"v_in{p}{q}") for q in range(4)] for p in range(2)]
        v_out = [[sem(f"v_out{p}{q}") for q in range(4)] for p in range(2)]
        wc_in = sem("wc_in")
        w_in = [sem(f"w_in{k}") for k in range(4)]
        t_zero = sem("t_zero")
        f_zero = sem("f_zero")
        wf_mm = sem("wf_mm")
        wf_cp = sem("wf_cp")
        v_act = sem("v_act")
        v_tp = sem("v_tp")
        pe_job = sem("pe_job")
        act_job = sem("act_job")
        dve_job = sem("dve_job")
        stage_cp = sem("stage_cp")
        stat_done = sem("stat_done")
        bn_agg = sem("bn_agg")
        bn_mm = sem("bn_mm")
        bn_dev = sem("bn_dev")
        bn_var = sem("bn_var")
        bn_sqrt = sem("bn_sqrt")
        sc_ready = sem("sc_ready")
        dve_chain = sem("dve_chain")
        a_ready = sem("a_ready")
        tail_in = sem("tail_in")
        fin_in = [sem(f"fin_in{k}") for k in range(2, CHUNKS)]
        read_mm = sem("read_mm")
        read_act = sem("read_act")
        read_dve = sem("read_dve")
        hq_out = [sem("hq_out0"), sem("hq_out1")]
        h_in = [sem("h_in0"), sem("h_in1")]
        k_sq = sem("k_sq")
        rows_set = sem("rows_set")
        pe_tail = sem("pe_tail")
        act_tail = sem("act_tail")
        dve_tail = sem("dve_tail")
        s_step = sem("s_step")
        s_root = sem("s_root")
        a_step = sem("a_step")
        comb_out = sem("comb_out")
        cb_in = [sem(f"cb_in{e}") for e in range(E)]
        hid_scaled = sem("hid_scaled")
        hid_mm = sem("hid_mm")
        hid_relu = sem("hid_relu")
        y_mm = sem("y_mm")
        y_cp = sem("y_cp")
        y_turn = sem("y_turn")
        y_done = sem("y_done")
        out_done = sem("out_done")
        passed = {e: sem(f"passed_{e}") for e in ("pe", "dve", "pool", "sp")}

        def stop_for(eng, name, signal, value):
            eng.wait_ge(signal, value)
            eng.sem_inc(passed[name], 1)

        CONSTS = [(fy[:, :], c_fy), (gx[:, :], c_g), (fyt[:, :], c_fyt), (gxf[:, :], c_gf), (fyi[:, :], c_fyi), (ident[:, :], c_id), (avg[:, :], c_avg),
                  (ones[:, :], c_ones), (image[:, :], c_image), (gi[0:96, :], c_gi), (pw[:, 0:4 * P], p_t), (pw[:, 4 * P:], p_e),
                  (chan[:, 0:LAYERS], w_b), (chan[:, LAYERS:2 * LAYERS], bn_g), (chan[:, 2 * LAYERS:3 * LAYERS], bn_b),
                  (qbd[:, 0:32], q_bd), (qbd[:, 32:33], q_b)]
        CONST_READY = 16 * len(CONSTS)

        def at_fwd(m):
            return m * (N_LAYER // 2) + N_ZERO // 2

        def at_mix(m):
            return len(FIELD) // 2 if m is None else at_fwd(m) + N_FWD // 2

        def at_inv(m):
            return at_mix(m) + len(MIX) // 2

        FWD_IN = len(FWD_FIRST) // 2
        INV_IN = len(INV_FIRST) // 2
        INV_END = N_INV // 2

        def layer(m):
            return 0 if m is None else m + 1

        block = ctx.enter_context(nc.Block())

        def read_out_store(sp, k):
            c = READ_ORDER[k]
            sp.wait_ge(read_act, 2 * k + 2)
            sp.wait_ge(read_dve, 2 * k + 2)
            for j in range(4):
                dst = h_dram[8 * c:8 * c + 8].rearrange("b (q g j) y -> j q g b y", q=XQ, j=4)[j]
                src = hq[k % 2][32 * j:32 * j + 4, :].rearrange("q (g b y) -> q g b y", g=4, y=S)
                sp.dma_start(dst, src).then_inc(hq_out[k % 2], 16)

        def final_store(sp, i):
            sp.wait_ge(y_done, i + 2)
            sp.dma_start(out[16 * i:16 * i + 16].rearrange("(t b) x y -> (b x) t y", b=2),
                         h[:, i * 512:(i + 1) * 512].rearrange("p (t y) -> p t y", y=D)).then_inc(out_done, 16)

        @block.sync
        def _(sp):
            for dst, src in CONSTS:
                sp.dma_start(dst, src).then_inc(const_in, 16)
            sp.dma_start(wconv[:, :], w_bd[0]).then_inc(wc_in, 16)
            sp.dma_start(fpix, x_t).then_inc(fpix_in, 16)
            sp.dma_start(fpos, c_pos).then_inc(fpix_in, 16)

            def emptied(half_base, j):
                a, d = done_after(half_base, j)
                stop_for(sp, "sp", act_job, a)
                stop_for(sp, "sp", dve_job, d)

            def pe_done(half_base, j):
                stop_for(sp, "sp", pe_job, half_base * 2 + (j + 1))

            def weights(m, piece):
                k = W_PLAN[piece]
                src = spec_w[:, piece * W:(piece + 1) * W] if m is None else \
                    spec_w[:, bass.ds(m * (KYG * KX * 2 * P) + (KYG * KX * 2 * P + piece * W), W)]
                sp.dma_start(w_slot[k], src).then_inc(w_in[k], 16)

            def stored(c, q):
                src = u_dram[c] if isinstance(c, int) else u_dram[bass.ds(c, 1)].rearrange("a p n -> (a p) n")
                return src[:, q * QUART:(q + 1) * QUART]

            def load(dst, c, p, q):
                sp.dma_start(dst[:, q * QUART:(q + 1) * QUART], stored(c, q)).then_inc(v_in[p][q], 16)

            def load_forward(c, q):
                src = u_dram[c] if isinstance(c, int) else u_dram[bass.ds(c, 1)].rearrange("a p n -> (a p) n")
                for bq in range(BQ):
                    sp.dma_start(v_fwd[bq * C:(bq + 1) * C, q * QUART:(q + 1) * QUART].rearrange("p (x w) -> p x w", w=P),
                                 src[q * C:(q + 1) * C, :].rearrange("p (x b w) -> p b x w", b=BQ, w=P)[:, bq])\
                      .then_inc(v_in[0][q], 16)

            def load_field(dst, c, p, q):
                src = x_f[c] if isinstance(c, int) else x_f[bass.ds(c, 1)].rearrange("a p n -> (a p) n")
                sp.dma_start(dst[:, 3 * QUART + q * 512:3 * QUART + (q + 1) * 512], src[:, q * 512:(q + 1) * 512])\
                  .then_inc(v_in[p][q], 16)

            def mixing(m):
                base = at_mix(m)
                pe_done(base, 7)
                fetch = load_field if m is None else load
                fetch(v_inv[0], 0, 0, 0)
                pe_done(base, 11)
                weights(m, 4)
                pe_done(base, 15)
                weights(m, 5)
                for q in range(1, 4):
                    fetch(v_inv[0], 0, 0, q)

            def store(seg, half_base, i, c):
                chunk = i * 2 + c
                for q in range(4):
                    emptied(half_base, place(seg, "out", c, 4 * q + 3))
                    sp.dma_start(stored(chunk, q), v_inv[c][:, q * QUART:(q + 1) * QUART])\
                      .then_inc(v_out[c][q], 16)

            def inverse(m):
                fetch = load_field if m is None else load
                base = at_mix(m)
                pe_done(base, len(MIX) - 1)
                for q in range(4):
                    fetch(v_inv[1], 1, 1, q)

                with sp.Fori(0, PAIRS - 1) as i:
                    for c in range(2):
                        store(INV_PAIR, at_inv(m) + INV_IN + i * (len(INV_PAIR) // 2), i, c)
                        stop_for(sp, "sp", stat_done, (i * 2 + layer(m) * CHUNKS) * 16 + (c * 16 + 16))
                        for q in range(4):
                            for stored in (range(4) if m is None and q == 0 else () if m is None else (q,)):
                                stop_for(sp, "sp", v_out[c][stored], (i + layer(m) * PAIRS) * 16 + 16)
                            fetch(v_inv[c], i * 2 + (2 + c), c, q)

            for piece in range(4):
                weights(None, piece)
            mixing(None)
            inverse(None)

            with sp.Fori(0, LAYERS - 1) as m:
                before = m * (N_LAYER // 2) + ((len(FIELD) + len(MIX)) // 2 + INV_IN + (PAIRS - 1) * (len(INV_PAIR) // 2))
                store(INV_LAST, before, PAIRS - 1, 0)
                for q in range(4):
                    stop_for(sp, "sp", v_out[0][q], m * (16 * PAIRS) + 16 * PAIRS)
                stop_for(sp, "sp", stat_done, m * (16 * CHUNKS) + 16 * (CHUNKS - 1))
                for q in range(4):
                    load_forward(0, q)
                store(INV_LAST, before, PAIRS - 1, 1)
                stop_for(sp, "sp", sc_ready, m + 1)
                sp.dma_start(wconv[:, :], w_bd[bass.ds(m + 1, 1)].rearrange("a p n -> (a p) n")).then_inc(wc_in, 16)
                for q in range(4):
                    stop_for(sp, "sp", v_out[1][q], m * (16 * PAIRS) + 16 * PAIRS)
                for q in range(4):
                    stop_for(sp, "sp", v_tp, m * (4 * CHUNKS) + (q + 1))
                    load_forward(1, q)
                with sp.Fori(0, PAIRS - 1) as i:
                    for c in range(2):
                        for q in range(4):
                            stop_for(sp, "sp", v_tp, m * (4 * CHUNKS) + i * 8 + (c * 4 + q + 5))
                            load_forward(i * 2 + (2 + c), q)
                last = at_fwd(m) + FWD_IN + (PAIRS - 1) * (len(FWD_PAIR) // 2)
                stop_for(sp, "sp", v_tp, m * (4 * CHUNKS) + 4 * CHUNKS)
                weights(m, 0)
                weights(m, 1)
                pe_done(last, place(FWD_LAST, "dftx", 0, BQ - 1))
                weights(m, 2)
                pe_done(last, place(FWD_LAST, "dfty", 1, 7))
                weights(m, 3)
                mixing(m)
                inverse(m)

            def load_last(k, quarters=range(4)):
                for q in quarters:
                    if k == 3 and q == 2:
                        sp.wait_ge(pe_job, pe_last + place(INV_LAST, "out", 0, 15) + 1)
                    sp.dma_start(v_last[READ_BUF[k]][q], stored(READ_ORDER[k], q)).then_inc(fin_in[k - 2], 16)

            pe_last = N_ALL - len(INV_LAST)
            sp.wait_ge(stage_cp, STAGED * LAYERS)
            for c in range(2):
                for q in range(4):
                    sp.wait_ge(v_out[c][q], 16 * (PAIRS * LAYERS - 1))
            load_last(2)
            load_last(3)
            sp.wait_ge(pe_job, pe_last + place(INV_LAST, "back", 1, BQ - 1, 1) + 1)
            load_last(4, (0, 1))
            sp.wait_ge(pe_job, N_ALL)
            for dst, src in ((wq_s, wqkv), (wo_s, wout), (wg_s, wgate), (b2_s, b2)):
                sp.dma_start(dst, src).then_inc(tail_in, 16)
            load_last(4, (2,))

            def load_h(k):
                c = READ_ORDER[k]
                sp.wait_ge(hq_out[k % 2], 64 * (k // 2 + 1))
                sp.dma_start(h[:, c * 256:(c + 1) * 256].rearrange("p (t y) -> p t y", y=D),
                             h_dram[8 * c:8 * c + 8].rearrange("(t b) x y -> (b x) t y", b=2)).then_inc(h_in[c // 4], 16)

            for k in range(CHUNKS):
                if k <= 4:
                    sp.wait_ge(read_mm, 4 * (k + 1))
                for number, quarters in {0: ((4, (3,)), (5, (0, 1, 2))), 1: ((5, (3,)),),
                                         2: ((6, range(4)),), 3: ((7, (0, 1, 2)),), 4: ((7, (3,)),)}.get(k, ()):
                    load_last(number, quarters)
                read_out_store(sp, k)
                if k >= 1:
                    load_h(k - 1)
            load_h(CHUNKS - 1)
            sp.wait_ge(read_mm, 4 * CHUNKS)
            for dst, src in ((w1s, w1t), (w2s, w2t), (b1s, b1), (bg_s, bg)):
                sp.dma_start(dst, src).then_inc(tail_in, 16)
            sp.wait_ge(act_tail, tail_count(len(TAIL) - 1)[0])
            for ab in range(2):
                sp.dma_start(comb_dram.rearrange("e (i ab t) -> ab e i t", ab=2, t=512)[ab],
                             cT[ab * D:ab * D + E, :].rearrange("e (i t) -> e i t", t=512)).then_inc(comb_out, 16)
            sp.wait_ge(comb_out, 32)
            for i in range(4):
                for e in range(E):
                    if i >= 1:
                        sp.wait_ge(hid_scaled, 16 * (i - 1) + 2 * e + 2)
                    sp.dma_start(cb[:, e * 1024:(e + 1) * 1024],
                                 comb_dram[e:e + 1, i * 1024:(i + 1) * 1024].to_broadcast([P, 1024]))\
                      .then_inc(cb_in[e], 16)
                if i >= 1:
                    final_store(sp, i - 1)
            final_store(sp, 3)
            sp.wait_ge(out_done, 16 * 4)

        @block.tensor
        def _(pe):
            pe.wait_ge(const_in, CONST_READY)
            pe.wait_ge(wc_in, 16)
            for q in range(4):
                mm = pe.matmul(bank[0][:, q * P:(q + 1) * P], pw[:, q * P:(q + 1) * P], wconv[:, :],
                               start=True, stop=True)
            mm.then_inc(wf_mm, 1)
            pe.wait_ge(wf_cp, 1)

            def emptied(half_base, j):
                a, d = done_after(half_base, j)
                pe.wait_ge(act_job, a)
                pe.wait_ge(dve_job, d)

            def run(seg, half_base, m, i=0):
                for j, job in enumerate(seg):
                    pe.wait_ge((act_job, dve_job)[j % 2], half_base + (j // 2 + 1))
                    product(seg, half_base, m, i, j, job)

            def product(seg, half_base, m, i, j, job):
                kind = job[0]
                ps = bank[j % BANKS]
                if kind == "fdfty":
                    c = job[1]
                    if c == 0:
                        pe.wait_ge(fpix_in, 32)
                        for f in range(3):
                            pe.matmul(ps[:, 96 + f * 48:96 + (f + 1) * 48], fpos[:, f * P:(f + 1) * P], fy[:, 0:48],
                                      start=True, stop=True)
                    for hf in range(2):
                        mm = pe.matmul(ps[:, hf * 48:(hf + 1) * 48], fpix[:, (2 * c + hf) * P:(2 * c + hf + 1) * P],
                                       fy[:, 0:48], start=True, stop=True)
                elif kind == "fdftx":
                    c = job[1]
                    emptied(half_base, place(seg, "fdfty", c))
                    for hb2 in range(4):
                        for ri in range(2):
                            at = hb2 * 96 + ri * 48
                            mm = pe.matmul(ps[0:48, hb2 * 96:(hb2 + 1) * 96], f_y[c % 2][:, at:at + 48],
                                           gxf[:, ri * 96:(ri + 1) * 96], start=(ri == 0), stop=(ri == 1))
                elif kind == "lift":
                    _, c, hf, b2_ = job
                    if hf == 0 and b2_ == 0:
                        emptied(half_base, place(seg, "fdftx", c))
                    at = (2 * hf + b2_) * 96
                    for kyg in range(KYG):
                        mm = pe.matmul(ps[:, kyg * 96:(kyg + 1) * 96], pw[:, (4 + kyg) * P:(5 + kyg) * P],
                                       f_x[c % 2][:, at:at + 96], start=True, stop=True)
                elif kind == "dfty":
                    _, c, n = job
                    if n == 0:
                        pe.wait_ge(v_tp, m * (4 * CHUNKS) + i * 8 + (4 * c + 4))
                    src = v_t[c % 2].rearrange("p (x h c) -> p x h c", h=2, c=C)
                    for k in range(4):
                        for half in range(2):
                            mm = pe.matmul(ps[:, k * P:(k + 1) * P], src[:, :, half, 4 * n + k],
                                           fyt[:, half * P:(half + 1) * P], start=(half == 0), stop=(half == 1))
                elif kind == "dftx":
                    _, c, bq = job
                    if bq == 0:
                        emptied(half_base, -1 if c == 0 else place(seg, "dfty", c, 7))
                    for kyg in range(KYG):
                        for ri in range(2):
                            at = bq * 768 + ri * 384 + kyg * P
                            mm = pe.matmul(ps[:, kyg * 96:(kyg + 1) * 96], fy_out[c][:, at:at + P],
                                           gx[:, ri * 96:(ri + 1) * 96], start=(ri == 0), stop=(ri == 1))
                elif kind == "mix":
                    n = job[1]
                    if n == 0:
                        emptied(half_base, -1)
                    if n % 4 == 0:
                        k = W_PLAN[n // 4]
                        uses = W_PLAN.count(k)
                        nth = W_PLAN[:n // 4].count(k) + 1
                        pe.wait_ge(w_in[k], 16 * nth if m is None else m * (16 * uses) + 16 * (uses + nth))
                    for k in range(3):
                        g = 3 * n + k
                        for ri in range(2):
                            at = (g % PIECE * 2 + ri) * P
                            x_at = g * XB + (1 - ri) * B
                            mm = pe.matmul(ps[:, k * P:(k + 1) * P], w_slot[W_PLAN[n // 4]][:, at:at + P],
                                           xs[:, x_at:x_at + P], start=(ri == 0), stop=(ri == 1))
                elif kind == "back":
                    _, c, bq, ri = job
                    if seg is INV_FIRST and bq == 0 and ri == 0:
                        emptied(half_base, -1)
                        pe.wait_ge(t_zero, 1 if m is None else m + 2)
                    elif bq == 0 and ri == 0:
                        pe.wait_ge(stage_cp, i * 2 + c if m is None else m * STAGED + i * 2 + (STAGED + c))
                    for kyg in range(KYG):
                        at = kyg * 576 + bq * 144 + ri * 48
                        src = stage[c % 2][:, at:at + 96]
                        if seg is INV_FIRST:
                            at += kyg * 576 * (CHUNKS - 1)
                            src = os_[:, at:at + 96]
                        mm = pe.transpose(ps[0:96, kyg * P:(kyg + 1) * P], src, ident[:, :])
                elif kind == "idftx":
                    _, c, n = job
                    if n == 0:
                        emptied(half_base, place(seg, "back", c, BQ - 1, 1))
                    src = turned[0:96, :].rearrange("p (k o) -> p k o", o=C)
                    for k in range(4):
                        mm = pe.matmul(ps[:, k * P:(k + 1) * P], src[:, :, 4 * n + k], gi[0:96, :],
                                       start=True, stop=True)
                else:
                    _, c, n = job
                    if n == 0:
                        emptied(half_base, -1 if c == 0 else place(seg, "idftx", c, 7))
                    if m is None and n < 4:
                        pe.wait_ge(v_in[c][n], i * 16 + 16)
                    if m is not None and n % 4 == 0:
                        pe.wait_ge(v_act, m * V_ACT + i * 8 + (4 * CHUNKS + c * 4 + n // 4 + 1))
                    for k in range(2):
                        at = (XR * k + n) * P
                        pe.matmul(ps[:, :].rearrange("p (q b y) -> p q b y", q=BQ, b=B2)[:, :, k],
                                  pix_inv[c][:, at:at + P], fyi[:, :], start=(k == 0), stop=False)
                    at, w = n * 512, wconv[:, :]
                    if m is None:
                        at, w = 3 * QUART + n % 4 * 512, wfield[:, n // 4 * P:(n // 4 + 1) * P]
                    mm = pe.matmul(ps[:, :], w, v_inv[c][:, at:at + 512], start=False, stop=True)
                mm.then_inc(pe_job, 1)

            def inverse(m):
                run(MIX, at_mix(m), m)
                run(INV_FIRST, at_inv(m), m)
                with pe.Fori(0, PAIRS - 1) as i:
                    run(INV_PAIR, at_inv(m) + INV_IN + i * (len(INV_PAIR) // 2), m, i)
                run(INV_LAST, at_inv(m) + INV_IN + (PAIRS - 1) * (len(INV_PAIR) // 2), m, PAIRS - 1)
                emptied(at_inv(m) + INV_END, -1)
                pe.wait_ge(bn_agg, layer(m) + 1)
                pe.matmul(bank[7][:, 0:1], avg[:, :], bnw[:, 0:1], start=True, stop=True).then_inc(bn_mm, 1)
                pe.wait_ge(bn_dev, layer(m) + 1)
                pe.matmul(bank[7][:, 8:9], avg[:, :], bnw[:, 2:3], start=True, stop=True).then_inc(bn_mm, 1)
                stop_for(pe, "pe", sc_ready, layer(m) + 1)

            run(FIELD, 0, None)
            inverse(None)
            with pe.Fori(0, LAYERS - 1) as m:
                run(FWD_FIRST, at_fwd(m), m)
                with pe.Fori(0, PAIRS - 1) as i:
                    run(FWD_PAIR, at_fwd(m) + FWD_IN + i * (len(FWD_PAIR) // 2), m, i)
                run(FWD_LAST, at_fwd(m) + FWD_IN + (PAIRS - 1) * (len(FWD_PAIR) // 2), m, PAIRS - 1)
                pe.wait_ge(wc_in, m * 16 + 32)
                inverse(m)

            pe.wait_ge(a_ready, 1)
            pe.matmul(bank[7][:, 0:1], wfield[:, 0:P], qbd[:, 0:1], start=True, stop=True).then_inc(bn_mm, 1)
            pe.wait_ge(a_ready, 2)
            for c in range(CHUNKS):
                if c >= 2:
                    pe.wait_ge(fin_in[c - 2], 64)
                for g in range(4):
                    n = 4 * c + g
                    if n >= BANKS:
                        pe.wait_ge((read_act, read_dve)[n % 2], (n - BANKS) // 2 + 1)
                    for j in range(4):
                        mm = pe.matmul(bank[n % BANKS][32 * j:32 * j + 32, :], a32[:, :],
                                       v_last[READ_BUF[c]][g][:, j * 512:(j + 1) * 512], start=True, stop=True)
                    mm.then_inc(read_mm, 1)
            pe.wait_ge(read_act, 2 * CHUNKS)
            pe.wait_ge(read_dve, 2 * CHUNKS)

            def start_tail(kind, j):
                n = tail_no(kind, j)
                if n >= BANKS:
                    tail_wait(n - BANKS)
                return bank[n % BANKS]

            def tail_wait(n):
                a, d = tail_count(n)
                if a:
                    pe.wait_ge(act_tail, a)
                if d:
                    pe.wait_ge(dve_tail, d)

            def flip(kind, j, src, width):
                ps = start_tail(kind, j)
                for k in range(4):
                    t = 4 * j + k
                    mm = pe.transpose(ps[0:width, k * P:(k + 1) * P], src[:, t * width:(t + 1) * width], ident[:, :])
                mm.then_inc(pe_tail, 1)

            k_v = wk[:, 0:4096].rearrange("p (t a c) -> p t a c", a=2, c=D)

            def tail_job(kind, j):
                if kind in ("xnT", "qT", "x2T"):
                    if j % 4 == 0 and kind != "qT":
                        pe.wait_ge(s_step, {"xnT": 1, "x2T": 5}[kind] + j // 4)
                    if kind == "qT" and j == 0:
                        pe.wait_ge(s_step, 4)
                    return flip(kind, j, xhl, P) if kind == "x2T" else flip(kind, j, xn, D)
                ps = start_tail(kind, j)
                if kind == "qkv":
                    if j == 0:
                        pe.wait_ge(s_step, 1)
                        pe.wait_ge(rows_set, 1)
                    tail_wait(tail_no("xnT", j // 2))
                    for k in range(2):
                        t = 2 * j + k
                        mm = pe.matmul(ps[:, k * 192:(k + 1) * 192], xnT[:, t * P:(t + 1) * P], wq_s,
                                       start=True, stop=True)
                elif kind == "knorm":
                    pe.wait_ge(k_sq, 1)
                    for t in range(TILES):
                        mm = pe.matmul(ps[0:D, 2 * t:2 * t + 2], sq[:, t * D:(t + 1) * D], image[:, :],
                                       start=True, stop=True)
                elif kind == "kv":
                    for k in range(8):
                        t, b = 8 * (j % 4) + k, j // 4
                        mm = pe.matmul(ps[0:D, k * D:(k + 1) * D], k_v[64 * b:64 * b + 64, t, 1, :],
                                       vv[64 * b:64 * b + 64, t * D:(t + 1) * D], start=True, stop=True)
                elif kind == "attnT":
                    tail_wait(tail_no("qT", j))
                    if j == 0:
                        pe.wait_ge(rows_set, 2)
                    for k in range(8):
                        b = 8 * j + k
                        at = (32 * (b % 2) + b // 2) * D
                        pe.matmul(ps[0:D, k * D:(k + 1) * D], kvs[:, at:at + D], qT[:, b * D:(b + 1) * D],
                                  start=(k == 0), stop=False)
                    mm = pe.matmul(ps[0:D, :], wq_s[:, 128:192], xnT[:, j * 512:(j + 1) * 512],
                                   start=False, stop=True)
                elif kind == "proj":
                    tail_wait(tail_no("attnT", 2 * j + 1))
                    for k in range(8):
                        t = 8 * j + k
                        mm = pe.matmul(ps[:, k * D:(k + 1) * D], atT[:, t * P:(t + 1) * P], wo_s, start=True, stop=True)
                elif kind == "gate":
                    tail_wait(tail_no("x2T", 4 * j + 3))
                    for k in range(16):
                        t = 16 * j + k
                        mm = pe.matmul(ps[:, k * E:(k + 1) * E], xnT_r.bitcast(F32)[:, t * P:(t + 1) * P], wg_s,
                                       start=True, stop=True)
                else:
                    if j == 0:
                        pe.wait_ge(s_step, 7)
                    for k in range(4):
                        mm = pe.transpose(ps[:, k * P:(k + 1) * P], xn[:, (4 * j + k) * P:(4 * j + k + 1) * P], ident[:, :])
                mm.then_inc(pe_tail, 1)

            pe.wait_ge(tail_in, 16 * 4)
            for kind, j in TAIL:
                tail_job(kind, j)
            tail_wait(len(TAIL) - 1)
            pe.wait_ge(tail_in, 16 * 8)
            pe.sem_inc(y_mm, 2)
            pe.sem_inc(y_turn, 1)
            def hidden(i, e, first):
                for ab in range(2):
                    at = i * 1024 + ab * 512
                    x_in = xnT_r[:, at:at + 512] if first else xnT_r[:, bass.ds(at, 512)]
                    for half in range(2):
                        n = 4 * e + 2 * ab + half
                        pe.wait_ge(hid_relu, i * 32 + (n + 1))
                        for part, w in enumerate((w1_high_r, w1_rest_r)):
                            mm = pe.matmul(bank[n % 4][:, :], w[:, e * H + half * P:e * H + (half + 1) * P],
                                           x_in, start=(part == 0), stop=(part == 1))
                        mm.then_inc(hid_mm, 1)

            def turn_back(i):
                stop_for(pe, "pe", y_cp, i + 2)
                stop_for(pe, "pe", y_done, i + 1)
                for t in range(4):
                    mm = pe.transpose(bank[5][:, t * P:(t + 1) * P], yT[:, t * P:(t + 1) * P], ident[:, :])
                mm.then_inc(y_turn, 1)

            def experts(i, first):
                hidden(i, 0, first)
                hidden(i, 1, first)
                if not first:
                    turn_back(i + -1)
                pe.wait_ge(y_cp, i + 1)
                weights = cT[:, i * 512:(i + 1) * 512] if first else cT[:, bass.ds(i * 512, 512)]
                pe.matmul(bank[4][:, :], b2_s, weights, start=True, stop=False)
                for e in range(E):
                    pe.wait_ge(hid_scaled, i * 16 + (2 * e + 2))
                    for half in range(2):
                        for ab in range(2):
                            mm = pe.matmul(bank[4][ab * D:(ab + 1) * D, :], w2s[:, (2 * e + half) * D:(2 * e + half + 1) * D],
                                           hb[e % 2][:, ab * 1024 + half * 512:ab * 1024 + (half + 1) * 512],
                                           start=False, stop=(e == E - 1 and half == 1))
                    mm.then_inc(y_mm, 1)
                    if e + 2 < E:
                        hidden(i, e + 2, first)

            experts(0, True)
            with pe.Fori(1, 4) as i:
                experts(i, False)
            turn_back(3)

        def unload(copy, neg, add_bias, j, job):
            kind = job[0]
            ps = bank[j % BANKS]
            if kind == "fdfty":
                if job[1] == 0:
                    for k in range(2):
                        for hf in range(2):
                            copy(f_y[k].rearrange("p (h m f) -> p h m f", h=2, f=4)[:, hf, :, 1:4],
                                 ps[:, 96:240].rearrange("p (f m) -> p m f", f=3))
                return copy(f_y[job[1] % 2].rearrange("p (m f) -> p m f", f=4)[:, :, 0], ps[:, 0:96])
            if kind == "fdftx":
                return copy(f_x[job[1] % 2][0:48, :], ps[0:48, 0:384])
            if kind == "dfty":
                _, c, n = job
                dst = fy_out[c % 2].rearrange("p (m c) -> p c m", c=C)
                return copy(dst[:, 4 * n:4 * n + 4, :], ps[:, :].rearrange("p (c m) -> p c m", c=4)[:, :, 0:96])
            if kind == "back":
                _, c, bq, ri = job
                at = bq * 1024 + ri * 384
                return copy(turned[0:96, at:at + 384], ps[0:96, 0:384])
            if kind == "idftx":
                _, c, n = job
                dst = pix_inv[c % 2].rearrange("p (m o) -> p o m", o=C)
                return copy(dst[:, 4 * n:4 * n + 4, :], ps[:, :].rearrange("p (o m) -> p o m", o=4))
            if kind == "mix":
                n = job[1]
                kyg, kx = 3 * n // KX, 3 * n % KX
                dst = os_[:, :].rearrange("p (g q m k) -> p g k m q", g=KYG, m=3 * B2, k=KX)[:, kyg, kx:kx + 3]
                src = ps[:, 0:384].rearrange("p (k m q) -> p k m q", k=3, m=2 * B2)
                copy(dst[:, :, 0:4], src)
                return neg(dst[:, :, 4:6], src[:, :, 0:2])
            assert kind == "out"
            _, c, n = job
            return add_bias(v_inv[c][:, n * 512:(n + 1) * 512], ps[:, :])

        def unload_spectra(copy, neg, j, job, chunk):
            src = bank[j % BANKS][:, 0:288].rearrange("p (k r q) -> p k r q", r=2, q=2)
            if job[0] == "lift":
                at = chunk * BQ + (job[3] * 32 + 2 * job[2])
                dst = xs[:, :].rearrange("p (k r b) -> p k r b", r=3, b=B)[:, :, :, at:at + 2]
            else:
                at = chunk * BQ + job[2]
                cols = slice(at, at + 1) if isinstance(at, int) else bass.ds(at, 1)
                dst = xs[:, :].rearrange("p (k r e b) -> p k r e b", r=3, e=B2, b=B // B2)[:, :, :, :, cols]\
                    .rearrange("p k r e b -> p k r (e b)")
            copy(dst[:, :, 1:3], src)
            return neg(dst[:, :, 0], src[:, :, 1])

        @block.scalar
        def _(act):
            def copy(dst, src):
                return act.activation(dst, src, ACT.Copy)

            def neg(dst, src):
                return act.activation(dst, src, ACT.Copy, scale=-1.0)

            def add_bias(dst, src):
                return act.activation(dst, src, ACT.Identity, bias=wb_now[:, 0:1])

            def run(seg, half_base, i, extra):
                for j in range(0, len(seg), 2):
                    act.wait_ge(pe_job, half_base * 2 + (j + 1))
                    job = seg[j]
                    if job[0] in ("dftx", "lift"):
                        chunk = job[1] if job[0] == "lift" else i * 2 + job[1]
                        unload_spectra(copy, neg, j, job, chunk).then_inc(act_job, 1)
                    else:
                        unload(copy, neg, add_bias, j, job).then_inc(act_job, 1)
                    if extra and j in extra:
                        extra[j]()

            def relu(at):
                act.activation(at, at, ACT.Relu, bias=sc[:, 1:2], scale=sc[:, 0:1]).then_inc(v_act, 1)

            def relu_forward(m, i, c, q):
                act.wait_ge(v_in[0][q], m * (16 * LOADS) + i * (2 * 16 * 4) + 16 * (PAIRS + 4 * (c + 1)))
                relu(v_fwd[:, q * QUART:(q + 1) * QUART])

            def relu_inverse(m, i, c, q):
                if c % 2:
                    act.wait_ge(v_in[1][q], m * (16 * PAIRS) + (i + c // 2) * 16 + 16 * (PAIRS + 1))
                else:
                    act.wait_ge(v_in[0][q], m * (16 * LOADS) + (i + c // 2) * 16 + 16 * (PAIRS + 4 * CHUNKS + 1))
                relu(v_inv[c % 2][:, q * QUART:(q + 1) * QUART])

            def four(step, positions, m, i, c):
                return {j: (lambda q=q: step(m, i, c, q)) for q, j in enumerate(positions)}

            def inverse(m):
                first = (lambda q: lambda: relu_inverse(m, 0, 0, q))
                run(MIX, at_mix(m), 0, m is not None and {22: first(0)})
                run(INV_FIRST, at_inv(m), 0, m is not None and {4: first(1), 10: first(2), 14: first(3)})

                def extra(i, c):
                    if m is None:
                        return {}
                    base = 32 * c
                    return four(relu_inverse, [base + k for k in (6, 12, 18, 24)], m, i, c + 1)

                with act.Fori(0, PAIRS - 1) as i:
                    run(INV_PAIR, at_inv(m) + INV_IN + i * (len(INV_PAIR) // 2), i, {**extra(i, 0), **extra(i, 1)})
                run(INV_LAST, at_inv(m) + INV_IN + (PAIRS - 1) * (len(INV_PAIR) // 2), PAIRS - 1, extra(PAIRS - 1, 0))
                act.wait_ge(bn_var, layer(m) + 1)
                act.activation(bnw[:, 4:5], bnw[:, 3:4], ACT.Sqrt).then_inc(bn_sqrt, 1)

            act.wait_ge(const_in, CONST_READY)
            act.sem_inc(act_job, 4)
            act.wait_ge(wf_mm, 1)
            act.activation(wfield[:, :], bank[0][:, :], ACT.Copy).then_inc(wf_cp, 1)
            act.wait_ge(f_zero, 1)
            run(FIELD, 0, 0, None)
            inverse(None)
            with act.Fori(0, LAYERS - 1) as m:
                act.wait_ge(sc_ready, m + 1)
                for q in range(4):
                    relu_forward(m, 0, 0, q)
                relu_forward(m, 0, 1, 0)
                relu_forward(m, 0, 1, 1)
                run(FWD_FIRST, at_fwd(m), 0, {0: lambda: relu_forward(m, 0, 1, 2), 2: lambda: relu_forward(m, 0, 1, 3)})
                for q in range(4):
                    act.wait_ge(v_out[1][q], m * (16 * PAIRS) + 16 * PAIRS)
                with act.Fori(0, PAIRS - 1) as i:
                    run(FWD_PAIR, at_fwd(m) + FWD_IN + i * (len(FWD_PAIR) // 2), i,
                        {**four(relu_forward, (0, 2, 4, 6), m, i, 2), **four(relu_forward, (12, 14, 16, 18), m, i, 3)})
                run(FWD_LAST, at_fwd(m) + FWD_IN + (PAIRS - 1) * (len(FWD_PAIR) // 2), PAIRS - 1, None)
                inverse(m)

            for c in range(CHUNKS):
                for g in (0, 2):
                    n = 4 * c + g
                    if g == 0 and c >= 2:
                        act.wait_ge(hq_out[c % 2], 64 * (c // 2))
                    act.wait_ge(read_mm, n + 1)
                    act.activation(hq[c % 2][:, g * 512:(g + 1) * 512], bank[n % BANKS][:, :], ACT.Identity,
                                   bias=bnw[:, 12:13]).then_inc(read_act, 1)

            def root(step, dst, src):
                act.wait_ge(s_root, step)
                act.activation(dst, src, ACT.Sqrt).then_inc(a_step, 1)

            def root_half(step, half):
                at = 16 * half
                root(step, small[:, 320 + at:336 + at], small[:, 288 + at:304 + at])

            root_half(1, 0)
            for n, (kind, j) in enumerate(TAIL):
                if kind in TAIL_ACT:
                    act.wait_ge(pe_tail, n + 1)
                    ps = bank[n % BANKS]
                    if kind == "qkv":
                        src = ps[:, 0:384].rearrange("p (t a c) -> p t a c", a=3, c=D)
                        act.activation(wk[:, 512 * (j // 2) + 256 * (j % 2):512 * (j // 2) + 256 * (j % 2) + 256]
                                       .rearrange("p (t a c) -> p t a c", a=2, c=D), src[:, :, 0:2], ACT.Square)
                        act.activation(vv[:, j * P:(j + 1) * P].rearrange("p (t c) -> p t c", c=D), src[:, :, 2],
                                       ACT.Copy).then_inc(act_tail, 1)
                    else:
                        dst, rows = {"xnT": (xnT, D), "qT": (qT, D), "attnT": (atT, D), "x2T": (xnT_r, P),
                                     "combT": (cT, P)}[kind]
                        act.activation(dst[0:rows, j * 512:(j + 1) * 512], ps[0:rows, :], ACT.Copy).then_inc(act_tail, 1)
                if (kind, j) == ("qkv", 1):
                    root_half(2, 1)
                if (kind, j) == ("qkv", 15):
                    act.wait_ge(s_step, 3)
                    act.activation(sq.rearrange("p (t c) -> p t c", c=D),
                                   wk[:, 0:4096].rearrange("p (t a c) -> p t a c", a=2, c=D)[:, :, 1], ACT.Square)\
                       .then_inc(k_sq, 1)
                    root(3, small[:, 320:352], small[:, 288:320])
                    root(4, small[0:D, 448:512], small[0:D, 384:448])
                if (kind, j) == ("attnT", 7):
                    root_half(5, 0)
                if (kind, j) == ("x2T", 3):
                    root_half(6, 1)
                if (kind, j) == ("x2T", 7):
                    act.wait_ge(s_root, 7)
                    act.activation(small[:, 320:352], small[:, 288:320], ACT.Exp).then_inc(a_step, 1)
            act.sem_inc(hid_relu, 4)
            act.sem_inc(y_cp, 1)
            with act.Fori(0, 4) as i:
                for e in range(E):
                    act.wait_ge(y_mm, i * 8 + (e + 1))
                    for k in range(4):
                        n = 4 * e + k
                        act.wait_ge(hid_mm, i * 32 + (n + 1))
                        act.activation(hb[e % 2][:, k * 512:(k + 1) * 512], bank[n % 4][:, :], ACT.Relu,
                                       bias=b1s[:, 2 * e + k % 2:2 * e + k % 2 + 1])\
                           .then_inc(hid_relu, 1)
                act.wait_ge(y_mm, i * 8 + 10)
                act.wait_ge(y_turn, i + 1)
                act.activation(yT, bank[4][:, :], ACT.Copy).then_inc(y_cp, 1)

        @block.vector
        def _(dve):
            chained = [0]

            def link(ins):
                chained[0] += 1
                ins.then_inc(dve_chain, 1)
                dve.wait_ge(dve_chain, chained[0])

            def copy(dst, src):
                return dve.tensor_copy(dst, src)

            def neg(dst, src):
                return dve.tensor_scalar(dst, src, -1.0, None, ALU.mult)

            def add_bias(dst, src):
                return dve.tensor_scalar(dst, src, wb_now[:, 0:1], None, ALU.add)

            def stat(seg, half_base, m, i, c, n):
                a, d = done_after(half_base, place(seg, "out", c, n))
                if place(seg, "out", c, n) % 2 == 0:
                    stop_for(dve, "dve", act_job, a)
                else:
                    stop_for(dve, "dve", dve_job, d)
                at = i * 192 + (c * 96 + n * 6)
                cols = slice(at, at + 6) if isinstance(at, int) else bass.ds(at, 6)
                dve.bn_stats(stats[:, cols], v_inv[c][:, n * 512:(n + 1) * 512]).then_inc(stat_done, 1)

            def turn(m, i, c, q):
                stop_for(dve, "dve", v_act, m * V_ACT + i * 8 + (4 * c + q + 1))
                at = slice(q * QUART, (q + 1) * QUART)
                dve.transpose(v_t[c % 2][:, at], v_fwd[:, at]).then_inc(v_tp, 1)

            def run(seg, half_base, m=None, i=0, turns={}):
                for j, job in enumerate(seg):
                    if j % 2:
                        dve.wait_ge(pe_job, half_base * 2 + (j + 1))
                        if job[0] in ("dftx", "lift"):
                            chunk = job[1] if job[0] == "lift" else i * 2 + job[1]
                            unload_spectra(copy, neg, j, job, chunk).then_inc(dve_job, 1)
                        else:
                            unload(copy, neg, add_bias, j, job).then_inc(dve_job, 1)
                    if j in turns:
                        turn(m, i, *turns[j])
                    if job[0] == "out":
                        _, c, n = job
                        for back in range(n - 2, (n if n == 15 else n - 2) + 1):
                            if back >= 0:
                                stat(seg, half_base, m, i, c, back)

            def batch_norm(m, wait_at):
                steps = [0]

                def step(ins):
                    steps[0] += 1
                    ins.then_inc(dve_chain, 1)
                    dve.wait_ge(dve_chain, wait_at(steps[0]))

                n = layer(m)

                def column(k):
                    return chan[:, k:k + 1] if m is None else chan[:, bass.ds(m + (k + 1), 1)]

                stop_for(dve, "dve", stat_done, n * (16 * CHUNKS) + 16 * CHUNKS)
                step(dve.bn_aggr(bnw[:, 0:2], stats[:, :]))
                dve.sem_inc(bn_agg, 1)
                dve.wait_ge(bn_mm, n * 2 + 1)
                step(dve.tensor_copy(bnw[:, 5:6], bank[7][:, 0:1]))
                step(dve.tensor_tensor(bnw[:, 6:7], bnw[:, 0:1], bnw[:, 5:6], ALU.subtract))
                step(dve.scalar_tensor_tensor(out=bnw[:, 2:3], in0=bnw[:, 6:7], scalar=bnw[:, 6:7],
                                              in1=bnw[:, 1:2], op0=ALU.mult, op1=ALU.add))
                dve.sem_inc(bn_dev, 1)
                dve.wait_ge(bn_mm, n * 2 + 2)
                step(dve.tensor_scalar(bnw[:, 3:4], bank[7][:, 8:9], BN_EPS, None, ALU.add))
                dve.sem_inc(bn_var, 1)
                dve.wait_ge(bn_sqrt, n + 1)
                step(dve.reciprocal(bnw[:, 6:7], bnw[:, 4:5]))
                step(dve.scalar_tensor_tensor(out=bnw[:, 7:8], in0=bnw[:, 6:7], scalar=bnw[:, 3:4],
                                              in1=bnw[:, 4:5], op0=ALU.mult, op1=ALU.add))
                step(dve.tensor_scalar(bnw[:, 6:7], bnw[:, 7:8], 0.5, None, ALU.mult))
                step(dve.reciprocal(bnw[:, 7:8], bnw[:, 6:7]))
                step(dve.tensor_tensor(sc[:, 0:1], bnw[:, 7:8], column(LAYERS), ALU.mult))
                step(dve.tensor_tensor(bnw[:, 6:7], sc[:, 0:1], bnw[:, 5:6], ALU.mult))
                step(dve.tensor_tensor(sc[:, 1:2], column(2 * LAYERS), bnw[:, 6:7], ALU.subtract))
                step(dve.tensor_copy(wb_now[:, 0:1], column(1)))
                dve.sem_inc(sc_ready, 1)
                assert steps[0] == BN_STEPS

            def inverse(m):
                run(MIX, at_mix(m))
                run(INV_FIRST, at_inv(m))
                with dve.Fori(0, PAIRS - 1) as i:
                    run(INV_PAIR, at_inv(m) + INV_IN + i * (len(INV_PAIR) // 2), m, i)
                run(INV_LAST, at_inv(m) + INV_IN + (PAIRS - 1) * (len(INV_PAIR) // 2), m, PAIRS - 1)

            dve.sem_inc(dve_job, 4)
            dve.wait_ge(const_in, CONST_READY)
            link(dve.tensor_copy(wb_now[:, 0:1], chan[:, 0:1]))
            dve.wait_ge(f_zero, 1)
            run(FIELD, 0)
            inverse(None)
            before = chained[0]
            batch_norm(None, lambda k: before + k)
            with dve.Fori(0, LAYERS - 1) as m:
                stop_for(dve, "dve", stage_cp, m * STAGED + STAGED)
                for q in range(4):
                    turn(m, 0, 0, q)
                turn(m, 0, 1, 0)
                run(FWD_FIRST, at_fwd(m), m, 0, {1: (1, 1), 3: (1, 2), 5: (1, 3)})
                for q in range(4):
                    stop_for(dve, "dve", v_out[1][q], m * (16 * PAIRS) + 16 * PAIRS)
                with dve.Fori(0, PAIRS - 1) as i:
                    run(FWD_PAIR, at_fwd(m) + FWD_IN + i * (len(FWD_PAIR) // 2), m, i,
                        {**{k: (2, q) for q, k in enumerate((3, 5, 7, 9))},
                         **{k: (3, q) for q, k in enumerate((15, 17, 19, 21))}})
                run(FWD_LAST, at_fwd(m) + FWD_IN + (PAIRS - 1) * (len(FWD_PAIR) // 2), m, PAIRS - 1)
                inverse(m)
                batch_norm(m, lambda k: m * BN_STEPS + (before + BN_STEPS + k))
            chained[0] = before + LAYERS * BN_STEPS

            def root_of(dst, a, r, tmp, a_val, floor=None):
                dve.sem_inc(s_root, 1)
                dve.wait_ge(a_step, a_val)
                if floor is not None:
                    link(dve.tensor_scalar(r, r, floor, None, ALU.max))
                link(dve.reciprocal(tmp, r))
                link(dve.tensor_tensor(tmp, tmp, a, ALU.mult))
                link(dve.tensor_tensor(tmp, tmp, r, ALU.add))
                link(dve.tensor_scalar(tmp, tmp, 0.5, floor, ALU.mult, ALU.max) if floor is not None
                     else dve.tensor_scalar(tmp, tmp, 0.5, None, ALU.mult))
                link(dve.reciprocal(dst, tmp))

            def wide(ap):
                return ap.rearrange("p (t y) -> p t y", y=D)

            def spread(ap):
                return ap.unsqueeze(2).to_broadcast([P, ap.shape[1], D])

            def norm_rows(half, a_val):
                mean, var, r, tmp, inv = (small[:, 256 + 32 * k + 16 * half:272 + 32 * k + 16 * half] for k in range(5))
                hh, xx, ss = (a[:, 1024 * half:1024 * (half + 1)] for a in (h, xn, sq))
                link(dve.tensor_reduce(mean, wide(hh), AX.X, ALU.add))
                link(dve.tensor_scalar(mean, mean, 1.0 / D, None, ALU.mult))
                link(dve.tensor_tensor(wide(xx), wide(hh), spread(mean), ALU.subtract))
                link(dve.tensor_tensor(ss, xx, xx, ALU.mult))
                link(dve.tensor_reduce(var, wide(ss), AX.X, ALU.add))
                link(dve.tensor_scalar(var, var, 1.0 / D, LN_EPS, ALU.mult, ALU.add))
                root_of(inv, var, r, tmp, a_val)
                link(dve.tensor_tensor(wide(xx), wide(xx), spread(inv), ALU.mult))
                if a_val >= 5:
                    parts = xhl[:, 2048 * half:2048 * (half + 1)].rearrange("p (t a y) -> p t a y", a=2, y=D)
                    link(dve.tensor_scalar(parts[:, :, 0].bitcast(I32), wide(xx).bitcast(I32), HIGH, None,
                                           ALU.bitwise_and))
                    link(dve.tensor_tensor(parts[:, :, 1], wide(xx), parts[:, :, 0], ALU.subtract))
                dve.sem_inc(s_step, 1)

            link(dve.tensor_scalar(a32[:, :], qbd[:, 0:32], sc[:, 0:1], None, ALU.mult))
            link(dve.tensor_scalar(wfield[:, 0:P], ones[:, :], sc[:, 1:2], None, ALU.mult))
            dve.sem_inc(a_ready, 1)
            dve.wait_ge(bn_mm, 2 * LAYERS + 1)
            link(dve.tensor_tensor(bnw[:, 12:13], bank[7][:, 0:1], qbd[:, 32:33], ALU.add))
            dve.sem_inc(a_ready, 1)
            dve.wait_ge(tail_in, 16 * 4)
            wq2 = wq_s[:, 0:128].rearrange("p (a c) -> p a c", a=2)
            link(dve.tensor_reduce(small[:, 256:258], wq2, AX.X, ALU.add))
            link(dve.tensor_scalar(small[:, 256:258], small[:, 256:258], 1.0 / D, None, ALU.mult))
            link(dve.tensor_tensor(wq2, wq2, small[:, 256:258].unsqueeze(2).to_broadcast([P, 2, D]),
                                   ALU.subtract))
            for c in range(CHUNKS):
                for g in (1, 3):
                    n = 4 * c + g
                    if g == 1 and c >= 2:
                        dve.wait_ge(hq_out[c % 2], 64 * (c // 2))
                    dve.wait_ge(read_mm, n + 1)
                    dve.tensor_scalar(hq[c % 2][:, g * 512:(g + 1) * 512], bank[n % BANKS][:, :], bnw[:, 12:13],
                                      None, ALU.add).then_inc(read_dve, 1)
            dve.wait_ge(h_in[0], 64)
            norm_rows(0, 1)
            dve.wait_ge(h_in[1], 64)
            norm_rows(1, 2)
            qk2 = wk[:, 0:4096].rearrange("p (t a c) -> p t a c", a=2, c=D)
            sums = small[:, 512:576]
            sums2 = sums.rearrange("p (t a) -> p t a", a=2)
            for half in range(2):
                dve.wait_ge(act_tail, tail_count(tail_no("qkv", 8 * half + 7))[0])
                link(dve.tensor_reduce(sums2[:, 16 * half:16 * (half + 1)], qk2[:, 16 * half:16 * (half + 1)],
                                       AX.X, ALU.add))
            link(dve.tensor_scalar(sums, sums, 1e-7, None, ALU.add))
            link(dve.reciprocal(sums, sums))
            link(dve.tensor_tensor(qk2[:, :, 1], qk2[:, :, 1], spread(sums2[:, :, 1]), ALU.mult))
            dve.sem_inc(s_step, 1)
            link(dve.tensor_tensor(wide(xn), qk2[:, :, 0], qk2[:, :, 0], ALU.mult))
            link(dve.tensor_reduce(small[:, 288:320], wide(xn), AX.X, ALU.add))
            for _ in range(2):
                link(dve.tensor_tensor(small[:, 288:320], small[:, 288:320], sums2[:, :, 0], ALU.mult))
            root_of(small[:, 256:288], small[:, 288:320], small[:, 320:352], small[:, 352:384], 3, floor=1e-12)
            link(dve.tensor_tensor(small[:, 256:288], small[:, 256:288], sums2[:, :, 0], ALU.mult))
            link(dve.tensor_tensor(wide(xn), qk2[:, :, 0], spread(small[:, 256:288]), ALU.mult))
            dve.sem_inc(s_step, 1)
            n = tail_no("knorm", 0)
            dve.wait_ge(pe_tail, n + 1)
            dve.tensor_copy(small[0:D, 384:448].rearrange("p (b t) -> p b t", b=2),
                            bank[n % BANKS][0:D, 0:64].rearrange("p (t b) -> p b t", b=2)).then_inc(dve_tail, 1)
            dve.wait_ge(dve_tail, tail_count(n)[1])
            root_of(small[0:D, 640:704], small[0:D, 384:448], small[0:D, 448:512], small[0:D, 576:640], 4, floor=1e-12)
            link(dve.tensor_scalar(small[0:D, 640:704], small[0:D, 640:704], float(S) ** -0.5, None, ALU.mult))
            for j in range(8):
                n = tail_no("kv", j)
                dve.wait_ge(pe_tail, n + 1)
                dve.tensor_tensor(wide(kvs[0:D, j * 512:(j + 1) * 512]), wide(bank[n % BANKS][0:D, :]),
                                  small[0:D, 640 + 8 * j:648 + 8 * j].unsqueeze(2).to_broadcast([D, 8, D]),
                                  ALU.mult).then_inc(dve_tail, 1)
            dve.wait_ge(tail_in, 16 * 8)
            link(dve.tensor_scalar(w1_high.bitcast(I32), w1s.bitcast(I32), HIGH, None, ALU.bitwise_and))
            link(dve.tensor_tensor(w1_rest_r[:, :], w1s, w1_high, ALU.subtract))
            link(dve.tensor_copy(w1_high_r[:, :], w1_high))
            for half in range(2):
                for j in (2 * half, 2 * half + 1):
                    n = tail_no("proj", j)
                    dve.wait_ge(pe_tail, n + 1)
                    hs = h[:, j * 512:(j + 1) * 512]
                    dve.tensor_tensor(hs, bank[n % BANKS][:, :], hs, ALU.add).then_inc(dve_tail, 1)
                dve.wait_ge(dve_tail, tail_count(n)[1])
                norm_rows(half, 5 + half)
            m1, dm, ex, den, pr = (small[:, 256 + 32 * k:288 + 32 * k] for k in range(5))
            pr2 = small[:, 416:448]

            def each(ap):
                return ap.rearrange("p (t e) -> p t e", e=E)

            def per(ap):
                return ap.unsqueeze(2).to_broadcast([P, TILES, E])

            for j in range(2):
                n = tail_no("gate", j)
                dve.wait_ge(pe_tail, n + 1)
                dve.tensor_tensor(each(score[:, j * P:(j + 1) * P]), each(bank[n % BANKS][:, 0:P]),
                                  bg_s.unsqueeze(1).to_broadcast([P, 16, E]), ALU.add).then_inc(dve_tail, 1)
            dve.wait_ge(dve_tail, tail_count(n)[1])
            dve.wait_ge(rows_set, 3)

            def pick(hot, top, tmp):
                link(dve.tensor_reduce(top, each(score), AX.X, ALU.max))
                link(dve.tensor_tensor(each(hot), each(score), per(top), ALU.is_equal))
                link(dve.tensor_tensor(hot, hot, rank, ALU.mult))
                link(dve.tensor_reduce(tmp, each(hot), AX.X, ALU.max))
                link(dve.tensor_tensor(each(hot), each(rank), per(tmp), ALU.is_equal))

            pick(hot1, m1, den)
            link(dve.scalar_tensor_tensor(out=score, in0=hot1, scalar=-3.0e38, in1=score, op0=ALU.mult, op1=ALU.add))
            pick(hot2, pr, den)
            link(dve.tensor_tensor(dm, pr, m1, ALU.subtract))
            dve.sem_inc(s_root, 1)
            dve.wait_ge(a_step, 7)
            link(dve.tensor_scalar(den, ex, 1.0, None, ALU.add))
            link(dve.reciprocal(pr, den))
            link(dve.tensor_tensor(pr2, pr, ex, ALU.mult))
            link(dve.tensor_tensor(each(hot1), each(hot1), per(pr), ALU.mult))
            link(dve.tensor_tensor(each(hot2), each(hot2), per(pr2), ALU.mult))
            for ab in range(2):
                link(dve.tensor_tensor(xn.rearrange("p (i t ab c) -> p ab i t c", i=4, t=4, ab=2)[:, ab, :, :, 0:E],
                                       hot1.rearrange("p (i ab t e) -> p ab i t e", ab=2, t=4, e=E)[:, ab],
                                       hot2.rearrange("p (i ab t e) -> p ab i t e", ab=2, t=4, e=E)[:, ab], ALU.add))
            dve.sem_inc(s_step, 1)
            dve.sem_inc(y_done, 1)
            def scale(i, e):
                dve.wait_ge(cb_in[e], i * 16 + 16)
                for ab in range(2):
                    dve.wait_ge(hid_relu, i * 32 + (4 * e + 2 * ab + 6))
                    hid = hb[e % 2][:, ab * 1024:(ab + 1) * 1024].rearrange("p (h t) -> p h t", h=2)
                    at = e * 1024 + ab * 512
                    dve.tensor_tensor(hid, hid, cb[:, at:at + 512].unsqueeze(1).to_broadcast([P, 2, 512]), ALU.mult)\
                       .then_inc(hid_scaled, 1)

            def finish(i, last):
                dve.wait_ge(y_turn, i + 2)
                hs = h[:, i * 512:(i + 1) * 512] if last else h[:, bass.ds(i * 512, 512)]
                hs = hs.rearrange("p (a t d) -> p t a d", a=2, d=D)
                dve.tensor_tensor(hs, bank[5][:, :].rearrange("p (t a d) -> p t a d", a=2, d=D), hs, ALU.add)\
                   .then_inc(y_done, 1)

            for e in range(E):
                scale(0, e)
            with dve.Fori(1, 4) as i:
                for e in range(E):
                    scale(i, e)
                    if e == 2:
                        finish(i + -1, False)
            finish(3, True)

        @block.gpsimd
        def _(pool):
            src = os_[:, :].rearrange("p (g n) -> p g n", g=KYG)

            def copy(chunk, c):
                at = chunk * 576
                cols = slice(at, at + 576) if isinstance(at, int) else bass.ds(at, 576)
                pool.tensor_copy(stage[c].rearrange("p (g n) -> p g n", g=KYG), src[:, :, cols]).then_inc(stage_cp, 1)

            def inverse(m):
                a, d = done_after(at_inv(m), -1)
                stop_for(pool, "pool", act_job, a)
                stop_for(pool, "pool", dve_job, d)
                copy(1, 1)
                with pool.Fori(0, PAIRS - 1) as i:
                    base = at_inv(m) + INV_IN + i * (len(INV_PAIR) // 2)
                    stop_for(pool, "pool", pe_job, base * 2 + 1)
                    copy(i * 2 + 2, 0)
                    stop_for(pool, "pool", pe_job, base * 2 + (place(INV_PAIR, "back", 1, BQ - 1, 1) + 1))
                    copy(i * 2 + 3, 1)

            pool.memset(area_o[:, COLS + 768:COLS + 2 * 768], 0.0).then_inc(f_zero, 1)
            pool.memset(turned, 0.0).then_inc(t_zero, 1)
            inverse(None)
            with pool.Fori(0, LAYERS - 1) as m:
                stop_for(pool, "pool", pe_job, at_mix(m) * 2)
                pool.memset(turned, 0.0).then_inc(t_zero, 1)
                inverse(m)
            pool.wait_ge(read_mm, 4 * 6)
            pool.memset(xnT[D:P, :], 1.0).then_inc(rows_set, 1)
            pool.wait_ge(read_mm, 4 * 7)
            pool.memset(atT[D:P, :], 1.0)
            pool.memset(kvs[D:P, :], 0.0)
            pool.wait_ge(read_mm, 4 * CHUNKS)
            pool.memset(qT[D:P, :], 0.0).then_inc(rows_set, 1)
            pool.wait_ge(pe_tail, tail_no("x2T", 7) + 1)
            for e in range(E):
                pool.memset(rank.rearrange("p (t e) -> p t e", e=E)[:, :, e], float(E - e))
            pool.memset(xn, 0.0).then_inc(rows_set, 1)


def _constants():
    f32 = np.float32
    y = np.arange(S)
    ky = np.arange(M)
    kx = np.concatenate([np.arange(M), np.arange(S - M, S)])
    x_of = np.arange(S)
    fy = np.zeros((B2, S, B2, 2, M))
    th = 2 * np.pi * np.outer(y, ky) / S
    for b in range(B2):
        fy[b, :, b, 0], fy[b, :, b, 1] = np.cos(th), -np.sin(th)
    fyt = np.zeros((BQ, S // 2, 2, BQ, 2, M))
    for b in range(BQ):
        fyt[b, :, :, b, 0] = np.cos(th).reshape(2, S // 2, M).transpose(1, 0, 2)
        fyt[b, :, :, b, 1] = -np.sin(th).reshape(2, S // 2, M).transpose(1, 0, 2)
    th = 2 * np.pi * np.outer(x_of, kx) / S
    g = np.zeros((2, 2, S, 2, 2, KX))
    for b in range(2):
        g[0, b, :, 0, b], g[0, b, :, 1, b] = np.cos(th), -np.sin(th)
        g[1, b, :, 0, b], g[1, b, :, 1, b] = np.sin(th), np.cos(th)
    xs = (np.arange(XQ)[None, :] * XR + np.arange(XR)[:, None]).reshape(-1)
    th = 2 * np.pi * np.outer(kx, xs) / S
    gi = np.zeros((2, B2, KX, B2, S))
    for b in range(B2):
        gi[0, b, :, b], gi[1, b, :, b] = np.cos(th), -np.sin(th)
    wt = np.where(ky == 0, 1.0, 2.0)[:, None] / (S * S)
    th = 2 * np.pi * np.outer(ky, y) / S
    fyi = np.zeros((BQ, 32, BQ, S))
    for b in range(BQ):
        fyi[b, 0:M, b], fyi[b, M:2 * M, b] = wt * np.cos(th), -wt * np.sin(th)
    avg = np.kron(np.ones((XQ, XQ)), np.eye(C)) / XQ
    pos = np.zeros((B2, S, 3, 2, S))
    at = np.linspace(0.0, 1.0, S, dtype=f32)
    pos[:, :, 0], pos[:, :, 1], pos[:, :, 2] = at, at[:, None, None], 1.0
    return {
        "c_pos": pos.reshape(P, -1).astype(f32),
        "c_fy": fy.reshape(P, -1).astype(f32),
        "c_fyt": np.pad(fyt.reshape(P, 2, 96), ((0, 0), (0, 0), (0, 32))).reshape(P, -1).astype(f32),
        "c_g": g.transpose(2, 1, 0, 5, 3, 4).reshape(P, -1).astype(f32),
        "c_gf": g.transpose(1, 2, 0, 5, 3, 4).reshape(P, -1).astype(f32),
        "c_gi": gi.reshape(96, P).astype(f32),
        "c_fyi": fyi.reshape(P, -1).astype(f32),
        "c_id": np.eye(P, dtype=f32),
        "c_avg": avg.astype(f32),
        "c_ones": np.ones((P, P), f32),
        "c_image": np.kron(np.eye(2), np.ones((S, 1))).astype(f32),
    }


def _layout(i):
    f32 = np.float32
    a = {k: np.asarray(v) for k, v in i.items()}
    x = a["x"].reshape(CHUNKS, BQ, B2, XQ, XR, S)
    pos = np.linspace(0.0, 1.0, S, dtype=f32)
    fields = np.zeros((CHUNKS, BQ, B2, XQ, XR, S, 4), f32)
    fields[..., 0] = x
    fields[..., 1] = pos.reshape(XQ, XR, 1)
    fields[..., 2] = pos
    fields[..., 3] = 1.0
    x_f = np.zeros((CHUNKS, 4, 32, XR // 4 * CH * S), f32)
    x_f[:, :, 0:16] = fields.transpose(0, 4, 3, 6, 1, 2, 5).reshape(CHUNKS, 4, 4, XQ, 4, -1)\
        .transpose(0, 1, 3, 4, 2, 5).reshape(CHUNKS, 4, 16, -1)
    p4 = np.concatenate([a["L0_tok_p_w"], a["L0_tok_p_b"][None]], 0)
    p_t = np.zeros((XQ, C, 4, 4, 32), f32)
    wbd = np.zeros((LAYERS, XQ, C, XQ, C), f32)
    qbd = np.zeros((XQ, C, 32), f32)
    for q in range(XQ):
        for k in range(4):
            p_t[q, :, k, k, 4 * q:4 * q + 4] = p4.T
        wbd[:, q, :, q] = a["L0_tok_w_w"]
        qbd[q, :, q] = a["L0_tok_q_w"][:, 0]
    p_e = np.zeros((KYG, 4, 4, KYG, 4, C), f32)
    w = np.concatenate([a["L0_tok_fw1"], a["L0_tok_fw2"]], 3).reshape(LAYERS, C, C, KX, KYG, 4, 2)
    spec = np.zeros((4, C, LAYERS, KYG, KX, 2, 4, C), f32)
    for k in range(4):
        spec[k, ..., k, :] = w[:, :, :, :, :, k].transpose(1, 0, 4, 3, 5, 2)
        for g in range(KYG):
            p_e[g, k, :, g, k] = p4

    def channels(t):
        return np.tile(t.T, (XQ, 1))

    def under(wm, bias):
        return np.concatenate([wm, bias[None], np.zeros((P - D - 1, len(bias)), f32)], 0)

    w1 = a["L0_ffn_W1"].reshape(E * H, D).T
    w2 = a["L0_ffn_W2"].reshape(E, D, 2, P).transpose(3, 0, 2, 1).reshape(P, -1)
    b2 = np.zeros((2, D, 2, D), f32)
    b2[0, 0:E, 0] = b2[1, 0:E, 1] = a["L0_ffn_b2"]
    return {
        "x_f": x_f.reshape(CHUNKS, P, -1),
        "x_t": x.transpose(2, 5, 0, 1, 3, 4).reshape(P, -1),
        "p_t": p_t.reshape(P, -1),
        "p_e": np.concatenate([p_e.reshape(48, -1), np.zeros((P - 48, KYG * P), f32)], 0),
        "w_bd": wbd.reshape(LAYERS, P, P),
        "w_b": channels(a["L0_tok_w_b"]),
        "spec_w": spec.reshape(P, -1),
        "bn_g": channels(a["L0_tok_bn_g"]),
        "bn_b": channels(a["L0_tok_bn_b"]),
        "q_bd": qbd.reshape(P, 32),
        "q_b": np.tile(a["L0_tok_q_b"].reshape(1, 1), (P, 1)),
        "wqkv": under(a["L0_attn_W_qkv"], a["L0_attn_b_qkv"]),
        "wout": under(a["L0_attn_W_out"], a["L0_attn_b_out"]),
        "wgate": np.concatenate([a["L0_ffn_Wg"].T] * 2, 0),
        "w1t": np.concatenate([w1] * 2, 0),
        "b1": a["L0_ffn_b1"].reshape(2 * E, P).T,
        "bg": np.tile(a["L0_ffn_bg"], (P, 1)),
        "w2t": w2,
        "b2": b2.reshape(P, P),
    }


def kernel(**inputs):
    import concourse.bacc as _bacc
    from concourse.bass_utils import run_bass_kernel_spmd as _run

    data = {**_layout(inputs), **_constants()}
    nc = _bacc.Bacc("TRN2", target_bir_lowering=False, num_devices=1)
    arrays, args = {}, {}
    for name, t in data.items():
        arrays[f"in_{name}"] = np.ascontiguousarray(t)
        args[name] = nc.dram_tensor(f"in_{name}", t.shape, mybir.dt.from_np(t.dtype), kind="ExternalInput").ap()
    args["out"] = nc.dram_tensor("out_0", (B, S, S), F32, kind="ExternalOutput").ap()
    build(nc, **args)
    r = _run(nc, [arrays], core_ids=[0])
    return r.results[0]["out_0"]
```
